# Optimizing a Trainium2 kernel written in Bass

```python
import numpy as np
import jax
import jax.numpy as jnp

def _softmax(x, axis=-1):
    return jax.nn.softmax(x, axis=axis)

def _gelu(x):
    return jax.nn.gelu(x, approximate=True)

def _silu(x):
    return jax.nn.silu(x)

def _sigmoid(x):
    return jax.nn.sigmoid(x)

def _layernorm(x, axis=-1, eps=1e-05):
    m = jnp.mean(x, axis=axis, keepdims=True)
    v = jnp.var(x, axis=axis, keepdims=True)
    return (x - m) / jnp.sqrt(v + eps)

def _scatter_add(tgt, idx, src, axis=0):
    return tgt.at[idx].add(src)

def _segment_sum(src, seg, n):
    return jax.ops.segment_sum(src, seg, n)
kernel_name = 'mk_xattn_ffn_d2_seqx_r4_5eabf1'

def setup_inputs(seed: int=0):
    np.random.seed(seed)
    _w = jnp.asarray

    def _rec_inputs():
        import jax
        import jax.numpy as jnp
        _rk = jax.random.key(seed)
        x = 7.22e-05 + 1 * jax.random.normal(jax.random.fold_in(_rk, 1), (16, 256, 256), jnp.float32)
        _lenS = 256 - jax.random.randint(jax.random.fold_in(_rk, 7), (16,), 0, max(1, 256 // 4) + 1, jnp.int32)
        _lenS2 = 256 - jax.random.randint(jax.random.fold_in(_rk, 8), (16,), 0, max(1, 256 // 4) + 1, jnp.int32)
        _ctx_1024P = jax.random.normal(jax.random.fold_in(_rk, 11), (16, 16, 256), jnp.float32)
        _ctx_1024c = jax.random.dirichlet(jax.random.fold_in(_rk, 511), 0.3 * jnp.ones((16,), jnp.float32), (16, 256))
        _ctx_1024t = jnp.einsum('bsk,bkd->bsd', _ctx_1024c, _ctx_1024P)
        _ctx_1024t = _ctx_1024t * jax.lax.rsqrt(jnp.mean(jnp.square(_ctx_1024t)) + 1e-12) * 0.953939
        ctx_1024 = 4.13588e-05 + 0.999923 * (_ctx_1024t + 0.3 * jax.random.normal(jax.random.fold_in(_rk, 611), (16, 256, 256), jnp.float32))
        _validS = jnp.arange(256)[None, :] < _lenS[:, None]
        _validS2 = jnp.arange(256)[None, :] < _lenS2[:, None]
        _causal = jnp.tril(jnp.ones((256, 256), dtype=bool))
        mask_1x1xSxS2_if1 = jnp.where(jnp.ones((1, 1, 256, 256), dtype=bool), 1, 0).astype(jnp.int32)
        return (x, ctx_1024, mask_1x1xSxS2_if1)
    x, ctx_1024, mask_1x1xSxS2_if1 = _rec_inputs()

    def _L0_xattn_setup():
        import jax, jax.numpy as jnp
        import numpy as np
        import math
        D_MODEL = 256
        N_HEADS = 16
        HEAD_DIM = D_MODEL // N_HEADS
        BATCH = 2
        SEQ = 1024
        key = jax.random.key(seed)
        ks = jax.random.split(key, 12)
        s = 0.02
        inp = {'query': jax.random.normal(ks[0], (BATCH, SEQ, D_MODEL), jnp.float32), 'key': jax.random.normal(ks[1], (BATCH, SEQ, D_MODEL), jnp.float32), 'value': jax.random.normal(ks[2], (BATCH, SEQ, D_MODEL), jnp.float32), 'mask': jnp.ones((1, 1, SEQ, SEQ), jnp.int32), 'Wq': jax.random.normal(ks[3], (D_MODEL, D_MODEL), jnp.float32) * s, 'bq': jax.random.normal(ks[4], (D_MODEL,), jnp.float32) * s, 'Wk': jax.random.normal(ks[5], (D_MODEL, D_MODEL), jnp.float32) * s, 'bk': jax.random.normal(ks[6], (D_MODEL,), jnp.float32) * s, 'Wv': jax.random.normal(ks[7], (D_MODEL, D_MODEL), jnp.float32) * s, 'bv': jax.random.normal(ks[8], (D_MODEL,), jnp.float32) * s, 'Wo': jax.random.normal(ks[9], (D_MODEL, D_MODEL), jnp.float32) * s, 'bo': jax.random.normal(ks[10], (D_MODEL,), jnp.float32) * s}
        return inp
    _L0_xattn_all = _L0_xattn_setup()
    _L0_xattn_in = {k: v for k, v in _L0_xattn_all.items() if k in ('Wq', 'bq', 'Wk', 'bk', 'Wv', 'bv', 'Wo', 'bo')}
    del _L0_xattn_all

    def _L0_ffn_setup():
        import jax, jax.numpy as jnp
        import numpy as np
        B, S, H, E, K, I = (1, 128, 256, 16, 4, 256)
        ALPHA, LIMIT = (1.702, 7.0)
        key = jax.random.key(seed)
        ks = jax.random.split(key, 7)
        return {'hidden_states': jax.random.normal(ks[0], (B, S, H), jnp.float32), 'router_w': jax.random.normal(ks[1], (H, E), jnp.float32) * 0.02, 'router_b': jax.random.normal(ks[2], (E,), jnp.float32) * 0.02, 'gate_up_proj': jax.random.normal(ks[3], (E, H, 2 * I), jnp.float32) * 0.02, 'gate_up_bias': jax.random.normal(ks[4], (E, 2 * I), jnp.float32) * 0.02, 'down_proj': jax.random.normal(ks[5], (E, I, H), jnp.float32) * 0.02, 'down_bias': jax.random.normal(ks[6], (E, H), jnp.float32) * 0.02}
    _L0_ffn_all = _L0_ffn_setup()
    _L0_ffn_in = {k: v for k, v in _L0_ffn_all.items() if k in ('router_w', 'router_b', 'gate_up_proj', 'gate_up_bias', 'down_proj', 'down_bias')}
    del _L0_ffn_all

    def _L1_xattn_setup():
        import jax, jax.numpy as jnp
        import numpy as np
        D_MODEL = 256
        H = 16
        D_K = D_MODEL // H
        B = 128
        N = 64

        def _proj_heads(x, W, b):
            y = jnp.einsum('bnd,ed->bne', x, W) + b
            bsz, n, _ = y.shape
            return y.reshape(bsz, n, H, D_K).transpose(0, 2, 1, 3)
        key = jax.random.key(seed)
        ks = jax.random.split(key, 8)
        s = 1.0 / np.sqrt(D_MODEL)
        return {'query': jax.random.normal(ks[0], (B, N, D_MODEL), jnp.float32), 'key': jax.random.normal(ks[1], (B, N, D_MODEL), jnp.float32), 'value': jax.random.normal(ks[2], (B, N, D_MODEL), jnp.float32), 'Wq': jax.random.normal(ks[3], (D_MODEL, D_MODEL), jnp.float32) * s, 'bq': jnp.zeros((D_MODEL,), jnp.float32), 'Wk': jax.random.normal(ks[4], (D_MODEL, D_MODEL), jnp.float32) * s, 'bk': jnp.zeros((D_MODEL,), jnp.float32), 'Wv': jax.random.normal(ks[5], (D_MODEL, D_MODEL), jnp.float32) * s, 'bv': jnp.zeros((D_MODEL,), jnp.float32), 'Wo': jax.random.normal(ks[6], (D_MODEL, D_MODEL), jnp.float32) * s, 'bo': jnp.zeros((D_MODEL,), jnp.float32)}
    _L1_xattn_all = _L1_xattn_setup()
    _L1_xattn_in = {k: v for k, v in _L1_xattn_all.items() if k in ('Wq', 'bq', 'Wk', 'bk', 'Wv', 'bv', 'Wo', 'bo')}
    del _L1_xattn_all

    def _L1_ffn_setup():
        import jax, jax.numpy as jnp
        import numpy as np
        DIM = 256
        HIDDEN = 768
        SCALE = 1.0 / 127.0

        def _dequant(w_int, dtype):
            return w_int.astype(dtype) * jnp.asarray(SCALE, dtype)
        key = jax.random.key(seed)
        k_x, k_g, k_u, k_d = jax.random.split(key, 4)
        x = jax.random.normal(k_x, (4, 512, DIM), dtype=jnp.float32)
        w_gate = jax.random.randint(k_g, (HIDDEN, DIM), -127, 128, dtype=jnp.int32)
        w_up = jax.random.randint(k_u, (HIDDEN, DIM), -127, 128, dtype=jnp.int32)
        w_down = jax.random.randint(k_d, (DIM, HIDDEN), -127, 128, dtype=jnp.int32)
        return {'x': x, 'w_gate': w_gate, 'w_up': w_up, 'w_down': w_down}
    _L1_ffn_all = _L1_ffn_setup()
    _L1_ffn_in = {k: v for k, v in _L1_ffn_all.items() if k in ('w_gate', 'w_up', 'w_down')}
    del _L1_ffn_all
    return {'x': x, 'ctx_1024': ctx_1024, 'mask_1x1xSxS2_if1': mask_1x1xSxS2_if1, 'L0_xattn_Wq': _L0_xattn_in['Wq'], 'L0_xattn_bq': _L0_xattn_in['bq'], 'L0_xattn_Wk': _L0_xattn_in['Wk'], 'L0_xattn_bk': _L0_xattn_in['bk'], 'L0_xattn_Wv': _L0_xattn_in['Wv'], 'L0_xattn_bv': _L0_xattn_in['bv'], 'L0_xattn_Wo': _L0_xattn_in['Wo'], 'L0_xattn_bo': _L0_xattn_in['bo'], 'L0_ffn_router_w': _L0_ffn_in['router_w'], 'L0_ffn_router_b': _L0_ffn_in['router_b'], 'L0_ffn_gate_up_proj': _L0_ffn_in['gate_up_proj'], 'L0_ffn_gate_up_bias': _L0_ffn_in['gate_up_bias'], 'L0_ffn_down_proj': _L0_ffn_in['down_proj'], 'L0_ffn_down_bias': _L0_ffn_in['down_bias'], 'L1_xattn_Wq': _L1_xattn_in['Wq'], 'L1_xattn_bq': _L1_xattn_in['bq'], 'L1_xattn_Wk': _L1_xattn_in['Wk'], 'L1_xattn_bk': _L1_xattn_in['bk'], 'L1_xattn_Wv': _L1_xattn_in['Wv'], 'L1_xattn_bv': _L1_xattn_in['bv'], 'L1_xattn_Wo': _L1_xattn_in['Wo'], 'L1_xattn_bo': _L1_xattn_in['bo'], 'L1_ffn_w_gate': _L1_ffn_in['w_gate'], 'L1_ffn_w_up': _L1_ffn_in['w_up'], 'L1_ffn_w_down': _L1_ffn_in['w_down']}

def reference(x, ctx_1024, mask_1x1xSxS2_if1, L0_xattn_Wq, L0_xattn_bq, L0_xattn_Wk, L0_xattn_bk, L0_xattn_Wv, L0_xattn_bv, L0_xattn_Wo, L0_xattn_bo, L0_ffn_router_w, L0_ffn_router_b, L0_ffn_gate_up_proj, L0_ffn_gate_up_bias, L0_ffn_down_proj, L0_ffn_down_bias, L1_xattn_Wq, L1_xattn_bq, L1_xattn_Wk, L1_xattn_bk, L1_xattn_Wv, L1_xattn_bv, L1_xattn_Wo, L1_xattn_bo, L1_ffn_w_gate, L1_ffn_w_up, L1_ffn_w_down):
    import jax
    import jax.numpy as jnp

    def _L0_xattn_ref(query, key, value, mask, Wq, bq, Wk, bk, Wv, bv, Wo, bo):
        import jax, jax.numpy as jnp
        import numpy as np
        import math
        D_MODEL = 256
        N_HEADS = 16
        HEAD_DIM = D_MODEL // N_HEADS
        BATCH = 2
        SEQ = 1024
        B, S, D = query.shape
        scale = 1.0 / math.sqrt(HEAD_DIM)

        def proj_split(x, W, b):
            y = x @ W.T + b
            return y.reshape(B, -1, N_HEADS, HEAD_DIM).transpose(0, 2, 1, 3)
        q = proj_split(query, Wq, bq)
        k = proj_split(key, Wk, bk)
        v = proj_split(value, Wv, bv)
        scores = jnp.einsum('bhqd,bhkd->bhqk', q, k) * scale
        scores = jnp.where(mask == 0, jnp.float32(-1000000000.0), scores)
        probs = jax.nn.softmax(scores, axis=-1)
        attn = jnp.einsum('bhqk,bhkd->bhqd', probs, v)
        out = attn.transpose(0, 2, 1, 3).reshape(B, S, D)
        return out @ Wo.T + bo

    def _L0_ffn_ref(hidden_states, router_w, router_b, gate_up_proj, gate_up_bias, down_proj, down_bias):
        import jax, jax.numpy as jnp
        import numpy as np
        B, S, H, E, K, I = (1, 128, 256, 16, 4, 256)
        ALPHA, LIMIT = (1.702, 7.0)
        b, s, h = hidden_states.shape
        x = hidden_states.reshape(-1, h)
        logits = x @ router_w + router_b
        topv, topi = jax.lax.top_k(logits, K)
        topw = jax.nn.softmax(topv, axis=-1)
        one_hot = (topi[..., None] == jnp.arange(E)).astype(topw.dtype)
        scores = jnp.einsum('tk,tke->te', topw, one_hot)
        gu = jnp.einsum('th,ehf->tef', x, gate_up_proj) + gate_up_bias
        gate = jnp.minimum(gu[..., ::2], LIMIT)
        up = jnp.clip(gu[..., 1::2], -LIMIT, LIMIT)
        glu = gate * jax.nn.sigmoid(gate * ALPHA)
        act = (up + 1.0) * glu
        expert_out = jnp.einsum('tei,eih->teh', act, down_proj) + down_bias
        out = jnp.einsum('te,teh->th', scores, expert_out)
        return out.reshape(b, s, h)

    def _L1_xattn_ref(query, key, value, Wq, bq, Wk, bk, Wv, bv, Wo, bo):
        import jax, jax.numpy as jnp
        import numpy as np
        D_MODEL = 256
        H = 16
        D_K = D_MODEL // H
        B = 128
        N = 64

        def _proj_heads(x, W, b):
            y = jnp.einsum('bnd,ed->bne', x, W) + b
            bsz, n, _ = y.shape
            return y.reshape(bsz, n, H, D_K).transpose(0, 2, 1, 3)
        q = _proj_heads(query, Wq, bq)
        k = _proj_heads(key, Wk, bk)
        v = _proj_heads(value, Wv, bv)
        scale = 1.0 / jnp.sqrt(jnp.asarray(D_K, q.dtype))
        scores = jnp.einsum('bhnd,chnd->hnbc', q, k) * scale
        p = jax.nn.softmax(scores, axis=-1)
        out = jnp.einsum('hnbc,chnd->bhnd', p, v)
        bsz, _, n, _ = out.shape
        out = out.transpose(0, 2, 1, 3).reshape(bsz, n, H * D_K)
        return jnp.einsum('bnd,ed->bne', out, Wo) + bo

    def _L1_ffn_ref(x, w_gate, w_up, w_down):
        import jax, jax.numpy as jnp
        import numpy as np
        DIM = 256
        HIDDEN = 768
        SCALE = 1.0 / 127.0

        def _dequant(w_int, dtype):
            return w_int.astype(dtype) * jnp.asarray(SCALE, dtype)
        wg = _dequant(w_gate, x.dtype)
        wu = _dequant(w_up, x.dtype)
        wd = _dequant(w_down, x.dtype)
        gate = jnp.einsum('bsd,hd->bsh', x, wg)
        up = jnp.einsum('bsd,hd->bsh', x, wu)
        h = jax.nn.silu(gate) * up
        return jnp.einsum('bsh,dh->bsd', h, wd)
    x = x + _L0_xattn_ref(_layernorm(x, axis=-1), ctx_1024, ctx_1024, mask_1x1xSxS2_if1, L0_xattn_Wq, L0_xattn_bq, L0_xattn_Wk, L0_xattn_bk, L0_xattn_Wv, L0_xattn_bv, L0_xattn_Wo, L0_xattn_bo)
    x = x + _L0_ffn_ref(_layernorm(x, axis=-1), L0_ffn_router_w, L0_ffn_router_b, L0_ffn_gate_up_proj, L0_ffn_gate_up_bias, L0_ffn_down_proj, L0_ffn_down_bias)
    x = x + _L1_xattn_ref(_layernorm(x, axis=-1), ctx_1024, ctx_1024, L1_xattn_Wq, L1_xattn_bq, L1_xattn_Wk, L1_xattn_bk, L1_xattn_Wv, L1_xattn_bv, L1_xattn_Wo, L1_xattn_bo)
    x = x + _L1_ffn_ref(_layernorm(x, axis=-1), L1_ffn_w_gate, L1_ffn_w_up, L1_ffn_w_down)
    return x

_drawn_inputs = setup_inputs


def setup_inputs(seed=0):
    import zlib

    import numpy as np

    out = dict(_drawn_inputs(seed))
    spreads = {'L1_xattn_bq': (0.0, 0.1),
     'L1_xattn_bk': (0.0, 2.0),
     'L1_xattn_bv': (0.0, 0.1),
     'L1_xattn_bo': (0.0, 0.1)}
    factors = {'L0_xattn_Wq': 8.0,
     'L0_xattn_bq': 26.38,
     'L0_xattn_Wk': 8.0,
     'L0_xattn_bk': 64.0,
     'L0_xattn_bv': 6.323,
     'L0_ffn_router_b': 6.595,
     'L0_ffn_gate_up_bias': 8.0,
     'L0_ffn_down_bias': 4.052}
    for name, (base, spread) in spreads.items():
        noise = np.random.default_rng([zlib.crc32(name.encode()), seed]).standard_normal(out[name].shape)
        drawn = base * np.exp(spread * noise) if base else spread * noise
        out[name] = jnp.asarray(drawn.astype(out[name].dtype))
    for name, factor in factors.items():
        out[name] = (out[name] * factor).astype(out[name].dtype)
    return out
```

```python
from contextlib import ExitStack

import numpy as np

import concourse.bass as bass
from concourse import mybir

ALU = mybir.AluOpType
ACT = mybir.ActivationFunctionType
F32 = mybir.dt.float32
F32R = mybir.dt.float32r
F16 = mybir.dt.float16
BF16 = mybir.dt.bfloat16
I32 = mybir.dt.int32
U32 = mybir.dt.uint32
AX_X = mybir.AxisListType.X

P = 128
D = 256
KC = D // P
TOKENS = 4096
H = 16
E = 16
DH = D // H
UNIT = 256
UNITS = TOKENS // UNIT
QT = UNIT // P
EPS = 1e-5
MSTEP = 32768.0
MASKED = 65280.0 * MSTEP
CREDIT = 16


def attention(nc, tag, x_in, x_out, ctx_t, w, mask_q, mask_k):
    with ExitStack() as ctx:
        def sb(name, shape, dt=F32):
            return ctx.enter_context(nc.sbuf_tensor(f"{tag}_{name}", shape, dt))

        def sem(name):
            return ctx.enter_context(nc.semaphore(f"{tag}_{name}"))

        ps_s = ctx.enter_context(nc.psum_tensor(f"{tag}_ps_s", [P, 2, QT, UNIT], F32))
        ps_t = ctx.enter_context(nc.psum_tensor(f"{tag}_ps_t", [P, 2, QT, UNIT], F32))
        ps_o = ctx.enter_context(nc.psum_tensor(f"{tag}_ps_o", [P, 2, 2, UNIT], F32))
        ps_a = ctx.enter_context(nc.psum_tensor(f"{tag}_ps_a", [P, 2, UNIT], F32))
        ps_b = ctx.enter_context(nc.psum_tensor(f"{tag}_ps_b", [P, 2, UNIT], F32))

        w_raw = sb("w_raw", [P, 4, D])
        wq = sb("wq", [P, 2, KC, D], F32R)
        wk = sb("wk", [P, 2, KC, D], F32R)
        wv = sb("wv", [P, 2, KC, D], F32R)
        wo = sb("wo", [P, 2, 4, D], F32R)
        bq = sb("bq", [P, 2])
        bk = sb("bk", [P, 2])
        bv = sb("bv", [P, D])
        bo = sb("bo", [P, D])
        ident = sb("ident", [P, P])
        ident16 = sb("ident16", [P, P], BF16)
        mraw = sb("mraw", [P, 2, QT, UNIT], I32)
        mbias = sb("mbias", [P, 2, QT, UNIT], BF16)
        half = sb("half", [P, QT])
        xin = sb("xin", [P, 2, QT, D])
        xbo = sb("xbo", [P, 2, QT, D])
        cin = sb("cin", [P, 2, KC, UNIT])
        chi = sb("chi", [P, 2, KC, UNIT], F32R)
        clo = sb("clo", [P, 2, KC, UNIT], F32R)
        qs = sb("qs", [P, 2, 8, UNIT], F16)
        ks = sb("ks", [P, 2, 8, UNIT], F16)
        v1 = sb("v1", [P, 2, QT, H, 32])
        stats = sb("stats", [P, QT, 6])
        mv = sb("mv", [P, QT, 2])
        rstd = sb("rstd", [P, QT])
        xn = sb("xn", [P, QT, D])
        xhi = sb("xhi", [P, KC, UNIT], F32R)
        xlo = sb("xlo", [P, KC, UNIT], F32R)
        nat = sb("nat", [P, 4, 2, UNIT], F16)
        mx = sb("mx", [P, QT, H])
        mt = sb("mt", [H, 2, UNIT], F16)
        pt = sb("pt", [P, 4, QT, UNIT])
        rec = sb("rec", [P, 2, UNIT])
        recs = sb("recs", [P, 2, UNIT])
        an = sb("an", [P, 2, UNIT])
        ahi = sb("ahi", [P, 4, UNIT], F32R)
        alo = sb("alo", [P, 4, UNIT], F32R)
        yout = sb("yout", [P, 2, QT, D])

        w_loaded = sem("w_loaded")
        w_used = sem("w_used")
        const_loaded = sem("const_loaded")
        const_ready = sem("const_ready")
        gp = sem("gp_setup")
        apart = sem("apart")
        with nc.Block() as block:
            @block.sync
            def _(sp):
                sp.dma_start(bq[:], w["bq"]).then_inc(const_loaded, 16)
                sp.dma_start(bk[:], w["bk"]).then_inc(const_loaded, 16)
                sp.dma_start(bv[:], w["bv"].partition_broadcast(P)).then_inc(const_loaded, 16)
                sp.dma_start(bo[:], w["bo"].partition_broadcast(P)).then_inc(const_loaded, 16)
                sp.dma_start(mraw[:, 0], mask_q).then_inc(const_loaded, 16)
                sp.dma_start(mraw[:, 1], mask_k).then_inc(const_loaded, 16)
                for n, name in enumerate(("wq", "wk", "wv", "wo")):
                    if n:
                        sp.wait_ge(w_used, n)
                    sp.dma_start(w_raw[:, 0:4 if name == "wo" else 2, :], w[name]).then_inc(w_loaded, 16)

            @block.gpsimd
            def _(pool):
                nc.gpsimd.memset(ident[:], 0.0).then_inc(gp, 1)
                nc.gpsimd.memset(ident16[:], 0.0).then_inc(gp, 1)
                nc.gpsimd.memset(v1[:], 1.0).then_inc(gp, 1)
                nc.gpsimd.memset(half[:], -0.5).then_inc(gp, 1)
                pool.wait_ge(gp, 4)
                for m in (ident, ident16):
                    nc.gpsimd.affine_select(out=m[:], in_=m[:], compare_op=ALU.not_equal, fill=1.0, base=0,
                                            pattern=[[-1, P]], channel_multiplier=1).then_inc(gp, 1)

            @block.vector
            def _(dve):
                for top in (32, 96):
                    nc.vector.memset(ks[top:top + 32], -MSTEP)
                done = 0
                for n, (name, dst) in enumerate((("wq", wq), ("wk", wk), ("wv", wv), ("wo", wo))):
                    c = 4 if name == "wo" else 2
                    dve.wait_ge(w_loaded, 16 * (n + 1))
                    if name == "wq":
                        nc.vector.tensor_scalar(w_raw[:, 0:c], w_raw[:, 0:c], DH ** -0.5, None, ALU.mult).then_inc(const_ready, 1)
                        done += 1
                        dve.wait_ge(const_ready, done)
                    nc.vector.tensor_copy(dst[:, 0], w_raw[:, 0:c]).then_inc(const_ready, 1)
                    done += 1
                    dve.wait_ge(const_ready, done)
                    nc.vector.tensor_tensor(dst[:, 1], w_raw[:, 0:c], dst[:, 0].bitcast(F32), ALU.subtract).then_inc(w_used, 1)
                dve.wait_ge(const_loaded, 96)
                nc.vector.tensor_scalar(bq[:], bq[:], DH ** -0.5, None, ALU.mult)
                nc.vector.tensor_scalar(mbias[:], mraw[:], 0.0, -MASKED, ALU.is_equal, ALU.mult)

        c1 = CREDIT
        x_loaded = [sem("x_loaded0"), sem("x_loaded1")]; ctx_loaded = [sem("ctx_loaded0"), sem("ctx_loaded1")]
        stats_done = sem("stats_done"); mv_done = sem("mv_done"); rs1 = sem("rs1"); rstd_done = sem("rstd_done")
        xn_done = sem("xn_done"); xt_done = sem("xt_done"); xhi_done = sem("xhi_done"); xlo_done = sem("xlo_done")
        chi_done = sem("chi_done"); clo_done = sem("clo_done"); xbo_done = sem("xbo_done")
        q_done = sem("q_done"); k_done = sem("k_done"); v_done = sem("v_done")
        qh_done = sem("qh_done"); ql_done = sem("ql_done"); kh_done = sem("kh_done"); kl_done = sem("kl_done")
        v1_done = sem("v1_done"); qs_stacked = sem("qs_stacked"); ks_stacked = sem("ks_stacked")
        s_done = sem("s_done"); max_done = sem("max_done"); mtr_done = sem("mtr_done"); mh_done = sem("mh_done")
        ml_done = sem("ml_done"); m_stacked = sem("m_stacked")
        st_done = sem("st_done"); exp_done = sem("exp_done"); pv_done = sem("pv_done")
        rec_done = sem("rec_done"); recs_done = sem("recs_done"); an_done = sem("an_done")
        ahi_done = sem("ahi_done"); alo_done = sem("alo_done"); wo_done = sem("wo_done"); y_done = sem("y_done")
        stored = [sem("stored0"), sem("stored1")]
        counters = {
            "act": [xhi_done, qh_done, kh_done, mh_done, exp_done, ahi_done],
            "dve": [stats_done, mv_done, xn_done, xlo_done, ql_done, kl_done, v1_done, max_done, ml_done,
                    rec_done, recs_done, an_done, alo_done, y_done],
            "pool": [rs1, rstd_done, chi_done, clo_done, xbo_done],
            "pe": [xt_done, q_done, k_done, v_done, s_done, mtr_done, st_done, pv_done, wo_done],
        }

        def run_units(eng, step):
            step(-2, 0, False, False, True)
            step(-1, 1, False, True, True)
            with eng.Fori(0, UNITS // 2 - 1) as r:
                step(r * 2, 0, True, True, True)
                step(r * 2 + 1, 1, True, True, True)
            step(UNITS - 2, 0, True, True, False)
            step(UNITS - 1, 1, True, False, False)

        def start(eng, sems):
            for s in sems:
                eng.sem_inc(s, CREDIT)

        with nc.Block() as block:
            @block.sync
            def _(sp):
                def load(u, b):
                    sp.wait_ge(xn_done, c1 + 2 * (u - 1))
                    sp.wait_ge(xbo_done, c1 + u - 1)
                    for q, view in enumerate(x_in(u)):
                        sp.dma_start(xin[:, b, q], view).then_inc(x_loaded[b], 16)
                    sp.wait_ge(clo_done, c1 + u - 1)
                    sp.sem_inc(apart, 1)
                    sp.dma_start(cin[:, b], ctx_t(u)).then_inc(ctx_loaded[b], 16)

                def step(u, b, t, s, p):
                    if not s and not t:
                        load(0, 0)
                        load(1, 1)
                    if s:
                        for i, done in ((0, mh_done), (1, ml_done)):
                            sp.wait_ge(done, c1 + u + 2)
                            for par in range(2):
                                row = 64 * par + 48 + i
                                sp.dma_start(qs[row:row + 1, 1 - b], mt[8 * par:8 * par + 8, i, :]).then_inc(m_stacked, 16)
                    if p:
                        if t:
                            sp.wait_ge(st_done, c1 + 16 * u + 16)
                            sp.sem_inc(apart, 1)
                        for dst, stacked, hi, lo, hi_done, lo_done, order in (
                                (qs, qs_stacked, 0, 1, qh_done, ql_done, (0, 2, 1)),
                                (ks, ks_stacked, 2, 3, kh_done, kl_done, (0, 1, 2))):
                            parts = (hi, lo, hi) if dst is qs else (hi, hi, lo)
                            sp.wait_ge(hi_done, c1 + u + 3)
                            for n in order:
                                if parts[n] == lo:
                                    sp.wait_ge(lo_done, c1 + u + 3)
                                for par in range(2):
                                    row = 64 * par + 16 * n
                                    sp.dma_start(dst[row:row + 16, b].rearrange("d (j m) t -> d j (m t)", m=2),
                                                 nat[64 * par:64 * par + 64, parts[n]].rearrange("p m t -> p (m t)")
                                                 ).then_inc(stacked, 16)
                        if not isinstance(u, int) or u + 4 < UNITS:
                            load(u + 4, b)
                    if t:
                        sp.wait_ge(y_done, c1 + u + 1)
                        for q, view in enumerate(x_out(u)):
                            sp.dma_start(view, yout[:, b, q]).then_inc(stored[b], 16)

                for b in range(2):
                    sp.sem_inc(stored[b], 16)
                step(-2, 0, False, False, True)
                step(-1, 1, False, True, True)
                with sp.Fori(0, UNITS // 2 - 2) as r:
                    step(r * 2, 0, True, True, True)
                    step(r * 2 + 1, 1, True, True, True)
                step(UNITS - 4, 0, True, True, True)
                step(UNITS - 3, 1, True, True, True)
                step(UNITS - 2, 0, True, True, False)
                step(UNITS - 1, 1, True, False, False)
                for b in range(2):
                    sp.wait_ge(stored[b], 16 + 32 * (UNITS // 2))

            @block.gpsimd
            def _(pool):
                start(pool, counters["pool"])

                def step(u, b, t, s, p):
                    if not p:
                        return
                    n = u + 2
                    pool.wait_ge(mv_done, c1 + 2 * n + 2)
                    pool.wait_ge(xn_done, c1 + 2 * n)
                    pool.sem_inc(apart, 1)
                    nc.gpsimd.tensor_scalar(rstd[:], mv[:, :, 1], EPS, None, ALU.add).then_inc(rs1, 1)
                    pool.wait_ge(rs1, c1 + n + 1)
                    nc.gpsimd.tensor_tensor(rstd[:], rstd[:], half[:], ALU.pow).then_inc(rstd_done, 1)
                    pool.wait_ge(ctx_loaded[b], (n - b) * 8 + 16)
                    pool.wait_ge(v_done, c1 + n - 1)
                    pool.sem_inc(apart, 1)
                    nc.gpsimd.tensor_copy(chi[:, b], cin[:, b]).then_inc(chi_done, 1)
                    pool.wait_ge(chi_done, c1 + n + 1)
                    nc.gpsimd.tensor_tensor(clo[:, b], cin[:, b], chi[:, b].bitcast(F32), ALU.subtract).then_inc(clo_done, 1)
                    pool.wait_ge(x_loaded[b], (n - b) * 16 + 32)
                    pool.wait_ge(y_done, c1 + n - 1)
                    for q in range(QT):
                        last = nc.gpsimd.tensor_tensor(xbo[:, b, q], xin[:, b, q], bo[:], ALU.add)
                    last.then_inc(xbo_done, 1)

                run_units(pool, step)

            @block.scalar
            def _(act):
                start(act, counters["act"])

                def step(u, b, t, s, p):
                    def exps(h):
                        act.wait_ge(st_done, c1 + 16 * u + h + 1)
                        act.wait_ge(pv_done, c1 + 16 * u + h - 3)
                        nc.scalar.activation(pt[:, h % 4], ps_t[:, h % 2], ACT.Exp).then_inc(exp_done, 1)

                    def part_high(g):
                        act.wait_ge(an_done, c1 + 2 * u + g + 1)
                        act.wait_ge(wo_done, c1 + u)
                        nc.scalar.copy(ahi[:, 2 * g:2 * g + 2], an[:]).then_inc(ahi_done, 1)

                    for h in range(H):
                        if t:
                            exps(h)
                        if h == 9 and p:
                            act.wait_ge(xt_done, c1 + u + 3)
                            act.wait_ge(q_done, c1 + u + 2)
                            nc.scalar.copy(xhi[:], ps_a[:]).then_inc(xhi_done, 1)
                        if h == 12 and t:
                            part_high(0)
                    if s:
                        act.wait_ge(mtr_done, c1 + u + 2)
                        if not t:
                            pass
                        else:
                            act.wait_ge(m_stacked, 64 * (u + 1))
                        nc.scalar.activation(mt[:, 0, :], ps_b[0:H, 0, :], ACT.Copy, scale=1.0 / MSTEP).then_inc(mh_done, 1)
                    if t:
                        part_high(1)
                    if p:
                        if s or t:
                            act.wait_ge(qs_stacked, 96 * (u + 2))
                            act.wait_ge(ks_stacked, 96 * (u + 2))
                        act.wait_ge(q_done, c1 + u + 3)
                        for m in range(2):
                            last = nc.scalar.activation(nat[:, 0, m], ps_a[:, m], ACT.Identity, bias=bq[:, m:m + 1])
                        last.then_inc(qh_done, 1)
                        act.wait_ge(k_done, c1 + u + 3)
                        for m in range(2):
                            last = nc.scalar.activation(nat[:, 2, m], ps_b[:, m], ACT.Identity, bias=bk[:, m:m + 1])
                        last.then_inc(kh_done, 1)

                run_units(act, step)

            @block.vector
            def _(dve):
                start(dve, counters["dve"])

                def step(u, b, t, s, p):
                    n = u + 2

                    def norm_a(g):
                        dve.wait_ge(pv_done, c1 + 16 * u + 8 * g + 8)
                        dve.wait_ge(recs_done, c1 + 2 * u + g)
                        nc.vector.reciprocal(rec[:], ps_o[:, g]).then_inc(rec_done, 1)

                    def norm_b(g):
                        dve.wait_ge(rec_done, c1 + 2 * u + g + 1)
                        dve.wait_ge(an_done, c1 + 2 * u + g)
                        dve.sem_inc(apart, 1)
                        nc.vector.stream_shuffle(recs[:], rec[:], [16 + i % 16 for i in range(32)]).then_inc(recs_done, 1)
                        dve.wait_ge(recs_done, c1 + 2 * u + g + 1)
                        dve.wait_ge(ahi_done, c1 + 2 * u + g)
                        dve.wait_ge(alo_done, c1 + 2 * u + g)
                        nc.vector.tensor_tensor(an[:], ps_o[:, g], recs[:], ALU.mult).then_inc(an_done, 1)

                    def part_low(g):
                        dve.wait_ge(ahi_done, c1 + 2 * u + g + 1)
                        nc.vector.tensor_tensor(alo[:, 2 * g:2 * g + 2], an[:], ahi[:, 2 * g:2 * g + 2].bitcast(F32),
                                                ALU.subtract).then_inc(alo_done, 1)

                    for h in range(H):
                        if s:
                            dve.wait_ge(s_done, c1 + 16 * (u + 1) + h + 1)
                            if h == 0:
                                dve.wait_ge(mtr_done, c1 + u + 1)
                            nc.vector.reduce_max(mx[:, :, 8 * (h % 2) + h // 2], ps_s[:, h % 2], AX_X).then_inc(max_done, 1)
                        if p and h == 1:
                            dve.wait_ge(x_loaded[b], (n - b) * 16 + 32)
                            for q in range(QT):
                                nc.vector.bn_stats(stats[:, q], xin[:, b, q]).then_inc(stats_done, 1)
                            for q in range(QT):
                                dve.wait_ge(stats_done, c1 + 2 * n + 1 + q)
                                dve.wait_ge(rstd_done, c1 + n)
                                dve.sem_inc(apart, 1)
                                nc.vector.bn_aggr(mv[:, q], stats[:, q]).then_inc(mv_done, 1)
                        if p and h == 4:
                            dve.wait_ge(rstd_done, c1 + n + 1)
                            dve.wait_ge(xt_done, c1 + n)
                            for q in range(QT):
                                nc.vector.tensor_scalar(xn[:, q], xin[:, b, q], mv[:, q, 0:1], rstd[:, q:q + 1],
                                                        ALU.subtract, ALU.mult).then_inc(xn_done, 1)
                        if p and h == 9:
                            dve.wait_ge(xhi_done, c1 + n + 1)
                            dve.wait_ge(q_done, c1 + n)
                            nc.vector.tensor_tensor(xlo[:], ps_a[:], xhi[:].bitcast(F32), ALU.subtract).then_inc(xlo_done, 1)
                        if t and h == 10:
                            norm_a(0)
                        if t and h == 11:
                            norm_b(0)
                        if t and h == 13:
                            part_low(0)
                    if s:
                        dve.wait_ge(mh_done, c1 + u + 2)
                        if t:
                            dve.wait_ge(m_stacked, 64 * (u + 1))
                        nc.vector.scalar_tensor_tensor(mt[:, 1, :], ps_b[0:H, 0, :], 1.0 / MSTEP, mt[:, 0, :],
                                                       ALU.mult, ALU.subtract).then_inc(ml_done, 1)
                    if t:
                        norm_a(1)
                        norm_b(1)
                        part_low(1)
                    if p:
                        for part, done, hi_done, ps, bias, lo_done in (
                                (1, q_done, qh_done, ps_a, bq, ql_done), (3, k_done, kh_done, ps_b, bk, kl_done)):
                            dve.wait_ge(hi_done, c1 + n + 1)
                            if s or t:
                                dve.wait_ge(qs_stacked if part == 1 else ks_stacked, 96 * n)
                            for m in range(2):
                                last = nc.vector.scalar_tensor_tensor(nat[:, part, m], ps[:, m], bias[:, m:m + 1],
                                                                      nat[:, part - 1, m], ALU.add, ALU.subtract)
                            last.then_inc(lo_done, 1)
                        dve.wait_ge(v_done, c1 + n + 1)
                        if t:
                            dve.wait_ge(pv_done, c1 + 16 * u + 16)
                        for q in range(QT):
                            last = nc.vector.tensor_tensor(v1[:, b, q, :, 0:DH],
                                                           ps_a[:, q].rearrange("p (h d) -> p h d", d=DH),
                                                           bv[:].rearrange("p (h d) -> p h d", d=DH), ALU.add)
                        last.then_inc(v1_done, 1)
                    if t:
                        dve.wait_ge(wo_done, c1 + u + 1)
                        dve.wait_ge(xbo_done, c1 + u + 1)
                        if isinstance(u, int):
                            if u >= 2:
                                dve.wait_ge(stored[b], 16 + 32 * (u // 2))
                        else:
                            dve.wait_ge(stored[b], 16 + (u - b) * 16)
                        nc.vector.tensor_tensor(yout[:, b], ps_b[:], xbo[:, b], ALU.add).then_inc(y_done, 1)

                run_units(dve, step)

            @block.tensor
            def _(pe):
                start(pe, counters["pe"])

                def three(out, pairs):
                    ops = [(x, y) for ah, al, bh, bl in pairs for x, y in ((ah, bh), (ah, bl), (al, bh))]
                    for i, (x, y) in enumerate(ops):
                        last = nc.tensor.matmul(out, x, y, start=i == 0, stop=i == len(ops) - 1)
                    return last

                def step(u, b, t, s, p):
                    n = u + 2

                    def values(h):
                        pe.wait_ge(exp_done, c1 + 16 * u + h + 1)
                        if h % 8 == 0:
                            pe.wait_ge(an_done, c1 + 2 * u + h // 8 - 1)
                        j, i = h % 4, h // 4
                        for kt in range(QT):
                            last = nc.tensor.matmul(ps_o[32 * j:32 * j + 32, i // 2, i % 2], v1[:, b, kt, h],
                                                    pt[:, h % 4, kt], start=kt == 0, stop=kt == QT - 1,
                                                    tile_position=(0, 32 * j))
                        last.then_inc(pv_done, 1)

                    for h in range(H):
                        base = 64 * (h % 2)
                        if s:
                            if h == 0:
                                pe.wait_ge(qs_stacked, 96 * (u + 2))
                                pe.wait_ge(ks_stacked, 96 * (u + 2))
                            pe.wait_ge(max_done, c1 + 16 * (u + 1) + h - 1)
                            for q in range(QT):
                                nc.tensor.matmul(ps_s[:, h % 2, q], ident16[:], mbias[:, 0, q], start=True, stop=False)
                                last = nc.tensor.matmul(ps_s[:, h % 2, q], qs[base:base + 48, 1 - b, h // 2, q * P:q * P + P],
                                                        ks[base:base + 48, 1 - b, h // 2, :], start=False, stop=True)
                            last.then_inc(s_done, 1)
                        if t:
                            if h == 0:
                                pe.wait_ge(m_stacked, 64 * (u + 1))
                            pe.wait_ge(exp_done, c1 + 16 * u + h - 1)
                            for k in range(QT):
                                nc.tensor.matmul(ps_t[:, h % 2, k], ident16[:], mbias[:, 1, k], start=True, stop=False)
                                last = nc.tensor.matmul(ps_t[:, h % 2, k], ks[base:base + 50, b, h // 2, k * P:k * P + P],
                                                        qs[base:base + 50, b, h // 2, :], start=False, stop=True)
                            last.then_inc(st_done, 1)
                            if h >= 2:
                                if h == 2:
                                    pe.wait_ge(v1_done, c1 + u + 1)
                                values(h - 2)
                        if p and h == 7:
                            pe.wait_ge(xn_done, c1 + 2 * n + 2)
                            pe.wait_ge(v1_done, c1 + n)
                            for q in range(QT):
                                for c in range(KC):
                                    last = nc.tensor.transpose(ps_a[:, c, q * P:q * P + P], xn[:, q, c * P:c * P + P], ident[:])
                            last.then_inc(xt_done, 1)
                    if t:
                        values(14)
                        values(15)
                    if s:
                        pe.wait_ge(max_done, c1 + 16 * (u + 1) + 16)
                        pe.wait_ge(y_done, c1 + u)
                        for q in range(QT):
                            last = nc.tensor.transpose(ps_b[0:H, 0, q * P:q * P + P], mx[:, q, :], ident[:])
                        last.then_inc(mtr_done, 1)
                    if p:
                        pe.wait_ge(xlo_done, c1 + n + 1)
                        for m in range(2):
                            cols = slice(m * P, m * P + P)
                            last = three(ps_a[:, m], [(wq[:, 0, c, cols], wq[:, 1, c, cols], xhi[:, c], xlo[:, c]) for c in range(KC)])
                        last.then_inc(q_done, 1)
                        pe.wait_ge(clo_done, c1 + n + 1)
                        pe.wait_ge(ml_done, c1 + u + 2 if s else c1)
                        for m in range(2):
                            cols = slice(m * P, m * P + P)
                            last = three(ps_b[:, m], [(wk[:, 0, c, cols], wk[:, 1, c, cols], chi[:, b, c], clo[:, b, c]) for c in range(KC)])
                        last.then_inc(k_done, 1)
                        pe.wait_ge(ql_done, c1 + n + 1)
                        for q in range(QT):
                            toks = slice(q * P, q * P + P)
                            last = three(ps_a[:, q], [(chi[:, b, c, toks], clo[:, b, c, toks], wv[:, 0, c], wv[:, 1, c]) for c in range(KC)])
                        last.then_inc(v_done, 1)
                    if t:
                        if p:
                            pe.wait_ge(kl_done, c1 + n + 1)
                        elif s:
                            pe.wait_ge(ml_done, c1 + u + 2)
                        pe.wait_ge(alo_done, c1 + 2 * u + 2)
                        for q in range(QT):
                            toks = slice(q * P, q * P + P)
                            last = three(ps_b[:, q], [(ahi[:, i, toks], alo[:, i, toks], wo[:, 0, i], wo[:, 1, i]) for i in range(4)])
                        last.then_inc(wo_done, 1)

                run_units(pe, step)


def norm_and_route(nc, x_in, w, xt_hi, xt_lo, xres, scores):
    with ExitStack() as ctx:
        def sb(name, shape, dt=F32):
            return ctx.enter_context(nc.sbuf_tensor(f"rt_{name}", shape, dt))

        def sem(name):
            return ctx.enter_context(nc.semaphore(f"rt_{name}"))

        T = TOKENS // P
        ps_x = ctx.enter_context(nc.psum_tensor("rt_ps_x", [P, 2, 512], F32))
        ps_l = ctx.enter_context(nc.psum_tensor("rt_ps_l", [P, 2, 512], F32))
        rw = sb("rw", [P, KC, E])
        rb = sb("rb", [P, E])
        ident = sb("ident", [P, P])
        half = sb("half", [P, 1])
        iota = sb("iota", [P, E])
        stats = sb("stats", [P, 6]); mv = sb("mv", [P, 2]); rstd = sb("rstd", [P, 1])
        xn = sb("xn", [P, D]); xt = sb("xt", [P, KC, P])
        logits = sb("logits", [P, E]); best = sb("best", [P, 8]); which = sb("which", [P, 8], U32)
        whichf = sb("whichf", [P, 8])
        neg = sb("neg", [P, 1]); wexp = sb("wexp", [P, 4]); total = sb("total", [P, 1]); rtot = sb("rtot", [P, 1])
        part = sb("part", [P, 4, E])
        loaded = sem("loaded"); gp = sem("gp"); apart = sem("apart"); vc = sem("vc"); rs = sem("rs"); xt_done = sem("xt_done")
        hi_done = sem("hi_done"); xtc = sem("xtc"); lg_done = sem("lg_done"); e_done = sem("e_done"); ran = sem("ran")
        mvd = sem("mvd")
        with nc.Block() as block:
            @block.sync
            def _(sp):
                sp.dma_start(rw[:], w["router_w"].rearrange("(c p) n -> p c n", p=P)).then_inc(loaded, 16)
                sp.dma_start(rb[:], w["router_b"].partition_broadcast(P)).then_inc(loaded, 16)
                sp.dma_start(xres[:], x_in.rearrange("(t p) d -> p t d", p=P)).then_inc(loaded, 16)

            @block.gpsimd
            def _(pool):
                nc.gpsimd.memset(ident[:], 0.0).then_inc(gp, 1)
                nc.gpsimd.memset(half[:], -0.5).then_inc(gp, 1)
                nc.gpsimd.iota(iota[:], [[1, E]], base=0, channel_multiplier=0, allow_small_or_imprecise_dtypes=True).then_inc(gp, 1)
                pool.wait_ge(gp, 3)
                nc.gpsimd.affine_select(out=ident[:], in_=ident[:], compare_op=ALU.not_equal, fill=1.0, base=0,
                                        pattern=[[-1, P]], channel_multiplier=1).then_inc(gp, 1)
                with pool.Fori(0, T) as i:
                    pool.wait_ge(mvd, i + 1)
                    pool.sem_inc(apart, 1)
                    nc.gpsimd.tensor_scalar(rstd[:], mv[:, 1:2], EPS, None, ALU.add).then_inc(rs, 1)
                    pool.wait_ge(rs, i * 2 + 1)
                    nc.gpsimd.tensor_tensor(rstd[:], rstd[:], half[:], ALU.pow).then_inc(rs, 1)

            NV = 17

            @block.vector
            def _(dve):
                dve.wait_ge(loaded, 48)
                dve.wait_ge(gp, 4)
                with dve.Fori(0, T) as i:
                    cnt = [0]

                    def link(ins):
                        cnt[0] += 1
                        ins.then_inc(vc, 1)
                        dve.wait_ge(vc, i * NV + cnt[0])

                    link(nc.vector.bn_stats(stats[:], xres[:, i, :]))
                    dve.sem_inc(apart, 1)
                    nc.vector.bn_aggr(mv[:], stats[:]).then_inc(mvd, 1)
                    dve.wait_ge(rs, i * 2 + 2)
                    link(nc.vector.tensor_scalar(xn[:], xres[:, i, :], mv[:, 0:1], rstd[:], ALU.subtract, ALU.mult))
                    dve.wait_ge(xt_done, i + 1)
                    link(nc.vector.tensor_copy(xt[:], ps_x[:, 0, 0:256].rearrange("p (c t) -> p c t", c=KC)))
                    dve.wait_ge(hi_done, i + 1)
                    link(nc.vector.tensor_tensor(xt_lo[:, :, bass.ds(i * P, P)], xt[:], xt_hi[:, :, bass.ds(i * P, P)], ALU.subtract))
                    dve.wait_ge(lg_done, i + 1)
                    link(nc.vector.tensor_tensor(logits[:], ps_l[:, 0, 0:E], rb[:], ALU.add))
                    dve.sem_inc(apart, 1)
                    link(nc.vector.max(best[:], logits[:]))
                    dve.sem_inc(apart, 1)
                    link(nc.vector.max_index(which[:], best[:], logits[:]))
                    link(nc.vector.tensor_copy(whichf[:], which[:]))
                    link(nc.vector.tensor_scalar(neg[:], best[:, 0:1], -1.0, None, ALU.mult))
                    dve.wait_ge(e_done, i + 1)
                    link(nc.vector.reciprocal(rtot[:], total[:]))
                    link(nc.vector.tensor_scalar(wexp[:], wexp[:], rtot[:], None, ALU.mult))
                    for k in range(4):
                        link(nc.vector.tensor_scalar(part[:, k], iota[:], whichf[:, k:k + 1], wexp[:, k:k + 1], ALU.is_equal, ALU.mult))
                    link(nc.vector.tensor_tensor(part[:, 0:2], part[:, 0:2], part[:, 2:4], ALU.add))
                    link(nc.vector.tensor_tensor(scores[:, i, :], part[:, 0], part[:, 1], ALU.add))
                    assert cnt[0] == NV, cnt

            @block.scalar
            def _(act):
                with act.Fori(0, T) as i:
                    act.wait_ge(vc, i * NV + 3)
                    nc.scalar.copy(xt_hi[:, :, bass.ds(i * P, P)], xt[:]).then_inc(hi_done, 1)
                    act.wait_ge(vc, i * NV + 9)
                    nc.scalar.activation(wexp[:], best[:, 0:4], ACT.Exp, bias=neg[:], accum_out=total[:]).then_inc(e_done, 1)

            @block.tensor
            def _(pe):
                pe.wait_ge(loaded, 48)
                pe.wait_ge(gp, 4)
                with pe.Fori(0, T) as i:
                    pe.wait_ge(vc, i * NV + 2)
                    for c in range(KC):
                        last = nc.tensor.transpose(ps_x[:, 0, c * P:c * P + P], xn[:, c * P:c * P + P], ident[:])
                    last.then_inc(xt_done, 1)
                    pe.wait_ge(vc, i * NV + 3)
                    for c in range(KC):
                        last = nc.tensor.matmul(ps_l[:, 0, 0:E], xt[:, c], rw[:, c], start=c == 0, stop=c == KC - 1)
                    last.then_inc(lg_done, 1)
                    pe.wait_ge(vc, i * NV + 5)


def dense_experts(nc, x_out, w, xt_hi, xt_lo, xres, scores):
    I2 = 256
    G = 8
    WS = 64.0
    with ExitStack() as ctx:
        def sb(name, shape, dt=F32):
            return ctx.enter_context(nc.sbuf_tensor(f"de_{name}", shape, dt))

        def sem(name):
            return ctx.enter_context(nc.semaphore(f"de_{name}"))

        ps_g = ctx.enter_context(nc.psum_tensor("de_ps_g", [P, 4, 512], F32))
        ps_y = ctx.enter_context(nc.psum_tensor("de_ps_y", [P, 4, 512], F32))
        wraw = sb("wraw", [P, 6, 256])
        draw = sb("draw", [P, 2, 256])
        whi = sb("whi", [P, 2, 512], F16); wlo = sb("wlo", [P, 2, 512], F16)
        dhi = sb("dhi", [P, 2, 256], F16); dlo = sb("dlo", [P, 2, 256], F16)
        gb = sb("gb", [P, 4]); db = sb("db", [P, 256])
        g1 = sb("g1", [P, 2, 512]); u1 = sb("u1", [P, 2, 512]); sg = sb("sg", [P, 2, 512])
        ahi = sb("ahi", [P, 2, 512], F16); alo = sb("alo", [P, 2, 512], F16)
        yt = sb("yt", [P, 4, 256])
        apart = sem("apart"); wl = sem("wl"); wr = sem("wr"); vc = sem("vc"); gd = sem("gd"); ac = sem("ac"); yd = sem("yd"); st = sem("st")
        NV = 17
        NW = 4
        with nc.Block() as block:
            @block.sync
            def _(sp):
                with sp.Fori(0, E) as e:
                    sp.wait_ge(vc, 1 + e * G * NV)
                    sp.sem_inc(apart, 1)
                    sp.dma_start(wraw[:, 0:4].rearrange("p (c n) m -> p c (n m)", c=2), w["gate_up"][bass.ds(e * 256, 256), :].rearrange("(c p) n -> p c n", p=P)).then_inc(wl, 16)
                    sp.dma_start(draw[:], w["down"][bass.ds(e * 256, 256), :].rearrange("(c p) n -> p c n", p=P)).then_inc(wl, 16)
                    sp.dma_start(gb[:], w["gu_bias"][:, bass.ds(e * 4, 4)]).then_inc(wl, 16)
                    sp.dma_start(db[:], w["d_bias"][bass.ds(e, 1), :].partition_broadcast(P)).then_inc(wl, 16)
                sp.wait_ge(vc, 1 + E * G * NV)
                sp.dma_start(x_out.rearrange("(t p) d -> p t d", p=P), xres[:]).then_inc(st, 16)
                sp.wait_ge(st, 16)

            @block.vector
            def _(dve):
                dve.sem_inc(vc, 1)
                with dve.Fori(0, E) as e:
                    dve.wait_ge(wl, e * 64 + 64)
                    nc.vector.tensor_scalar(wraw[:, 0:4], wraw[:, 0:4], WS, None, ALU.mult).then_inc(wr, 1)
                    dve.wait_ge(wr, e * 6 + 1)
                    nc.vector.tensor_copy(whi[:].rearrange("p c n -> p (c n)"), wraw[:, 0:4].rearrange("p c n -> p (c n)")).then_inc(wr, 1)
                    dve.wait_ge(wr, e * 6 + 2)
                    nc.vector.tensor_tensor(wlo[:].rearrange("p c n -> p (c n)"), wraw[:, 0:4].rearrange("p c n -> p (c n)"), whi[:].rearrange("p c n -> p (c n)"), ALU.subtract).then_inc(wr, 1)
                    nc.vector.tensor_scalar(draw[:], draw[:], WS, None, ALU.mult).then_inc(wr, 1)
                    dve.wait_ge(wr, e * 6 + 4)
                    nc.vector.tensor_copy(dhi[:], draw[:]).then_inc(wr, 1)
                    dve.wait_ge(wr, e * 6 + 5)
                    nc.vector.tensor_tensor(dlo[:], draw[:], dhi[:], ALU.subtract).then_inc(wr, 1)
                    with dve.Fori(0, G) as g:
                        it = e * G + g
                        cnt = [0]

                        def link(ins):
                            cnt[0] += 1
                            ins.then_inc(vc, 1)
                            dve.wait_ge(vc, 1 + it * NV + cnt[0])

                        dve.wait_ge(gd, it + 1)
                        for m in range(2):
                            link(nc.vector.tensor_scalar(g1[:, m], ps_g[:, m], 1.0 / WS, gb[:, m:m + 1], ALU.mult, ALU.add))
                            link(nc.vector.tensor_scalar(u1[:, m], ps_g[:, 2 + m], 1.0 / WS, gb[:, 2 + m:3 + m], ALU.mult, ALU.add))
                        link(nc.vector.tensor_scalar(g1[:], g1[:], 7.0, None, ALU.min))
                        link(nc.vector.tensor_scalar(u1[:], u1[:], -7.0, 7.0, ALU.max, ALU.min))
                        link(nc.vector.scalar_tensor_tensor(u1[:], u1[:], 1.0, g1[:], ALU.add, ALU.mult))
                        dve.wait_ge(ac, it * 2 + 1)
                        link(nc.vector.tensor_tensor(u1[:], u1[:], sg[:], ALU.mult))
                        dve.wait_ge(ac, it * 2 + 2)
                        link(nc.vector.tensor_tensor(alo[:], u1[:], ahi[:], ALU.subtract))
                        dve.wait_ge(yd, it + 1)
                        for t in range(4):
                            link(nc.vector.scalar_tensor_tensor(yt[:, t], ps_y[:, t, 0:256], 1.0 / WS, db[:], ALU.mult, ALU.add))
                        for t in range(4):
                            tile = g * 4 + t
                            link(nc.vector.scalar_tensor_tensor(xres[:, tile, :], yt[:, t], scores[:, tile, bass.ds(e, 1)], xres[:, tile, :], ALU.mult, ALU.add))
                        assert cnt[0] == NV, cnt

            @block.scalar
            def _(act):
                with act.Fori(0, E * G) as it:
                    act.wait_ge(vc, 1 + it * NV + 5)
                    nc.scalar.activation(sg[:], g1[:], ACT.Sigmoid, scale=1.702).then_inc(ac, 1)
                    act.wait_ge(vc, 1 + it * NV + 8)
                    nc.scalar.copy(ahi[:], u1[:]).then_inc(ac, 1)

            @block.tensor
            def _(pe):
                with pe.Fori(0, E) as e:
                    pe.wait_ge(wr, e * 6 + 6)
                    pe.sem_inc(apart, 1)
                    with pe.Fori(0, G) as g:
                        it = e * G + g
                        pe.wait_ge(vc, 1 + it * NV)
                        for m in range(4):
                            ops = [(a, b, c) for c in range(2) for a, b in ((whi, xt_hi), (whi, xt_lo), (wlo, xt_hi))]
                            for n, (a, b, c) in enumerate(ops):
                                last = nc.tensor.matmul(ps_g[:, m], a[:, c, m * P:m * P + P], b[:, c, bass.ds(g * 512, 512)], start=n == 0, stop=n == 5)
                        last.then_inc(gd, 1)
                        pe.wait_ge(vc, 1 + it * NV + 9)
                        for t in range(4):
                            ops = [(a, b, c) for c in range(2) for a, b in ((ahi, dhi), (ahi, dlo), (alo, dhi))]
                            for n, (a, b, c) in enumerate(ops):
                                last = nc.tensor.matmul(ps_y[:, t, 0:256], a[:, c, t * P:t * P + P], b[:, c], start=n == 0, stop=n == 5)
                        last.then_inc(yd, 1)


def gated_ffn(nc, x_in, x_out, w):
    U = 512
    UN = TOKENS // U
    QT = U // P
    HC = 768 // P
    S = float(np.float32(1.0 / 127.0))
    with ExitStack() as ctx:
        def sb(name, shape, dt=F32):
            return ctx.enter_context(nc.sbuf_tensor(f"ff_{name}", shape, dt))

        def sem(name):
            return ctx.enter_context(nc.semaphore(f"ff_{name}"))

        ps_x = ctx.enter_context(nc.psum_tensor("ff_ps_x", [P, KC, U], F32))
        ps_g = ctx.enter_context(nc.psum_tensor("ff_ps_g", [P, 2, 2, U], F32))
        ps_y = ctx.enter_context(nc.psum_tensor("ff_ps_y", [P, 2, U], F32))
        wint = sb("wint", [P, 768], I32)
        wf = sb("wf", [P, 768])
        wg = sb("wg", [P, 2, KC, 768], F32R)
        wu = sb("wu", [P, 2, KC, 768], F32R)
        wd = sb("wd", [P, 2, HC, D], F32R)
        ident = sb("ident", [P, P]); half = sb("half", [P, QT])
        xin = sb("xin", [P, 2, QT, D])
        xres = sb("xres", [P, 2, QT, D])
        stats = sb("stats", [P, QT, 6]); mv = sb("mv", [P, QT, 2]); rstd = sb("rstd", [P, QT])
        xn = sb("xn", [P, QT, D])
        xhi = sb("xhi", [P, KC, U], F32R); xlo = sb("xlo", [P, KC, U], F32R)
        sg = sb("sg", [P, 2, U]); hf = sb("hf", [P, 2, U])
        hhi = sb("hhi", [P, 2, HC, U], F32R); hlo = sb("hlo", [P, 2, HC, U], F32R)
        yout = sb("yout", [P, 2, QT, D])

        w_loaded = sem("w_loaded"); w_split = sem("w_split"); gp = sem("gp"); apart = sem("apart")
        with nc.Block() as block:
            @block.sync
            def _(sp):
                n = 0
                for c in range(KC):
                    for name in ("wg", "wu"):
                        if n:
                            sp.wait_ge(w_split, 3 * n)
                        sp.dma_start(wint[:], w[name][c * P:c * P + P, :]).then_inc(w_loaded, 16)
                        n += 1
                for g in range(2):
                    sp.wait_ge(w_split, 3 * n)
                    sp.dma_start(wint[:].rearrange("p (c n) -> p c n", n=D), w["wd"][g * 384:g * 384 + 384, :].rearrange("(c p) n -> p c n", p=P)).then_inc(w_loaded, 16)
                    n += 1

            @block.gpsimd
            def _(pool):
                nc.gpsimd.memset(ident[:], 0.0).then_inc(gp, 1)
                nc.gpsimd.memset(half[:], -0.5).then_inc(gp, 1)
                pool.wait_ge(gp, 2)
                nc.gpsimd.affine_select(out=ident[:], in_=ident[:], compare_op=ALU.not_equal, fill=1.0, base=0,
                                        pattern=[[-1, P]], channel_multiplier=1).then_inc(gp, 1)

            @block.vector
            def _(dve):
                parts = [(t[:, 0, c], t[:, 1, c]) for c in range(KC) for t in (wg, wu)]
                parts += [(wd[:, 0, 3 * g:3 * g + 3].rearrange("p c n -> p (c n)"),
                           wd[:, 1, 3 * g:3 * g + 3].rearrange("p c n -> p (c n)")) for g in range(2)]
                for n, (hi, lo) in enumerate(parts):
                    dve.wait_ge(w_loaded, 16 * n + 16)
                    nc.vector.tensor_copy(wf[:], wint[:]).then_inc(w_split, 1)
                    dve.wait_ge(w_split, 3 * n + 1)
                    nc.vector.tensor_copy(hi, wf[:]).then_inc(w_split, 1)
                    dve.wait_ge(w_split, 3 * n + 2)
                    nc.vector.tensor_tensor(lo, wf[:], hi.bitcast(F32), ALU.subtract).then_inc(w_split, 1)
                    dve.wait_ge(w_split, 3 * n + 3)

        c1 = CREDIT
        x_loaded = [sem("x_loaded0"), sem("x_loaded1")]
        res_loaded = [sem("res_loaded0"), sem("res_loaded1")]
        stats_done = sem("stats_done"); mv_done = sem("mv_done"); rs1 = sem("rs1"); rstd_done = sem("rstd_done")
        xn_done = sem("xn_done"); xt_done = sem("xt_done"); xhi_done = sem("xhi_done"); xlo_done = sem("xlo_done")
        gu_done = sem("gu_done"); sg_done = sem("sg_done"); hf_done = sem("hf_done"); hhi_done = sem("hhi_done")
        hlo_done = sem("hlo_done"); y_done = sem("y_done"); out_done = sem("out_done")
        stored = [sem("stored0"), sem("stored1")]
        counters = {
            "act": [xhi_done, sg_done, hhi_done],
            "dve": [stats_done, mv_done, xn_done, xlo_done, hf_done, out_done],
            "pool": [rs1, rstd_done, hlo_done],
            "pe": [xt_done, gu_done, y_done],
        }

        def start(eng, sems):
            for s in sems:
                eng.sem_inc(s, CREDIT)

        def run_units(eng, step):
            step(-1, 1, True, False, False)
            step(0, 0, True, True, False)
            with eng.Fori(0, UN // 2 - 1) as r:
                step(r * 2 + 1, 1, True, True, True)
                step(r * 2 + 2, 0, True, True, True)
            step(UN - 1, 1, False, True, True)
            step(UN, 0, False, False, True)

        with nc.Block() as block:
            @block.sync
            def _(sp):
                def step(u, b, more, here, d):
                    if more:
                        sp.wait_ge(xn_done, c1 + 4 * (u + 1))
                        sp.dma_start(xin[:, b], x_in(u + 2)).then_inc(x_loaded[b], 16)
                    if here:
                        sp.wait_ge(out_done, c1 + 4 * (u - 1))
                        sp.dma_start(xres[:, b], x_in(u)).then_inc(res_loaded[b], 16)
                    if d:
                        sp.wait_ge(out_done, c1 + 4 * u)
                        sp.dma_start(x_out(u - 1), yout[:, 1 - b]).then_inc(stored[1 - b], 16)

                for b in range(2):
                    sp.sem_inc(stored[b], 16)
                step(-2, 0, True, False, False)
                step(-1, 1, True, False, False)
                step(0, 0, True, True, False)
                with sp.Fori(0, UN // 2 - 2) as r:
                    step(r * 2 + 1, 1, True, True, True)
                    step(r * 2 + 2, 0, True, True, True)
                step(UN - 3, 1, True, True, True)
                step(UN - 2, 0, False, True, True)
                step(UN - 1, 1, False, True, True)
                step(UN, 0, False, False, True)
                for b in range(2):
                    sp.wait_ge(stored[b], 16 + 16 * (UN // 2))

            @block.gpsimd
            def _(pool):
                start(pool, counters["pool"])

                def step(u, b, n, g, d):
                    def low(j):
                        pool.wait_ge(hhi_done, c1 + 6 * u + j + 1)
                        nc.gpsimd.tensor_tensor(hlo[:, b, j], hf[:, j % 2], hhi[:, b, j].bitcast(F32), ALU.subtract).then_inc(hlo_done, 1)

                    for j in range(HC):
                        if g:
                            low(j)
                        if n and j == 0:
                            pool.wait_ge(mv_done, c1 + 4 * (u + 1) + 4)
                            pool.wait_ge(xn_done, c1 + 4 * (u + 1))
                            pool.sem_inc(apart, 1)
                            nc.gpsimd.tensor_scalar(rstd[:], mv[:, :, 1], EPS, None, ALU.add).then_inc(rs1, 1)
                            pool.wait_ge(rs1, c1 + u + 2)
                            nc.gpsimd.tensor_tensor(rstd[:], rstd[:], half[:], ALU.pow).then_inc(rstd_done, 1)

                run_units(pool, step)

            @block.scalar
            def _(act):
                start(act, counters["act"])

                def step(u, b, n, g, d):
                    def silu(j):
                        act.wait_ge(gu_done, c1 + 6 * u + j + 1)
                        act.wait_ge(hf_done, c1 + 6 * u + j - 1)
                        nc.scalar.activation(sg[:, j % 2], ps_g[:, j % 2, 0], ACT.Silu, scale=S).then_inc(sg_done, 1)

                    def high(j):
                        act.wait_ge(hf_done, c1 + 6 * u + j + 1)
                        if j == 0:
                            act.wait_ge(y_done, c1 + 4 * (u - 1))
                        nc.scalar.copy(hhi[:, b, j], hf[:, j % 2]).then_inc(hhi_done, 1)

                    if g:
                        for j in range(HC):
                            silu(j)
                            if j:
                                high(j - 1)
                    if n:
                        act.wait_ge(xt_done, c1 + u + 2)
                        for c in range(KC):
                            last = nc.scalar.copy(xhi[:, c], ps_x[:, c])
                        last.then_inc(xhi_done, 1)
                    if g:
                        high(HC - 1)

                run_units(act, step)

            @block.vector
            def _(dve):
                start(dve, counters["dve"])

                def step(u, b, n, g, d):
                    m = u + 1
                    for j in range(HC):
                        if g:
                            dve.wait_ge(sg_done, c1 + 6 * u + j + 1)
                            dve.wait_ge(hlo_done, c1 + 6 * u + j - 1)
                            nc.vector.tensor_tensor(hf[:, j % 2], ps_g[:, j % 2, 1], sg[:, j % 2], ALU.mult).then_inc(hf_done, 1)
                        if n and j == 0:
                            dve.wait_ge(x_loaded[1 - b], (m - (1 - b)) * 8 + 16)
                            for q in range(QT):
                                nc.vector.bn_stats(stats[:, q], xin[:, 1 - b, q]).then_inc(stats_done, 1)
                            for q in range(QT):
                                dve.wait_ge(stats_done, c1 + 4 * m + 1 + q)
                                dve.sem_inc(apart, 1)
                                nc.vector.bn_aggr(mv[:, q], stats[:, q]).then_inc(mv_done, 1)
                        if n and j == 2:
                            dve.wait_ge(rstd_done, c1 + m + 1)
                            dve.wait_ge(xt_done, c1 + m)
                            for q in range(QT):
                                nc.vector.tensor_scalar(xn[:, q], xin[:, 1 - b, q], mv[:, q, 0:1], rstd[:, q:q + 1],
                                                        ALU.subtract, ALU.mult).then_inc(xn_done, 1)
                        if d and j >= 2:
                            t = j - 2
                            dve.wait_ge(y_done, c1 + 4 * (u - 1) + t + 1)
                            if t == 0:
                                dve.wait_ge(res_loaded[1 - b], (u - 1 - (1 - b)) * 8 + 16)
                                if isinstance(u, int):
                                    if (u - 1) // 2 > 0:
                                        dve.wait_ge(stored[1 - b], 16 + 16 * ((u - 1) // 2))
                                else:
                                    dve.wait_ge(stored[1 - b], 16 + (u - 1 - (1 - b)) * 8)
                            nc.vector.scalar_tensor_tensor(yout[:, 1 - b, t], ps_y[:, t % 2, 0:D], S * S, xres[:, 1 - b, t],
                                                           ALU.mult, ALU.add).then_inc(out_done, 1)
                    if n:
                        dve.wait_ge(xhi_done, c1 + m + 1)
                        for c in range(KC):
                            last = nc.vector.tensor_tensor(xlo[:, c], ps_x[:, c], xhi[:, c].bitcast(F32), ALU.subtract)
                        last.then_inc(xlo_done, 1)

                run_units(dve, step)

            @block.tensor
            def _(pe):
                start(pe, counters["pe"])

                def step(u, b, n, g, d):
                    for j in range(HC):
                        if g:
                            if j == 0:
                                pe.wait_ge(xlo_done, c1 + u + 1)
                            pe.wait_ge(hf_done, c1 + 6 * u + j - 1)
                            for i, wt in enumerate((wg, wu)):
                                ops = [(wt[:, a, c, j * P:j * P + P], (xhi, xlo)[x][:, c]) for c in range(KC)
                                       for a, x in ((0, 0), (0, 1), (1, 0))]
                                for k, (l, r) in enumerate(ops):
                                    last = nc.tensor.matmul(ps_g[:, j % 2, i], l, r, start=k == 0, stop=k == 5)
                            last.then_inc(gu_done, 1)
                        if d and j < 4:
                            if j == 0:
                                pe.wait_ge(hlo_done, c1 + 6 * u)
                            pe.wait_ge(out_done, c1 + 4 * (u - 1) + j - 1)
                            toks = slice(j * P, j * P + P)
                            ops = [((hhi, hlo)[a][:, 1 - b, c, toks], wd[:, x, c]) for c in range(HC)
                                   for a, x in ((0, 0), (0, 1), (1, 0))]
                            for k, (l, r) in enumerate(ops):
                                last = nc.tensor.matmul(ps_y[:, j % 2, 0:D], l, r, start=k == 0, stop=k == len(ops) - 1)
                            last.then_inc(y_done, 1)
                        if n and j == 4:
                            pe.wait_ge(xn_done, c1 + 4 * (u + 1) + 4)
                            pe.wait_ge(xlo_done, c1 + u + 1)
                            for q in range(QT):
                                for c in range(KC):
                                    last = nc.tensor.transpose(ps_x[:, c, q * P:q * P + P], xn[:, q, c * P:c * P + P], ident[:])
                            last.then_inc(xt_done, 1)

                run_units(pe, step)


def build(nc, ins, out, only=None):
    x = ins["x"]
    scratch = lambda name: nc.dram_tensor(name, [TOKENS, D], F32, kind="Internal").ap()
    x1 = out if only == "L0" else scratch("x1")
    x2 = out if only == "MOE" else scratch("x2")
    x3 = out if only == "L1" else scratch("x3")

    def natural(a):
        return lambda u: [a[bass.ds(u * UNIT + q * P, P), :] for q in range(2)]

    def wide(a):
        return lambda u: a[bass.ds(u * 512, 512), :].rearrange("(q p) d -> p q d", p=P)

    def by_position(a):
        v = a.rearrange("(b n) d -> n b d", b=16)
        return lambda u: [v[bass.ds(u * 16 + 8 * q, 8)] for q in range(2)]

    def weights(layer):
        w = {n: ins[f"{layer}_{n}"] for n in ("wq", "wk", "wv", "wo", "bq", "bk", "bv", "bo")}
        for n in ("wq", "wk", "wv", "wo"):
            w[n] = w[n].rearrange("(c p) n -> p c n", p=P)
        return w

    def tiles(a):
        return a.rearrange("(q p) k -> p q k", p=P)

    def ctx_units(a):
        return lambda u: a[:, bass.ds(u * UNIT, UNIT)].rearrange("(c p) t -> p c t", p=P)

    if only in (None, "L0"):
        attention(nc, "l0", natural(x), natural(x1), ctx_units(ins["ctxT0"]), weights("L0"), tiles(ins["mask"]), tiles(ins["maskT"]))
    if only in (None, "MOE"):
        with nc.sbuf_tensor("xt_hi", [P, KC, TOKENS], F16) as xt_hi, nc.sbuf_tensor("xt_lo", [P, KC, TOKENS], F16) as xt_lo, \
                nc.sbuf_tensor("xres", [P, TOKENS // P, D], F32) as xres, nc.sbuf_tensor("scores", [P, TOKENS // P, E], F32) as scores:
            norm_and_route(nc, ins["x1in"] if only else x1, ins, xt_hi, xt_lo, xres, scores)
            dense_experts(nc, x2, ins, xt_hi, xt_lo, xres, scores)
    if only in (None, "L1"):
        attention(nc, "l1", by_position(ins["x1in"] if only else x2), by_position(x3), ctx_units(ins["ctxT1"]), weights("L1"), tiles(ins["near"]), tiles(ins["near"]))
    if only in (None, "FFN"):
        gated_ffn(nc, wide(ins["x1in"] if only else x3), wide(out), ins)


_ORDER = np.array([(4 * jj + 2 * m + par) * DH + d for m in range(2) for par in range(2) for d in range(DH) for jj in range(4)])


def layout(i):
    a = {"x": i["x"].reshape(TOKENS, D)}
    ctx = i["ctx_1024"]
    a["ctxT0"] = ctx.transpose(2, 0, 1).reshape(D, TOKENS)
    a["ctxT1"] = ctx.transpose(2, 1, 0).reshape(D, TOKENS)
    a["mask"] = i["mask_1x1xSxS2_if1"][0, 0]
    a["maskT"] = a["mask"].T
    pos = np.arange(UNIT) // 16
    a["near"] = (pos[:, None] == pos[None, :]).astype(np.int32)
    for layer in ("L0", "L1"):
        for n in ("q", "k"):
            a[f"{layer}_w{n}"] = i[f"{layer}_xattn_W{n}"].T[:, _ORDER]
            a[f"{layer}_b{n}"] = i[f"{layer}_xattn_b{n}"][_ORDER].reshape(2, P).T
        a[f"{layer}_wv"] = i[f"{layer}_xattn_Wv"].T
        wo = np.zeros((H, 2, DH, D), np.float32)
        wo[:, 0] = i[f"{layer}_xattn_Wo"].T.reshape(H, DH, D)
        a[f"{layer}_wo"] = wo.reshape(2 * D, D)
        a[f"{layer}_bv"] = i[f"{layer}_xattn_bv"]
        a[f"{layer}_bo"] = i[f"{layer}_xattn_bo"]
    a["router_w"] = i["L0_ffn_router_w"]
    a["router_b"] = i["L0_ffn_router_b"]
    gu = i["L0_ffn_gate_up_proj"].reshape(E, D, D, 2).transpose(0, 1, 3, 2)
    a["gate_up"] = gu.reshape(E * D, 2 * D)
    a["gu_bias"] = i["L0_ffn_gate_up_bias"].reshape(E, D, 2).transpose(0, 2, 1).reshape(E * 4, P).T
    a["down"] = i["L0_ffn_down_proj"].reshape(E * D, D)
    a["d_bias"] = i["L0_ffn_down_bias"]
    a["wg"] = i["L1_ffn_w_gate"].T
    a["wu"] = i["L1_ffn_w_up"].T
    a["wd"] = i["L1_ffn_w_down"].T
    return {k: np.ascontiguousarray(v) for k, v in a.items()}


def kernel(**inputs):
    import concourse.bacc as bacc
    from concourse.bass_utils import run_bass_kernel_spmd

    arrays = {f"in_{k}": v for k, v in layout({k: np.asarray(v) for k, v in inputs.items()}).items()}
    nc = bacc.Bacc("TRN2", target_bir_lowering=False, num_devices=1)
    ins = {k[3:]: nc.dram_tensor(k, v.shape, mybir.dt.from_np(v.dtype), kind="ExternalInput").ap() for k, v in arrays.items()}
    out = nc.dram_tensor("out", [TOKENS, D], F32, kind="ExternalOutput").ap()
    build(nc, ins, out)
    r = run_bass_kernel_spmd(nc, [arrays], core_ids=[0])
    return r.results[0]["out"].reshape(16, 256, D)
```

```python
from contextlib import ExitStack

import numpy as np

import concourse.bass as bass
from concourse import mybir

ALU = mybir.AluOpType
ACT = mybir.ActivationFunctionType
F32 = mybir.dt.float32
F32R = mybir.dt.float32r
F16 = mybir.dt.float16
BF16 = mybir.dt.bfloat16
I32 = mybir.dt.int32
U32 = mybir.dt.uint32
AX_X = mybir.AxisListType.X

P = 128
D = 256
KC = D // P
TOKENS = 4096
H = 16
E = 16
DH = D // H
UNIT = 256
UNITS = TOKENS // UNIT
QT = UNIT // P
EPS = 1e-5
MSTEP = 32768.0
MASKED = 65280.0 * MSTEP
SLOT_ROWS = 256
TILES = 80
CREDIT = 16


def clear(nc, sems):
    with nc.Block() as block:
        @block.gpsimd
        def _(pool):
            for s in sems:
                pool.sem_clear(s)


def attention(nc, tag, x_in, x_out, ctx_t, w, mask_q, mask_k):
    with ExitStack() as ctx:
        def sb(name, shape, dt=F32):
            return ctx.enter_context(nc.sbuf_tensor(f"{tag}_{name}", shape, dt))

        sems = []

        def sem(name):
            sems.append(ctx.enter_context(nc.semaphore(f"{tag}_{name}")))
            return sems[-1]

        ps_s = ctx.enter_context(nc.psum_tensor(f"{tag}_ps_s", [P, 2, QT, UNIT], F32))
        ps_t = ctx.enter_context(nc.psum_tensor(f"{tag}_ps_t", [P, 2, QT, UNIT], F32))
        ps_o = ctx.enter_context(nc.psum_tensor(f"{tag}_ps_o", [P, 2, 2, UNIT], F32))
        ps_a = ctx.enter_context(nc.psum_tensor(f"{tag}_ps_a", [P, 2, UNIT], F32))
        ps_b = ctx.enter_context(nc.psum_tensor(f"{tag}_ps_b", [P, 2, UNIT], F32))

        w_raw = sb("w_raw", [P, 4, D])
        wq = sb("wq", [P, 2, KC, D], F32R)
        wk = sb("wk", [P, 2, KC, D], F32R)
        wv = sb("wv", [P, 2, KC, D], F32R)
        wo = sb("wo", [P, 2, 4, D], F32R)
        bq = sb("bq", [P, 2])
        bk = sb("bk", [P, 2])
        bv = sb("bv", [P, D])
        bo = sb("bo", [P, D])
        ident = sb("ident", [P, P])
        ident16 = sb("ident16", [P, P], BF16)
        mraw = sb("mraw", [P, 2, QT, UNIT], I32)
        mbias = sb("mbias", [P, 2, QT, UNIT], BF16)
        half = sb("half", [P, QT])
        xin = sb("xin", [P, 2, QT, D])
        xbo = sb("xbo", [P, 2, QT, D])
        cin = sb("cin", [P, 2, KC, UNIT])
        chi = sb("chi", [P, 2, KC, UNIT], F32R)
        clo = sb("clo", [P, 2, KC, UNIT], F32R)
        qs = sb("qs", [P, 2, 8, UNIT], F16)
        ks = sb("ks", [P, 2, 8, UNIT], F16)
        v1 = sb("v1", [P, 2, QT, H, 32])
        stats = sb("stats", [P, QT, 6])
        mv = sb("mv", [P, QT, 2])
        rstd = sb("rstd", [P, QT])
        xn = sb("xn", [P, QT, D])
        xhi = sb("xhi", [P, KC, UNIT], F32R)
        xlo = sb("xlo", [P, KC, UNIT], F32R)
        nat = sb("nat", [P, 4, 2, UNIT], F16)
        mx = sb("mx", [P, QT, H])
        mt = sb("mt", [H, 2, UNIT], F16)
        pt = sb("pt", [P, 4, QT, UNIT])
        rec = sb("rec", [P, 2, UNIT])
        recs = sb("recs", [P, 2, UNIT])
        an = sb("an", [P, 2, UNIT])
        ahi = sb("ahi", [P, 4, UNIT], F32R)
        alo = sb("alo", [P, 4, UNIT], F32R)
        yout = sb("yout", [P, 2, QT, D])

        w_loaded = sem("w_loaded")
        w_used = sem("w_used")
        const_loaded = sem("const_loaded")
        const_ready = sem("const_ready")
        gp = sem("gp_setup")
        apart = sem("apart")
        with nc.Block() as block:
            @block.sync
            def _(sp):
                sp.dma_start(bq[:], w["bq"]).then_inc(const_loaded, 16)
                sp.dma_start(bk[:], w["bk"]).then_inc(const_loaded, 16)
                sp.dma_start(bv[:], w["bv"].partition_broadcast(P)).then_inc(const_loaded, 16)
                sp.dma_start(bo[:], w["bo"].partition_broadcast(P)).then_inc(const_loaded, 16)
                sp.dma_start(mraw[:, 0], mask_q).then_inc(const_loaded, 16)
                sp.dma_start(mraw[:, 1], mask_k).then_inc(const_loaded, 16)
                for n, name in enumerate(("wq", "wk", "wv", "wo")):
                    if n:
                        sp.wait_ge(w_used, n)
                    sp.dma_start(w_raw[:, 0:4 if name == "wo" else 2, :], w[name]).then_inc(w_loaded, 16)

            @block.gpsimd
            def _(pool):
                nc.gpsimd.memset(ident[:], 0.0).then_inc(gp, 1)
                nc.gpsimd.memset(ident16[:], 0.0).then_inc(gp, 1)
                nc.gpsimd.memset(v1[:], 1.0).then_inc(gp, 1)
                nc.gpsimd.memset(half[:], -0.5).then_inc(gp, 1)
                pool.wait_ge(gp, 4)
                for m in (ident, ident16):
                    nc.gpsimd.affine_select(out=m[:], in_=m[:], compare_op=ALU.not_equal, fill=1.0, base=0,
                                            pattern=[[-1, P]], channel_multiplier=1).then_inc(gp, 1)

            @block.vector
            def _(dve):
                for top in (32, 96):
                    nc.vector.memset(ks[top:top + 32], -MSTEP)
                done = 0
                for n, (name, dst) in enumerate((("wq", wq), ("wk", wk), ("wv", wv), ("wo", wo))):
                    c = 4 if name == "wo" else 2
                    dve.wait_ge(w_loaded, 16 * (n + 1))
                    if name == "wq":
                        nc.vector.tensor_scalar(w_raw[:, 0:c], w_raw[:, 0:c], DH ** -0.5, None, ALU.mult).then_inc(const_ready, 1)
                        done += 1
                        dve.wait_ge(const_ready, done)
                    nc.vector.tensor_copy(dst[:, 0], w_raw[:, 0:c]).then_inc(const_ready, 1)
                    done += 1
                    dve.wait_ge(const_ready, done)
                    nc.vector.tensor_tensor(dst[:, 1], w_raw[:, 0:c], dst[:, 0].bitcast(F32), ALU.subtract).then_inc(w_used, 1)
                dve.wait_ge(const_loaded, 96)
                nc.vector.tensor_scalar(bq[:], bq[:], DH ** -0.5, None, ALU.mult)
                nc.vector.tensor_scalar(mbias[:], mraw[:], 0.0, -MASKED, ALU.is_equal, ALU.mult)

        c1 = CREDIT
        x_loaded = [sem("x_loaded0"), sem("x_loaded1")]; ctx_loaded = [sem("ctx_loaded0"), sem("ctx_loaded1")]
        stats_done = sem("stats_done"); mv_done = sem("mv_done"); rs1 = sem("rs1"); rstd_done = sem("rstd_done")
        xn_done = sem("xn_done"); xt_done = sem("xt_done"); xhi_done = sem("xhi_done"); xlo_done = sem("xlo_done")
        chi_done = sem("chi_done"); clo_done = sem("clo_done"); xbo_done = sem("xbo_done")
        q_done = sem("q_done"); k_done = sem("k_done"); v_done = sem("v_done")
        qh_done = sem("qh_done"); ql_done = sem("ql_done"); kh_done = sem("kh_done"); kl_done = sem("kl_done")
        v1_done = sem("v1_done"); qs_stacked = sem("qs_stacked"); ks_stacked = sem("ks_stacked")
        s_done = sem("s_done"); max_done = sem("max_done"); mtr_done = sem("mtr_done"); mh_done = sem("mh_done")
        ml_done = sem("ml_done"); m_stacked = sem("m_stacked")
        st_done = sem("st_done"); exp_done = sem("exp_done"); pv_done = sem("pv_done")
        rec_done = sem("rec_done"); recs_done = sem("recs_done"); an_done = sem("an_done")
        ahi_done = sem("ahi_done"); alo_done = sem("alo_done"); wo_done = sem("wo_done"); y_done = sem("y_done")
        stored = [sem("stored0"), sem("stored1")]
        counters = {
            "act": [xhi_done, qh_done, kh_done, mh_done, exp_done, ahi_done],
            "dve": [stats_done, mv_done, xn_done, xlo_done, ql_done, kl_done, v1_done, max_done, ml_done,
                    rec_done, recs_done, an_done, alo_done, y_done],
            "pool": [rs1, rstd_done, chi_done, clo_done, xbo_done],
            "pe": [xt_done, q_done, k_done, v_done, s_done, mtr_done, st_done, pv_done, wo_done],
        }

        def run_units(eng, step):
            step(-2, 0, False, False, True)
            step(-1, 1, False, True, True)
            with eng.Fori(0, UNITS // 2 - 1) as r:
                step(r * 2, 0, True, True, True)
                step(r * 2 + 1, 1, True, True, True)
            step(UNITS - 2, 0, True, True, False)
            step(UNITS - 1, 1, True, False, False)

        def start(eng, sems):
            for s in sems:
                eng.sem_inc(s, CREDIT)

        with nc.Block() as block:
            @block.sync
            def _(sp):
                def load(u, b):
                    sp.wait_ge(xn_done, c1 + 2 * (u - 1))
                    sp.wait_ge(xbo_done, c1 + u - 1)
                    for q, view in enumerate(x_in(u)):
                        sp.dma_start(xin[:, b, q], view).then_inc(x_loaded[b], 16)
                    sp.wait_ge(clo_done, c1 + u - 1)
                    sp.sem_inc(apart, 1)
                    sp.dma_start(cin[:, b], ctx_t(u)).then_inc(ctx_loaded[b], 16)

                def step(u, b, t, s, p):
                    if not s and not t:
                        load(0, 0)
                        load(1, 1)
                    if s:
                        for i, done in ((0, mh_done), (1, ml_done)):
                            sp.wait_ge(done, c1 + u + 2)
                            for par in range(2):
                                row = 64 * par + 48 + i
                                sp.dma_start(qs[row:row + 1, 1 - b], mt[8 * par:8 * par + 8, i, :]).then_inc(m_stacked, 16)
                    if p:
                        if t:
                            sp.wait_ge(st_done, c1 + 16 * u + 16)
                            sp.sem_inc(apart, 1)
                        for dst, stacked, hi, lo, hi_done, lo_done, order in (
                                (qs, qs_stacked, 0, 1, qh_done, ql_done, (0, 2, 1)),
                                (ks, ks_stacked, 2, 3, kh_done, kl_done, (0, 1, 2))):
                            parts = (hi, lo, hi) if dst is qs else (hi, hi, lo)
                            sp.wait_ge(hi_done, c1 + u + 3)
                            for n in order:
                                if parts[n] == lo:
                                    sp.wait_ge(lo_done, c1 + u + 3)
                                for par in range(2):
                                    row = 64 * par + 16 * n
                                    sp.dma_start(dst[row:row + 16, b].rearrange("d (j m) t -> d j (m t)", m=2),
                                                 nat[64 * par:64 * par + 64, parts[n]].rearrange("p m t -> p (m t)")
                                                 ).then_inc(stacked, 16)
                        if not isinstance(u, int) or u + 4 < UNITS:
                            load(u + 4, b)
                    if t:
                        sp.wait_ge(y_done, c1 + u + 1)
                        for q, view in enumerate(x_out(u)):
                            sp.dma_start(view, yout[:, b, q]).then_inc(stored[b], 16)

                for b in range(2):
                    sp.sem_inc(stored[b], 16)
                step(-2, 0, False, False, True)
                step(-1, 1, False, True, True)
                with sp.Fori(0, UNITS // 2 - 2) as r:
                    step(r * 2, 0, True, True, True)
                    step(r * 2 + 1, 1, True, True, True)
                step(UNITS - 4, 0, True, True, True)
                step(UNITS - 3, 1, True, True, True)
                step(UNITS - 2, 0, True, True, False)
                step(UNITS - 1, 1, True, False, False)
                for b in range(2):
                    sp.wait_ge(stored[b], 16 + 32 * (UNITS // 2))

            @block.gpsimd
            def _(pool):
                start(pool, counters["pool"])

                def step(u, b, t, s, p):
                    if not p:
                        return
                    n = u + 2
                    pool.wait_ge(mv_done, c1 + 2 * n + 2)
                    pool.wait_ge(xn_done, c1 + 2 * n)
                    pool.sem_inc(apart, 1)
                    nc.gpsimd.tensor_scalar(rstd[:], mv[:, :, 1], EPS, None, ALU.add).then_inc(rs1, 1)
                    pool.wait_ge(rs1, c1 + n + 1)
                    nc.gpsimd.tensor_tensor(rstd[:], rstd[:], half[:], ALU.pow).then_inc(rstd_done, 1)
                    pool.wait_ge(ctx_loaded[b], (n - b) * 8 + 16)
                    pool.wait_ge(v_done, c1 + n - 1)
                    pool.sem_inc(apart, 1)
                    nc.gpsimd.tensor_copy(chi[:, b], cin[:, b]).then_inc(chi_done, 1)
                    pool.wait_ge(chi_done, c1 + n + 1)
                    nc.gpsimd.tensor_tensor(clo[:, b], cin[:, b], chi[:, b].bitcast(F32), ALU.subtract).then_inc(clo_done, 1)
                    pool.wait_ge(x_loaded[b], (n - b) * 16 + 32)
                    pool.wait_ge(y_done, c1 + n - 1)
                    for q in range(QT):
                        last = nc.gpsimd.tensor_tensor(xbo[:, b, q], xin[:, b, q], bo[:], ALU.add)
                    last.then_inc(xbo_done, 1)

                run_units(pool, step)

            @block.scalar
            def _(act):
                start(act, counters["act"])

                def step(u, b, t, s, p):
                    def exps(h):
                        act.wait_ge(st_done, c1 + 16 * u + h + 1)
                        act.wait_ge(pv_done, c1 + 16 * u + h - 3)
                        nc.scalar.activation(pt[:, h % 4], ps_t[:, h % 2], ACT.Exp).then_inc(exp_done, 1)

                    def part_high(g):
                        act.wait_ge(an_done, c1 + 2 * u + g + 1)
                        act.wait_ge(wo_done, c1 + u)
                        nc.scalar.copy(ahi[:, 2 * g:2 * g + 2], an[:]).then_inc(ahi_done, 1)

                    for h in range(H):
                        if t:
                            exps(h)
                        if h == 9 and p:
                            act.wait_ge(xt_done, c1 + u + 3)
                            act.wait_ge(q_done, c1 + u + 2)
                            nc.scalar.copy(xhi[:], ps_a[:]).then_inc(xhi_done, 1)
                        if h == 12 and t:
                            part_high(0)
                    if s:
                        act.wait_ge(mtr_done, c1 + u + 2)
                        if not t:
                            pass
                        else:
                            act.wait_ge(m_stacked, 64 * (u + 1))
                        nc.scalar.activation(mt[:, 0, :], ps_b[0:H, 0, :], ACT.Copy, scale=1.0 / MSTEP).then_inc(mh_done, 1)
                    if t:
                        part_high(1)
                    if p:
                        if s or t:
                            act.wait_ge(qs_stacked, 96 * (u + 2))
                            act.wait_ge(ks_stacked, 96 * (u + 2))
                        act.wait_ge(q_done, c1 + u + 3)
                        for m in range(2):
                            last = nc.scalar.activation(nat[:, 0, m], ps_a[:, m], ACT.Identity, bias=bq[:, m:m + 1])
                        last.then_inc(qh_done, 1)
                        act.wait_ge(k_done, c1 + u + 3)
                        for m in range(2):
                            last = nc.scalar.activation(nat[:, 2, m], ps_b[:, m], ACT.Identity, bias=bk[:, m:m + 1])
                        last.then_inc(kh_done, 1)

                run_units(act, step)

            @block.vector
            def _(dve):
                start(dve, counters["dve"])

                def step(u, b, t, s, p):
                    n = u + 2

                    def norm_a(g):
                        dve.wait_ge(pv_done, c1 + 16 * u + 8 * g + 8)
                        dve.wait_ge(recs_done, c1 + 2 * u + g)
                        nc.vector.reciprocal(rec[:], ps_o[:, g]).then_inc(rec_done, 1)

                    def norm_b(g):
                        dve.wait_ge(rec_done, c1 + 2 * u + g + 1)
                        dve.wait_ge(an_done, c1 + 2 * u + g)
                        dve.sem_inc(apart, 1)
                        nc.vector.stream_shuffle(recs[:], rec[:], [16 + i % 16 for i in range(32)]).then_inc(recs_done, 1)
                        dve.wait_ge(recs_done, c1 + 2 * u + g + 1)
                        dve.wait_ge(ahi_done, c1 + 2 * u + g)
                        dve.wait_ge(alo_done, c1 + 2 * u + g)
                        nc.vector.tensor_tensor(an[:], ps_o[:, g], recs[:], ALU.mult).then_inc(an_done, 1)

                    def part_low(g):
                        dve.wait_ge(ahi_done, c1 + 2 * u + g + 1)
                        nc.vector.tensor_tensor(alo[:, 2 * g:2 * g + 2], an[:], ahi[:, 2 * g:2 * g + 2].bitcast(F32),
                                                ALU.subtract).then_inc(alo_done, 1)

                    for h in range(H):
                        if s:
                            dve.wait_ge(s_done, c1 + 16 * (u + 1) + h + 1)
                            if h == 0:
                                dve.wait_ge(mtr_done, c1 + u + 1)
                            nc.vector.reduce_max(mx[:, :, 8 * (h % 2) + h // 2], ps_s[:, h % 2], AX_X).then_inc(max_done, 1)
                        if p and h == 1:
                            dve.wait_ge(x_loaded[b], (n - b) * 16 + 32)
                            for q in range(QT):
                                nc.vector.bn_stats(stats[:, q], xin[:, b, q]).then_inc(stats_done, 1)
                            for q in range(QT):
                                dve.wait_ge(stats_done, c1 + 2 * n + 1 + q)
                                dve.wait_ge(rstd_done, c1 + n)
                                dve.sem_inc(apart, 1)
                                nc.vector.bn_aggr(mv[:, q], stats[:, q]).then_inc(mv_done, 1)
                        if p and h == 4:
                            dve.wait_ge(rstd_done, c1 + n + 1)
                            dve.wait_ge(xt_done, c1 + n)
                            for q in range(QT):
                                nc.vector.tensor_scalar(xn[:, q], xin[:, b, q], mv[:, q, 0:1], rstd[:, q:q + 1],
                                                        ALU.subtract, ALU.mult).then_inc(xn_done, 1)
                        if p and h == 9:
                            dve.wait_ge(xhi_done, c1 + n + 1)
                            dve.wait_ge(q_done, c1 + n)
                            nc.vector.tensor_tensor(xlo[:], ps_a[:], xhi[:].bitcast(F32), ALU.subtract).then_inc(xlo_done, 1)
                        if t and h == 10:
                            norm_a(0)
                        if t and h == 11:
                            norm_b(0)
                        if t and h == 13:
                            part_low(0)
                    if s:
                        dve.wait_ge(mh_done, c1 + u + 2)
                        if t:
                            dve.wait_ge(m_stacked, 64 * (u + 1))
                        nc.vector.scalar_tensor_tensor(mt[:, 1, :], ps_b[0:H, 0, :], 1.0 / MSTEP, mt[:, 0, :],
                                                       ALU.mult, ALU.subtract).then_inc(ml_done, 1)
                    if t:
                        norm_a(1)
                        norm_b(1)
                        part_low(1)
                    if p:
                        for part, done, hi_done, ps, bias, lo_done in (
                                (1, q_done, qh_done, ps_a, bq, ql_done), (3, k_done, kh_done, ps_b, bk, kl_done)):
                            dve.wait_ge(hi_done, c1 + n + 1)
                            if s or t:
                                dve.wait_ge(qs_stacked if part == 1 else ks_stacked, 96 * n)
                            for m in range(2):
                                last = nc.vector.scalar_tensor_tensor(nat[:, part, m], ps[:, m], bias[:, m:m + 1],
                                                                      nat[:, part - 1, m], ALU.add, ALU.subtract)
                            last.then_inc(lo_done, 1)
                        dve.wait_ge(v_done, c1 + n + 1)
                        if t:
                            dve.wait_ge(pv_done, c1 + 16 * u + 16)
                        for q in range(QT):
                            last = nc.vector.tensor_tensor(v1[:, b, q, :, 0:DH],
                                                           ps_a[:, q].rearrange("p (h d) -> p h d", d=DH),
                                                           bv[:].rearrange("p (h d) -> p h d", d=DH), ALU.add)
                        last.then_inc(v1_done, 1)
                    if t:
                        dve.wait_ge(wo_done, c1 + u + 1)
                        dve.wait_ge(xbo_done, c1 + u + 1)
                        if isinstance(u, int):
                            if u >= 2:
                                dve.wait_ge(stored[b], 16 + 32 * (u // 2))
                        else:
                            dve.wait_ge(stored[b], 16 + (u - b) * 16)
                        nc.vector.tensor_tensor(yout[:, b], ps_b[:], xbo[:, b], ALU.add).then_inc(y_done, 1)

                run_units(dve, step)

            @block.tensor
            def _(pe):
                start(pe, counters["pe"])

                def three(out, pairs):
                    ops = [(x, y) for ah, al, bh, bl in pairs for x, y in ((ah, bh), (ah, bl), (al, bh))]
                    for i, (x, y) in enumerate(ops):
                        last = nc.tensor.matmul(out, x, y, start=i == 0, stop=i == len(ops) - 1)
                    return last

                def step(u, b, t, s, p):
                    n = u + 2

                    def values(h):
                        pe.wait_ge(exp_done, c1 + 16 * u + h + 1)
                        if h % 8 == 0:
                            pe.wait_ge(an_done, c1 + 2 * u + h // 8 - 1)
                        j, i = h % 4, h // 4
                        for kt in range(QT):
                            last = nc.tensor.matmul(ps_o[32 * j:32 * j + 32, i // 2, i % 2], v1[:, b, kt, h],
                                                    pt[:, h % 4, kt], start=kt == 0, stop=kt == QT - 1,
                                                    tile_position=(0, 32 * j))
                        last.then_inc(pv_done, 1)

                    for h in range(H):
                        base = 64 * (h % 2)
                        if s:
                            if h == 0:
                                pe.wait_ge(qs_stacked, 96 * (u + 2))
                                pe.wait_ge(ks_stacked, 96 * (u + 2))
                            pe.wait_ge(max_done, c1 + 16 * (u + 1) + h - 1)
                            for q in range(QT):
                                nc.tensor.matmul(ps_s[:, h % 2, q], ident16[:], mbias[:, 0, q], start=True, stop=False)
                                last = nc.tensor.matmul(ps_s[:, h % 2, q], qs[base:base + 48, 1 - b, h // 2, q * P:q * P + P],
                                                        ks[base:base + 48, 1 - b, h // 2, :], start=False, stop=True)
                            last.then_inc(s_done, 1)
                        if t:
                            if h == 0:
                                pe.wait_ge(m_stacked, 64 * (u + 1))
                            pe.wait_ge(exp_done, c1 + 16 * u + h - 1)
                            for k in range(QT):
                                nc.tensor.matmul(ps_t[:, h % 2, k], ident16[:], mbias[:, 1, k], start=True, stop=False)
                                last = nc.tensor.matmul(ps_t[:, h % 2, k], ks[base:base + 50, b, h // 2, k * P:k * P + P],
                                                        qs[base:base + 50, b, h // 2, :], start=False, stop=True)
                            last.then_inc(st_done, 1)
                            if h >= 2:
                                if h == 2:
                                    pe.wait_ge(v1_done, c1 + u + 1)
                                values(h - 2)
                        if p and h == 7:
                            pe.wait_ge(xn_done, c1 + 2 * n + 2)
                            pe.wait_ge(v1_done, c1 + n)
                            for q in range(QT):
                                for c in range(KC):
                                    last = nc.tensor.transpose(ps_a[:, c, q * P:q * P + P], xn[:, q, c * P:c * P + P], ident[:])
                            last.then_inc(xt_done, 1)
                    if t:
                        values(14)
                        values(15)
                    if s:
                        pe.wait_ge(max_done, c1 + 16 * (u + 1) + 16)
                        pe.wait_ge(y_done, c1 + u)
                        for q in range(QT):
                            last = nc.tensor.transpose(ps_b[0:H, 0, q * P:q * P + P], mx[:, q, :], ident[:])
                        last.then_inc(mtr_done, 1)
                    if p:
                        pe.wait_ge(xlo_done, c1 + n + 1)
                        for m in range(2):
                            cols = slice(m * P, m * P + P)
                            last = three(ps_a[:, m], [(wq[:, 0, c, cols], wq[:, 1, c, cols], xhi[:, c], xlo[:, c]) for c in range(KC)])
                        last.then_inc(q_done, 1)
                        pe.wait_ge(clo_done, c1 + n + 1)
                        pe.wait_ge(ml_done, c1 + u + 2 if s else c1)
                        for m in range(2):
                            cols = slice(m * P, m * P + P)
                            last = three(ps_b[:, m], [(wk[:, 0, c, cols], wk[:, 1, c, cols], chi[:, b, c], clo[:, b, c]) for c in range(KC)])
                        last.then_inc(k_done, 1)
                        pe.wait_ge(ql_done, c1 + n + 1)
                        for q in range(QT):
                            toks = slice(q * P, q * P + P)
                            last = three(ps_a[:, q], [(chi[:, b, c, toks], clo[:, b, c, toks], wv[:, 0, c], wv[:, 1, c]) for c in range(KC)])
                        last.then_inc(v_done, 1)
                    if t:
                        if p:
                            pe.wait_ge(kl_done, c1 + n + 1)
                        elif s:
                            pe.wait_ge(ml_done, c1 + u + 2)
                        pe.wait_ge(alo_done, c1 + 2 * u + 2)
                        for q in range(QT):
                            toks = slice(q * P, q * P + P)
                            last = three(ps_b[:, q], [(ahi[:, i, toks], alo[:, i, toks], wo[:, 0, i], wo[:, 1, i]) for i in range(4)])
                        last.then_inc(wo_done, 1)

                run_units(pe, step)

        clear(nc, sems)


def routed_experts(nc, x_in, x_out, w):
    T = TOKENS // P
    C = 4
    CH = T // C
    K = 4
    R = SLOT_ROWS
    NH = TILES * (R // P)
    WS = 64.0
    LIMIT = 7.0
    ALPHA = 1.702
    with ExitStack() as ctx:
        def sb(name, shape, dt=F32):
            return ctx.enter_context(nc.sbuf_tensor(f"ex_{name}", shape, dt))

        def sem(name):
            return ctx.enter_context(nc.semaphore(f"ex_{name}"))

        rows_dram = nc.dram_tensor("moe_rows", [TOKENS, 2 * D], F16, kind="Internal").ap()
        y_dram = nc.dram_tensor("moe_out", [TILES * R, D], F32, kind="Internal").ap()

        gu_hi = sb("gu_hi", [P, E, KC, 2 * D], F16); gu_lo = sb("gu_lo", [P, E, KC, 2 * D], F16)
        dn_hi = sb("dn_hi", [P, E, KC, D], F16); dn_lo = sb("dn_lo", [P, E, KC, D], F16)
        g_bias = sb("g_bias", [P, E, 4]); d_bias = sb("d_bias", [E, D])
        scores = sb("scores", [P, T, E]); wts = sb("wts", [P, T, K]); pos = sb("pos", [P, T, K], U32)
        token = sb("token", [P, NH], U32)
        expert = sb("expert", [1, TILES], U32)
        ident = sb("ident", [P, P]); ident16 = sb("ident16", [P, P], F16)
        apart = sem("apart")

        with ExitStack() as rctx:
            def rt(name, shape, dt=F32):
                return rctx.enter_context(nc.sbuf_tensor(f"rt_{name}", shape, dt))

            def rsem(name):
                return rctx.enter_context(nc.semaphore(f"rt_{name}"))

            ps_x = rctx.enter_context(nc.psum_tensor("rt_ps_x", [P, KC, C * P], F32))
            ps_l = rctx.enter_context(nc.psum_tensor("rt_ps_l", [P, 2, 512], F32))
            ps_r = rctx.enter_context(nc.psum_tensor("rt_ps_r", [P, 2, 512], F32))
            ps_t = rctx.enter_context(nc.psum_tensor("rt_ps_t", [P, 512], F32))
            raw = rt("raw", [P, 2, 3, 2 * D])
            rw = rt("rw", [P, KC, E]); rb = rt("rb", [P, E]); half = rt("half", [P, C])
            before = rt("before", [P, P], BF16); ones = rt("ones", [P, P], BF16)
            iota = rt("iota", [P, E]); fills = rt("fills", [P, E]); row_iota = rt("row_iota", [P, P], F16)
            half_iota = rt("half_iota", [P, NH], F16); tile_iota = rt("tile_iota", [1, TILES])
            token_id = rt("token_id", [P, T]); carry = rt("carry", [P, E, T]); one_e = rt("one_e", [P, E])
            xin = rt("xin", [P, 2, C, D]); xn = rt("xn", [P, 2, C, D]); xh = rt("xh", [P, 2, C, 2, D], F16)
            stats = rt("stats", [P, C, 6]); mv = rt("mv", [P, C, 2]); rstd = rt("rstd", [P, C])
            xt = rt("xt", [P, KC, C * P])
            logits = rt("logits", [P, C, E]); high = rt("high", [P, C, 8]); where = rt("where", [P, C, 8], U32)
            best = rt("best", [P, T, K]); whichf = rt("whichf", [P, T, K])

            loaded = rsem("loaded"); gp = rsem("gp")
            x_loaded = [rsem("x_loaded0"), rsem("x_loaded1")]; w_loaded = [rsem("w_loaded0"), rsem("w_loaded1")]
            h_stored = [rsem("h_stored0"), rsem("h_stored1")]
            stats_done = rsem("stats_done"); mv_done = rsem("mv_done"); var_done = rsem("var_done"); rstd_done = rsem("rstd_done")
            xn_done = rsem("xn_done"); hi_done = rsem("hi_done"); lo_done = rsem("lo_done")
            xt_done = rsem("xt_done"); xt_copied = rsem("xt_copied"); lg_done = rsem("lg_done"); lg_added = rsem("lg_added")
            w_hi = rsem("w_hi"); w_lo = rsem("w_lo"); chosen = rsem("chosen"); max_done = rsem("max_done"); index_done = rsem("index_done")

            def chunks(eng, step):
                with eng.Fori(0, CH // 2 - 1) as r:
                    for b in range(2):
                        step(r * 2 + b, r, b, True)
                for b in range(2):
                    step(CH - 2 + b, CH // 2 - 1, b, False)

            with nc.Block() as block:
                @block.sync
                def _(sp):
                    sp.dma_start(rw[:], w["router_w"].rearrange("(c p) n -> p c n", p=P)).then_inc(loaded, 16)
                    sp.dma_start(rb[:], w["router_b"].partition_broadcast(P)).then_inc(loaded, 16)
                    sp.dma_start(g_bias[:].rearrange("p e f -> p (e f)"), w["gu_bias"]).then_inc(loaded, 16)
                    sp.dma_start(d_bias[:], w["d_bias"]).then_inc(loaded, 16)

                    def load(u, b):
                        sp.dma_start(xin[:, b], x_in[bass.ds(u * C * P, C * P), :].rearrange("(q p) d -> p q d", p=P)).then_inc(x_loaded[b], 16)

                    def load_weights(e, b):
                        sp.dma_start(raw[:, b, 0:KC], w["gate_up"][bass.ds(e * D, D), :].rearrange("(c p) n -> p c n", p=P)).then_inc(w_loaded[b], 16)
                        sp.dma_start(raw[:, b, KC].rearrange("p (c n) -> p c n", c=KC),
                                     w["down"][bass.ds(e * D, D), :].rearrange("(c p) n -> p c n", p=P)).then_inc(w_loaded[b], 16)

                    for b in range(2):
                        load(b, b)
                        load_weights(b, b)

                    def step(u, r, b, more):
                        if more:
                            sp.wait_ge(xn_done, u * C + C)
                            load(u + 2, b)
                        sp.wait_ge(hi_done, u + 1)
                        sp.sem_inc(apart, 1)
                        sp.wait_ge(lo_done, CREDIT + u + 1)
                        sp.sem_inc(apart, 1)
                        sp.dma_start(rows_dram[bass.ds(u * C * P, C * P), :].rearrange("(q p) d -> p q d", p=P),
                                     xh[:, b].rearrange("p q a d -> p q (a d)")).then_inc(h_stored[b], 16)
                        for n in range(2 if more or b == 0 else 0):
                            sp.wait_ge(w_lo, u * 4 + 2 * n + 2)
                            sp.sem_inc(apart, 1)
                            load_weights(u * 2 + n + 2, n)

                    chunks(sp, step)
                    for b in range(2):
                        sp.wait_ge(h_stored[b], 16 * (CH // 2 + 1))

                @block.gpsimd
                def _(pool):
                    sets = ((ident, 0.0), (ident16, 0.0), (half, -0.5), (before, 0.0), (ones, 1.0), (carry, 1.0), (one_e, 1.0))
                    for t, v in sets:
                        nc.gpsimd.memset(t[:], v).then_inc(gp, 1)
                    nc.gpsimd.iota(iota[:], [[1, E]], base=0, channel_multiplier=0, allow_small_or_imprecise_dtypes=True).then_inc(gp, 1)
                    nc.gpsimd.iota(fills[:], [[R, E]], base=0, channel_multiplier=0, allow_small_or_imprecise_dtypes=True).then_inc(gp, 1)
                    nc.gpsimd.iota(row_iota[:], [[1, P]], base=0, channel_multiplier=0, allow_small_or_imprecise_dtypes=True).then_inc(gp, 1)
                    nc.gpsimd.iota(half_iota[:], [[1, NH]], base=0, channel_multiplier=0, allow_small_or_imprecise_dtypes=True).then_inc(gp, 1)
                    nc.gpsimd.iota(tile_iota[:], [[1, TILES]], base=0, channel_multiplier=0, allow_small_or_imprecise_dtypes=True).then_inc(gp, 1)
                    nc.gpsimd.iota(token_id[:], [[P, T]], base=-TOKENS // 2, channel_multiplier=1, allow_small_or_imprecise_dtypes=True).then_inc(gp, 1)
                    pool.wait_ge(gp, 13)
                    for m in (ident, ident16):
                        nc.gpsimd.affine_select(out=m[:], in_=m[:], compare_op=ALU.not_equal, fill=1.0, base=0,
                                                pattern=[[-1, P]], channel_multiplier=1).then_inc(gp, 1)
                    nc.gpsimd.affine_select(out=before[:], in_=before[:], compare_op=ALU.is_ge, fill=1.0, base=0,
                                            pattern=[[-1, P]], channel_multiplier=1).then_inc(gp, 1)
                    nc.gpsimd.memset(carry[:, :, 0:1], 0.0).then_inc(gp, 1)

                    def step(u, r, b, more):
                        pool.wait_ge(mv_done, u * C + C)
                        pool.sem_inc(apart, 1)
                        nc.gpsimd.tensor_scalar(rstd[:], mv[:, :, 1], EPS, None, ALU.add).then_inc(var_done, 1)
                        pool.wait_ge(var_done, u + 1)
                        nc.gpsimd.tensor_tensor(rstd[:], rstd[:], half[:], ALU.pow).then_inc(rstd_done, 1)
                        pool.wait_ge(hi_done, u + 1)
                        nc.gpsimd.tensor_tensor(xh[:, b, :, 1], xn[:, b], xh[:, b, :, 0], ALU.subtract).then_inc(lo_done, 1)

                    pool.sem_inc(lo_done, CREDIT)
                    chunks(pool, step)

                @block.vector
                def _(dve):
                    dve.wait_ge(gp, 17)
                    dve.wait_ge(loaded, 64)
                    nc.vector.tensor_scalar(g_bias[:], g_bias[:], WS, None, ALU.mult).then_inc(chosen, 1)
                    dve.wait_ge(chosen, 1)
                    nc.vector.tensor_scalar(g_bias[:, :, 2:4], g_bias[:, :, 2:4], WS, None, ALU.add)
                    dve.sem_inc(lg_added, CREDIT)

                    def step(u, r, b, more):
                        dve.wait_ge(x_loaded[b], r * 16 + 16)
                        dve.sem_inc(apart, 1)
                        for q in range(C):
                            nc.vector.bn_stats(stats[:, q], xin[:, b, q]).then_inc(stats_done, 1)
                        dve.wait_ge(stats_done, u * C + C)
                        dve.sem_inc(apart, 1)
                        for q in range(C):
                            nc.vector.bn_aggr(mv[:, q], stats[:, q]).then_inc(mv_done, 1)
                        for n in range(2):
                            e = u * 2 + n
                            dve.wait_ge(w_hi, e * 2 + 2)
                            nc.vector.scalar_tensor_tensor(gu_lo[:, bass.ds(e, 1)].rearrange("p o c n -> p (o c) n"), raw[:, n, 0:KC], WS,
                                                           gu_hi[:, bass.ds(e, 1)].rearrange("p o c n -> p (o c) n"), ALU.mult, ALU.subtract).then_inc(w_lo, 1)
                            nc.vector.scalar_tensor_tensor(dn_lo[:, bass.ds(e, 1)].rearrange("p o c n -> p (o c) n"), raw[:, n, KC].rearrange("p (c n) -> p c n", c=KC), WS,
                                                           dn_hi[:, bass.ds(e, 1)].rearrange("p o c n -> p (o c) n"), ALU.mult, ALU.subtract).then_inc(w_lo, 1)
                        dve.wait_ge(rstd_done, u + 1)
                        dve.wait_ge(lo_done, CREDIT + u - 1)
                        dve.wait_ge(xt_done, CREDIT + u - 1)
                        for q in range(C):
                            nc.vector.tensor_scalar(xn[:, b, q], xin[:, b, q], mv[:, q, 0:1], rstd[:, q:q + 1], ALU.subtract, ALU.mult).then_inc(xn_done, 1)
                        dve.wait_ge(lg_done, CREDIT + u + 1)
                        nc.vector.tensor_tensor(logits[:], ps_l[:, b, 0:C * E].rearrange("p (q e) -> p q e", e=E),
                                                rb[:].unsqueeze(1).to_broadcast([P, C, E]), ALU.add).then_inc(lg_added, 1)
                        dve.wait_ge(lg_added, CREDIT + u + 1)
                        dve.sem_inc(apart, 1)
                        for q in range(C):
                            nc.vector.max(high[:, q], logits[:, q]).then_inc(max_done, 1)
                        dve.wait_ge(max_done, u * C + C)
                        dve.sem_inc(apart, 1)
                        for q in range(C):
                            nc.vector.max_index(where[:, q], high[:, q], logits[:, q]).then_inc(index_done, 1)
                        nc.vector.tensor_copy(best[:, bass.ds(u * C, C)], high[:, :, 0:K]).then_inc(chosen, 1)
                        dve.wait_ge(index_done, u * C + C)
                        nc.vector.tensor_copy(whichf[:, bass.ds(u * C, C)], where[:, :, 0:K]).then_inc(chosen, 1)

                    chunks(dve, step)

                @block.scalar
                def _(act):
                    def step(u, r, b, more):
                        for n in range(2):
                            e = u * 2 + n
                            act.wait_ge(w_loaded[n], u * 32 + 32)
                            nc.scalar.activation(gu_hi[:, bass.ds(e, 1)].rearrange("p o c n -> p (o c) n"), raw[:, n, 0:KC], ACT.Copy, scale=WS).then_inc(w_hi, 1)
                            nc.scalar.activation(dn_hi[:, bass.ds(e, 1)].rearrange("p o c n -> p (o c) n"), raw[:, n, KC].rearrange("p (c n) -> p c n", c=KC), ACT.Copy, scale=WS).then_inc(w_hi, 1)
                        act.wait_ge(xn_done, u * C + C)
                        act.wait_ge(h_stored[b], r * 16 + 16)
                        nc.scalar.copy(xh[:, b, :, 0], xn[:, b]).then_inc(hi_done, 1)
                        act.wait_ge(xt_done, CREDIT + u + 1)
                        nc.scalar.copy(xt[:], ps_x[:]).then_inc(xt_copied, 1)

                    for s in h_stored:
                        act.sem_inc(s, 16)
                    chunks(act, step)

                @block.tensor
                def _(pe):
                    def step(u, r, b, more):
                        pe.wait_ge(xn_done, u * C + C)
                        for q in range(C):
                            for c in range(KC):
                                last = nc.tensor.transpose(ps_x[:, c, q * P:q * P + P], xn[:, b, q, c * P:c * P + P], ident[:])
                        last.then_inc(xt_done, 1)
                        pe.wait_ge(xt_copied, u + 1)
                        pe.wait_ge(lg_added, CREDIT + u - 1)
                        for q in range(C):
                            for c in range(KC):
                                last = nc.tensor.matmul(ps_l[:, b, q * E:q * E + E], xt[:, c, q * P:q * P + P], rw[:, c], start=c == 0, stop=c == KC - 1)
                        last.then_inc(lg_done, 1)

                    pe.wait_ge(gp, 17)
                    pe.wait_ge(loaded, 64)
                    for s in (xt_done, lg_done):
                        pe.sem_inc(s, CREDIT)
                    chunks(pe, step)

            ex = rt("ex", [P, T, K]); total = rt("total", [P, T])
            hot = rt("hot", [P, T, K, E]); prod = rt("prod", [P, T, K, E]); took = rt("took", [P, T, E], BF16)
            sums = rt("sums", [P, T, E]); upto = rt("upto", [P, E, T]); rank = rt("rank", [P, T, E])
            over = rt("over", [P, E, E]); tiles = rt("tiles", [P, E]); end = rt("end", [P, E]); first = rt("first", [P, E])
            posf = rt("posf", [P, T, K]); lane = rt("lane", [P, T, K], U32); group = rt("group", [P, T, K], U32)
            lanef = rt("lanef", [P, T, K], F16); groupf = rt("groupf", [P, T, K])
            past = rt("past", [1, TILES, E]); owner = rt("owner", [1, TILES]); tokenf = rt("tokenf", [P, NH])
            at_lane = rt("at_lane", [P, 4, K, P], F16); at_group = rt("at_group", [P, 4, K, NH], F16)
            step_done = rsem("step_done"); ex_done = rsem("ex_done"); took_done = rsem("took_done"); rank_done = rsem("rank_done")
            lanes_done = rsem("lanes_done"); groups_done = rsem("groups_done"); added = rsem("added"); inverted = rsem("inverted")
            with nc.Block() as block:
                @block.vector
                def _(dve):
                    n = 0

                    def then(ins):
                        nonlocal n
                        n += 1
                        ins.then_inc(step_done, 1)
                        dve.wait_ge(step_done, n)

                    nc.vector.tensor_tensor(ex[:], best[:, :, 0:K], best[:, :, 0:1].to_broadcast([P, T, K]), ALU.subtract).then_inc(ex_done, 1)
                    then(nc.vector.tensor_tensor(hot[:], whichf[:].unsqueeze(3).to_broadcast([P, T, K, E]),
                                                 iota[:].unsqueeze(1).unsqueeze(1).to_broadcast([P, T, K, E]), ALU.is_equal))
                    then(nc.vector.reduce_sum(sums[:], hot[:].rearrange("p t k e -> p t e k"), axis=AX_X))
                    nc.vector.tensor_copy(took[:], sums[:]).then_inc(took_done, 1)
                    dve.wait_ge(ex_done, 2)
                    then(nc.vector.reduce_sum(total[:], ex[:], axis=AX_X))
                    then(nc.vector.reciprocal(total[:], total[:]))
                    then(nc.vector.tensor_tensor(wts[:], ex[:], total[:].unsqueeze(2).to_broadcast([P, T, K]), ALU.mult))
                    then(nc.vector.tensor_tensor(prod[:], hot[:], wts[:].unsqueeze(3).to_broadcast([P, T, K, E]), ALU.mult))
                    then(nc.vector.reduce_sum(scores[:], prod[:].rearrange("p t k e -> p t e k"), axis=AX_X))
                    dve.wait_ge(rank_done, 1)
                    then(nc.vector.tensor_copy(sums[:], ps_r[:, 0].rearrange("p (t e) -> p t e", e=E)))
                    then(nc.vector.tensor_copy(prod[:, 0:T // K].rearrange("p a k e -> p (a k e)").rearrange("p (e t) -> p e t", e=E), sums[:].rearrange("p t e -> p e t")))
                    then(nc.vector.tensor_tensor_scan(upto[:].rearrange("p e t -> p (e t)"), carry[:].rearrange("p e t -> p (e t)"),
                                                      prod[:, 0:T // K].rearrange("p a k e -> p (a k e)"), 0.0, ALU.mult, ALU.add))
                    then(nc.vector.tensor_tensor(over[:], upto[:, :, T - 1:T].to_broadcast([P, E, E]),
                                                 fills[:].unsqueeze(1).to_broadcast([P, E, E]), ALU.is_gt))
                    then(nc.vector.reduce_sum(tiles[:], over[:], axis=AX_X))
                    then(nc.vector.tensor_tensor_scan(end[:], one_e[:], tiles[:], 0.0, ALU.mult, ALU.add))
                    then(nc.vector.tensor_tensor(first[:], end[:], tiles[:], ALU.subtract))
                    then(nc.vector.tensor_scalar(first[:], first[:], float(R), None, ALU.mult))
                    then(nc.vector.tensor_tensor(rank[:], upto[:].rearrange("p e t -> p t e"), sums[:], ALU.subtract))
                    then(nc.vector.tensor_tensor(rank[:], rank[:], ps_r[:, 1].rearrange("p (t e) -> p t e", e=E), ALU.add))
                    then(nc.vector.tensor_tensor(rank[:], rank[:], first[:].unsqueeze(1).to_broadcast([P, T, E]), ALU.add))
                    then(nc.vector.tensor_tensor(prod[:], hot[:], rank[:].unsqueeze(2).to_broadcast([P, T, K, E]), ALU.mult))
                    then(nc.vector.reduce_sum(posf[:], prod[:], axis=AX_X))
                    then(nc.vector.tensor_copy(pos[:], posf[:]))
                    nc.vector.tensor_scalar(lane[:], pos[:], P - 1, None, ALU.bitwise_and).then_inc(step_done, 1)
                    then(nc.vector.tensor_scalar(group[:], pos[:], 7, None, ALU.logical_shift_right))
                    n += 1
                    dve.wait_ge(step_done, n)
                    nc.vector.tensor_copy(lanef[:], lane[:]).then_inc(step_done, 1)
                    then(nc.vector.tensor_copy(groupf[:], group[:]))
                    n += 1
                    dve.wait_ge(step_done, n)
                    for t in range(T):
                        s = t % 4
                        if t >= 4:
                            dve.wait_ge(added, t - 3)
                        nc.vector.tensor_tensor(at_lane[:, s], lanef[:, t].unsqueeze(2).to_broadcast([P, K, P]),
                                                row_iota[:].unsqueeze(1).to_broadcast([P, K, P]), ALU.is_equal).then_inc(lanes_done, 1)
                        for k in range(K):
                            nc.vector.tensor_scalar(at_group[:, s, k], half_iota[:], groupf[:, t, k:k + 1], token_id[:, t:t + 1],
                                                    ALU.is_equal, ALU.mult).then_inc(groups_done, 1)
                    then(nc.vector.tensor_tensor(past[:], end[0:1].unsqueeze(1).to_broadcast([1, TILES, E]),
                                                 tile_iota[:].unsqueeze(2).to_broadcast([1, TILES, E]), ALU.is_le))
                    then(nc.vector.reduce_sum(owner[:], past[:], axis=AX_X))
                    nc.vector.tensor_scalar(expert[:], owner[:], float(E - 1), None, ALU.min)
                    dve.wait_ge(inverted, 1)
                    then(nc.vector.tensor_scalar(tokenf[:], ps_t[:, 0:NH], float(TOKENS // 2), None, ALU.add))
                    nc.vector.tensor_copy(token[:], tokenf[:])

                @block.scalar
                def _(act):
                    act.wait_ge(ex_done, 1)
                    nc.scalar.activation(ex[:], ex[:], ACT.Exp).then_inc(ex_done, 1)

                @block.tensor
                def _(pe):
                    pe.wait_ge(took_done, 1)
                    nc.tensor.matmul(ps_r[:, 0], ones[:], took[:].rearrange("p t e -> p (t e)"), start=True, stop=True)
                    nc.tensor.matmul(ps_r[:, 1], before[:], took[:].rearrange("p t e -> p (t e)"), start=True, stop=True).then_inc(rank_done, 1)
                    for t in range(T):
                        pe.wait_ge(lanes_done, t + 1)
                        pe.wait_ge(groups_done, K * (t + 1))
                        for k in range(K):
                            last = nc.tensor.matmul(ps_t[:, 0:NH], at_lane[:, t % 4, k], at_group[:, t % 4, k],
                                                    start=t == 0 and k == 0, stop=t == T - 1 and k == K - 1)
                        last.then_inc(added, 1)
                    pe.wait_ge(added, T)
                    pe.sem_inc(inverted, 1)

        with ExitStack() as cctx:
            def cb(name, shape, dt=F32):
                return cctx.enter_context(nc.sbuf_tensor(f"cp_{name}", shape, dt))

            def csem(name):
                return cctx.enter_context(nc.semaphore(f"cp_{name}"))

            ps_x = cctx.enter_context(nc.psum_tensor("cp_ps_x", [P, 2, 2, KC, R], F16))
            ps_g = cctx.enter_context(nc.psum_tensor("cp_ps_g", [P, 2, 4, R], F32))
            ps_y = cctx.enter_context(nc.psum_tensor("cp_ps_y", [P, 2, 2, D], F32))
            slot_token = cb("slot_token", [P, 2, 2], U32)
            rows = cb("rows", [P, 2, 2, 2 * D], F16)
            xt = cb("xt", [P, 2, 2, KC, R], F16)
            gate = cb("gate", [P, 2, 2, R]); up = cb("up", [P, 2, 2, R]); sg = cb("sg", [P, 2, 2, R])
            act_f = cb("act_f", [P, 2, 2, R]); a_hi = cb("a_hi", [P, 2, 2, R], F16); a_lo = cb("a_lo", [P, 2, 2, R], F16)
            yout = cb("yout", [P, 2, 2, D])
            idx_set = csem("idx_set"); xt_done = csem("xt_done"); xt_copied = csem("xt_copied"); gu_done = csem("gu_done")
            gate_done = csem("gate_done"); up_done = csem("up_done"); upg_done = csem("upg_done"); sg_done = csem("sg_done")
            act_done = csem("act_done"); ahi_done = csem("ahi_done"); alo_done = csem("alo_done")
            y_done = csem("y_done"); y_copied = csem("y_copied")
            gathered = [csem("gathered0"), csem("gathered1")]; stored = [csem("stored0"), csem("stored1")]

            def run(eng, counts, step):
                for s in counts:
                    eng.sem_inc(s, CREDIT)
                for i in range(-2, 2):
                    step(i, i % 2)
                with eng.Fori(1, TILES // 2 - 1) as r:
                    for b in range(2):
                        step(r * 2 + b, b)
                for i in range(TILES - 2, TILES + 2):
                    step(i, i % 2)

            def live(i, ahead):
                return not isinstance(i, int) or 0 <= i + ahead < TILES

            def at(i, each=1):
                return i * each + (each + CREDIT)

            def at_gather(i, b):
                return (i - b) * 16 + 32

            def at_store(i, b):
                return (i - b) * 8 + (16 + PAIR_CREDIT)

            PAIR_CREDIT = 64

            def expert_of(i, engine):
                return nc.values_load(expert[0:1, bass.ds(i, 1)], engines=[engine], min_val=0, max_val=E - 1,
                                      skip_runtime_bounds_check_because="the minimum with E - 1 bounds it")

            with nc.Block() as block:
                @block.sync
                def _(sp):
                    def step(i, b):
                        if live(i, -2):
                            sp.wait_ge(y_copied, at(i - 2))
                            sp.sem_inc(apart, 1)
                            sp.dma_start(y_dram[bass.ds((i - 2) * R, R), :].rearrange("(q p) d -> p q d", p=P), yout[:, b]).then_inc(stored[b], 16)

                    for s in stored:
                        sp.sem_inc(s, PAIR_CREDIT)
                    run(sp, [], step)
                    for b in range(2):
                        sp.wait_ge(stored[b], at_store(TILES - 2 + b, b))

                @block.gpsimd
                def _(pool):
                    def step(i, b):
                        if live(i, 2):
                            pool.wait_ge(idx_set, at(i + 2))
                            pool.wait_ge(xt_done, at(i))
                            pool.sem_inc(apart, 1)
                            for h in range(2):
                                nc.gpsimd.indirect_dma_start(rows[:, b, h], None, rows_dram[:, :],
                                                             bass.IndirectOffsetOnAxis(ap=slot_token[:, b, h:h + 1], axis=0)).then_inc(gathered[b], 16)
                        if live(i, 0):
                            pool.wait_ge(ahi_done, at(i))
                            pool.wait_ge(y_done, at(i - 2))
                            nc.gpsimd.tensor_tensor(a_lo[:, b], act_f[:, b], a_hi[:, b], ALU.subtract).then_inc(alo_done, 1)

                    run(pool, [alo_done], step)

                @block.vector
                def _(dve):
                    def step(i, b):
                        if live(i, 2):
                            if live(i, 0):
                                dve.wait_ge(gathered[b], at_gather(i, b))
                            nc.vector.tensor_copy(slot_token[:, b], token[:, bass.ds(i * 2 + 4, 2)]).then_inc(idx_set, 1)
                        if live(i, 0):
                            e = expert_of(i, mybir.EngineType.DVE)
                            dve.wait_ge(gu_done, at(i))
                            for m in range(2):
                                nc.vector.tensor_scalar(gate[:, b, m], ps_g[:, b, m], g_bias[:, bass.ds(e, 1), m], LIMIT * WS, ALU.add, ALU.min).then_inc(gate_done, 1)
                            for m in range(2):
                                nc.vector.tensor_scalar(up[:, b, m], ps_g[:, b, 2 + m], g_bias[:, bass.ds(e, 1), 2 + m], (1 - LIMIT) * WS, ALU.add, ALU.max).then_inc(up_done, 1)
                            dve.wait_ge(up_done, at(i, 2))
                            nc.vector.scalar_tensor_tensor(up[:, b], up[:, b], (1 + LIMIT) * WS, gate[:, b], ALU.min, ALU.mult).then_inc(upg_done, 1)
                            dve.wait_ge(upg_done, at(i))
                            dve.wait_ge(sg_done, at(i))
                            dve.wait_ge(alo_done, at(i - 2))
                            nc.vector.scalar_tensor_tensor(act_f[:, b], up[:, b], 1.0 / (WS * WS), sg[:, b], ALU.mult, ALU.mult).then_inc(act_done, 1)

                    run(dve, [idx_set, gate_done, up_done, upg_done, act_done], step)

                @block.scalar
                def _(act):
                    def step(i, b):
                        if live(i, 1):
                            act.wait_ge(xt_done, at(i + 1))
                            act.wait_ge(gu_done, at(i - 1))
                            nc.scalar.copy(xt[:, 1 - b], ps_x[:, 1 - b]).then_inc(xt_copied, 1)
                        if live(i, 0):
                            act.wait_ge(gate_done, at(i, 2))
                            act.wait_ge(act_done, at(i - 2))
                            nc.scalar.activation(sg[:, b], gate[:, b], ACT.Sigmoid, scale=ALPHA / WS).then_inc(sg_done, 1)
                            act.wait_ge(act_done, at(i))
                            act.wait_ge(y_done, at(i - 2))
                            nc.scalar.copy(a_hi[:, b], act_f[:, b]).then_inc(ahi_done, 1)
                        if live(i, -2):
                            act.wait_ge(y_done, at(i - 2))
                            act.wait_ge(stored[b], at_store(i - 4, b))
                            nc.scalar.activation(yout[:, b], ps_y[:, b], ACT.Copy, scale=1.0 / WS).then_inc(y_copied, 1)

                    run(act, [xt_copied, sg_done, ahi_done, y_copied], step)

                @block.tensor
                def _(pe):
                    def step(i, b):
                        if live(i, 1):
                            n = 1 - b
                            pe.wait_ge(gathered[n], at_gather(i + 1, n))
                            pe.wait_ge(xt_copied, at(i - 1))
                            for part in range(2):
                                for c in range(KC):
                                    for h in range(2):
                                        last = nc.tensor.transpose(ps_x[:, n, part, c, h * P:h * P + P], rows[:, n, h, part * D + c * P:part * D + c * P + P], ident16[:])
                            last.then_inc(xt_done, 1)
                        if live(i, 0):
                            e = expert_of(i, mybir.EngineType.PE)
                            pe.wait_ge(xt_copied, at(i))
                            pe.wait_ge(gate_done, at(i - 2, 2))
                            pe.wait_ge(up_done, at(i - 2, 2))
                            pe.sem_inc(apart, 1)
                            for m in range(4):
                                ops = [(wt, part, c) for c in range(KC) for wt, part in ((gu_hi, 0), (gu_hi, 1), (gu_lo, 0))]
                                for n, (wt, part, c) in enumerate(ops):
                                    last = nc.tensor.matmul(ps_g[:, b, m], wt[:, bass.ds(e, 1), c, m * P:m * P + P].rearrange("p o n -> p (o n)"),
                                                            xt[:, b, part, c], start=n == 0, stop=n == len(ops) - 1)
                            last.then_inc(gu_done, 1)
                        if live(i, -2):
                            e = expert_of(i - 2, mybir.EngineType.PE)
                            pe.wait_ge(alo_done, at(i - 2))
                            pe.wait_ge(y_copied, at(i - 4))
                            for h in range(2):
                                ops = [(a, wt, c) for c in range(KC) for a, wt in ((a_hi, dn_hi), (a_hi, dn_lo), (a_lo, dn_hi))]
                                for n, (a, wt, c) in enumerate(ops):
                                    last = nc.tensor.matmul(ps_y[:, b, h], a[:, b, c, h * P:h * P + P], wt[:, bass.ds(e, 1), c].rearrange("p o n -> p (o n)"),
                                                            start=n == 0, stop=n == len(ops) - 1)
                            last.then_inc(y_done, 1)

                    run(pe, [xt_done, gu_done, y_done], step)

        with ExitStack() as mctx:
            def mb(name, shape, dt=F32):
                return mctx.enter_context(nc.sbuf_tensor(f"cb_{name}", shape, dt))

            def msem(name):
                return mctx.enter_context(nc.semaphore(f"cb_{name}"))

            ps_s = mctx.enter_context(nc.psum_tensor("cb_ps_s", [P, 2, 512], F32))
            ps_d = mctx.enter_context(nc.psum_tensor("cb_ps_d", [P, 2, 512], F32))
            xin = mb("xin", [P, 2, D]); picked = mb("picked", [P, 2, K, D]); slot = mb("slot", [P, 2, K], U32)
            sc = mb("sc", [P, 2, E]); sct = mb("sct", [E, 2, P]); acc = mb("acc", [P, 2, D])
            x_loaded = [msem("x_loaded0"), msem("x_loaded1")]; picked_done = [msem("picked0"), msem("picked1")]
            stored = [msem("stored0"), msem("stored1")]
            slot_set = msem("slot_set"); sc_set = msem("sc_set"); sct_done = msem("sct_done"); sct_copied = msem("sct_copied"); bias_done = msem("bias_done"); added = msem("added")

            def tiles_of(eng, counts, step):
                for s in counts:
                    eng.sem_inc(s, CREDIT)
                step(0, 0, True)
                step(1, 1, True)
                with eng.Fori(1, T // 2) as r:
                    for b in range(2):
                        step(r * 2 + b, b, False)

            with nc.Block() as block:
                @block.sync
                def _(sp):
                    def load(t, b):
                        sp.dma_start(xin[:, b], x_in[bass.ds(t * P, P), :]).then_inc(x_loaded[b], 16)

                    def store(t, b):
                        sp.wait_ge(added, t * 5 + (CREDIT + 5))
                        sp.sem_inc(apart, 1)
                        sp.dma_start(x_out[bass.ds(t * P, P), :], acc[:, b]).then_inc(stored[b], 16)

                    for b in range(2):
                        load(b, b)
                    with sp.Fori(0, T // 2 - 1) as r:
                        for b in range(2):
                            store(r * 2 + b, b)
                            load(r * 2 + b + 2, b)
                    for b in range(2):
                        store(T - 2 + b, b)
                    for b in range(2):
                        sp.wait_ge(stored[b], 8 * T)

                @block.gpsimd
                def _(pool):
                    def step(t, b, fresh):
                        pool.wait_ge(slot_set, t + (CREDIT + 1))
                        pool.wait_ge(added, t * 5 + (CREDIT - 5))
                        pool.sem_inc(apart, 1)
                        for k in range(K):
                            nc.gpsimd.indirect_dma_start(picked[:, b, k], None, y_dram[:, :],
                                                         bass.IndirectOffsetOnAxis(ap=slot[:, b, k:k + 1], axis=0)).then_inc(picked_done[b], 16)

                    tiles_of(pool, [], step)

                @block.vector
                def _(dve):
                    def set_slots(t, b):
                        nc.vector.tensor_copy(slot[:, b], pos[:, bass.ds(t, 1)].rearrange("p o k -> p (o k)")).then_inc(slot_set, 1)

                    def step(t, b, last):
                        dve.wait_ge(x_loaded[b], (t - b) * 8 + 16)
                        dve.wait_ge(bias_done, t + (CREDIT + 1))
                        if not (isinstance(t, int) and t < 2):
                            dve.wait_ge(stored[b], (t - b) * 8)
                        nc.vector.tensor_tensor(acc[:, b], xin[:, b], ps_d[:, b, 0:D], ALU.add).then_inc(added, 1)
                        dve.wait_ge(picked_done[b], (t - b) * 32 + 64)
                        for k in range(K):
                            dve.wait_ge(added, t * 5 + (CREDIT + 1 + k))
                            nc.vector.scalar_tensor_tensor(acc[:, b], picked[:, b, k], wts[:, bass.ds(t, 1), k], acc[:, b], ALU.mult, ALU.add).then_inc(added, 1)
                        if not last:
                            set_slots(t + 2, b)

                    for s in (slot_set, added):
                        dve.sem_inc(s, CREDIT)
                    for b in range(2):
                        set_slots(b, b)
                    for b in range(2):
                        step(b, b, False)
                    with dve.Fori(1, T // 2 - 1) as r:
                        for b in range(2):
                            step(r * 2 + b, b, False)
                    for b in range(2):
                        step(T - 2 + b, b, True)

                @block.scalar
                def _(act):
                    def step(t, b, fresh):
                        act.wait_ge(sct_done, t + (CREDIT - 1))
                        nc.scalar.copy(sc[:, b], scores[:, bass.ds(t, 1)].rearrange("p o e -> p (o e)")).then_inc(sc_set, 1)
                        act.wait_ge(sct_done, t + (CREDIT + 1))
                        act.wait_ge(bias_done, t + (CREDIT - 1))
                        nc.scalar.copy(sct[:, b], ps_s[0:E, b, 0:P]).then_inc(sct_copied, 1)

                    tiles_of(act, [sct_copied, sc_set], step)

                @block.tensor
                def _(pe):
                    def step(t, b, fresh):
                        pe.wait_ge(sc_set, t + (CREDIT + 1))
                        pe.wait_ge(sct_copied, t + (CREDIT - 1))
                        nc.tensor.transpose(ps_s[0:E, b, 0:P], sc[:, b], ident[:]).then_inc(sct_done, 1)
                        pe.wait_ge(sct_copied, t + (CREDIT + 1))
                        pe.wait_ge(added, t * 5 + (CREDIT - 5))
                        nc.tensor.matmul(ps_d[:, b, 0:D], sct[:, b], d_bias[:], start=True, stop=True).then_inc(bias_done, 1)

                    tiles_of(pe, [sct_done, bias_done], step)


def gated_ffn(nc, x_in, x_out, w):
    U = 512
    UN = TOKENS // U
    QT = U // P
    HC = 768 // P
    S = float(np.float32(1.0 / 127.0))
    with ExitStack() as ctx:
        def sb(name, shape, dt=F32):
            return ctx.enter_context(nc.sbuf_tensor(f"ff_{name}", shape, dt))

        def sem(name):
            return ctx.enter_context(nc.semaphore(f"ff_{name}"))

        ps_x = ctx.enter_context(nc.psum_tensor("ff_ps_x", [P, KC, U], F32))
        ps_g = ctx.enter_context(nc.psum_tensor("ff_ps_g", [P, 2, 2, U], F32))
        ps_y = ctx.enter_context(nc.psum_tensor("ff_ps_y", [P, 2, U], F32))
        wint = sb("wint", [P, 768], I32)
        wf = sb("wf", [P, 768])
        wg = sb("wg", [P, 2, KC, 768], F32R)
        wu = sb("wu", [P, 2, KC, 768], F32R)
        wd = sb("wd", [P, 2, HC, D], F32R)
        ident = sb("ident", [P, P]); half = sb("half", [P, QT])
        xin = sb("xin", [P, 2, QT, D])
        xres = sb("xres", [P, 2, QT, D])
        stats = sb("stats", [P, QT, 6]); mv = sb("mv", [P, QT, 2]); rstd = sb("rstd", [P, QT])
        xn = sb("xn", [P, QT, D])
        xhi = sb("xhi", [P, KC, U], F32R); xlo = sb("xlo", [P, KC, U], F32R)
        sg = sb("sg", [P, 2, U]); hf = sb("hf", [P, 2, U])
        hhi = sb("hhi", [P, 2, HC, U], F32R); hlo = sb("hlo", [P, 2, HC, U], F32R)
        yout = sb("yout", [P, 2, QT, D])

        w_loaded = sem("w_loaded"); w_split = sem("w_split"); gp = sem("gp"); apart = sem("apart")
        with nc.Block() as block:
            @block.sync
            def _(sp):
                n = 0
                for c in range(KC):
                    for name in ("wg", "wu"):
                        if n:
                            sp.wait_ge(w_split, 3 * n)
                        sp.dma_start(wint[:], w[name][c * P:c * P + P, :]).then_inc(w_loaded, 16)
                        n += 1
                for g in range(2):
                    sp.wait_ge(w_split, 3 * n)
                    sp.dma_start(wint[:].rearrange("p (c n) -> p c n", n=D), w["wd"][g * 384:g * 384 + 384, :].rearrange("(c p) n -> p c n", p=P)).then_inc(w_loaded, 16)
                    n += 1

            @block.gpsimd
            def _(pool):
                nc.gpsimd.memset(ident[:], 0.0).then_inc(gp, 1)
                nc.gpsimd.memset(half[:], -0.5).then_inc(gp, 1)
                pool.wait_ge(gp, 2)
                nc.gpsimd.affine_select(out=ident[:], in_=ident[:], compare_op=ALU.not_equal, fill=1.0, base=0,
                                        pattern=[[-1, P]], channel_multiplier=1).then_inc(gp, 1)

            @block.vector
            def _(dve):
                parts = [(t[:, 0, c], t[:, 1, c]) for c in range(KC) for t in (wg, wu)]
                parts += [(wd[:, 0, 3 * g:3 * g + 3].rearrange("p c n -> p (c n)"),
                           wd[:, 1, 3 * g:3 * g + 3].rearrange("p c n -> p (c n)")) for g in range(2)]
                for n, (hi, lo) in enumerate(parts):
                    dve.wait_ge(w_loaded, 16 * n + 16)
                    nc.vector.tensor_copy(wf[:], wint[:]).then_inc(w_split, 1)
                    dve.wait_ge(w_split, 3 * n + 1)
                    nc.vector.tensor_copy(hi, wf[:]).then_inc(w_split, 1)
                    dve.wait_ge(w_split, 3 * n + 2)
                    nc.vector.tensor_tensor(lo, wf[:], hi.bitcast(F32), ALU.subtract).then_inc(w_split, 1)
                    dve.wait_ge(w_split, 3 * n + 3)

        c1 = CREDIT
        x_loaded = [sem("x_loaded0"), sem("x_loaded1")]
        res_loaded = [sem("res_loaded0"), sem("res_loaded1")]
        stats_done = sem("stats_done"); mv_done = sem("mv_done"); rs1 = sem("rs1"); rstd_done = sem("rstd_done")
        xn_done = sem("xn_done"); xt_done = sem("xt_done"); xhi_done = sem("xhi_done"); xlo_done = sem("xlo_done")
        gu_done = sem("gu_done"); sg_done = sem("sg_done"); hf_done = sem("hf_done"); hhi_done = sem("hhi_done")
        hlo_done = sem("hlo_done"); y_done = sem("y_done"); out_done = sem("out_done")
        stored = [sem("stored0"), sem("stored1")]
        counters = {
            "act": [xhi_done, sg_done, hhi_done],
            "dve": [stats_done, mv_done, xn_done, xlo_done, hf_done, out_done],
            "pool": [rs1, rstd_done, hlo_done],
            "pe": [xt_done, gu_done, y_done],
        }

        def start(eng, sems):
            for s in sems:
                eng.sem_inc(s, CREDIT)

        def run_units(eng, step):
            step(-1, 1, True, False, False)
            step(0, 0, True, True, False)
            with eng.Fori(0, UN // 2 - 1) as r:
                step(r * 2 + 1, 1, True, True, True)
                step(r * 2 + 2, 0, True, True, True)
            step(UN - 1, 1, False, True, True)
            step(UN, 0, False, False, True)

        with nc.Block() as block:
            @block.sync
            def _(sp):
                def step(u, b, more, here, d):
                    if more:
                        sp.wait_ge(xn_done, c1 + 4 * (u + 1))
                        sp.dma_start(xin[:, b], x_in(u + 2)).then_inc(x_loaded[b], 16)
                    if here:
                        sp.wait_ge(out_done, c1 + 4 * (u - 1))
                        sp.dma_start(xres[:, b], x_in(u)).then_inc(res_loaded[b], 16)
                    if d:
                        sp.wait_ge(out_done, c1 + 4 * u)
                        sp.dma_start(x_out(u - 1), yout[:, 1 - b]).then_inc(stored[1 - b], 16)

                for b in range(2):
                    sp.sem_inc(stored[b], 16)
                step(-2, 0, True, False, False)
                step(-1, 1, True, False, False)
                step(0, 0, True, True, False)
                with sp.Fori(0, UN // 2 - 2) as r:
                    step(r * 2 + 1, 1, True, True, True)
                    step(r * 2 + 2, 0, True, True, True)
                step(UN - 3, 1, True, True, True)
                step(UN - 2, 0, False, True, True)
                step(UN - 1, 1, False, True, True)
                step(UN, 0, False, False, True)
                for b in range(2):
                    sp.wait_ge(stored[b], 16 + 16 * (UN // 2))

            @block.gpsimd
            def _(pool):
                start(pool, counters["pool"])

                def step(u, b, n, g, d):
                    def low(j):
                        pool.wait_ge(hhi_done, c1 + 6 * u + j + 1)
                        nc.gpsimd.tensor_tensor(hlo[:, b, j], hf[:, j % 2], hhi[:, b, j].bitcast(F32), ALU.subtract).then_inc(hlo_done, 1)

                    for j in range(HC):
                        if g:
                            low(j)
                        if n and j == 0:
                            pool.wait_ge(mv_done, c1 + 4 * (u + 1) + 4)
                            pool.wait_ge(xn_done, c1 + 4 * (u + 1))
                            pool.sem_inc(apart, 1)
                            nc.gpsimd.tensor_scalar(rstd[:], mv[:, :, 1], EPS, None, ALU.add).then_inc(rs1, 1)
                            pool.wait_ge(rs1, c1 + u + 2)
                            nc.gpsimd.tensor_tensor(rstd[:], rstd[:], half[:], ALU.pow).then_inc(rstd_done, 1)

                run_units(pool, step)

            @block.scalar
            def _(act):
                start(act, counters["act"])

                def step(u, b, n, g, d):
                    def silu(j):
                        act.wait_ge(gu_done, c1 + 6 * u + j + 1)
                        act.wait_ge(hf_done, c1 + 6 * u + j - 1)
                        nc.scalar.activation(sg[:, j % 2], ps_g[:, j % 2, 0], ACT.Silu, scale=S).then_inc(sg_done, 1)

                    def high(j):
                        act.wait_ge(hf_done, c1 + 6 * u + j + 1)
                        if j == 0:
                            act.wait_ge(y_done, c1 + 4 * (u - 1))
                        nc.scalar.copy(hhi[:, b, j], hf[:, j % 2]).then_inc(hhi_done, 1)

                    if g:
                        for j in range(HC):
                            silu(j)
                            if j:
                                high(j - 1)
                    if n:
                        act.wait_ge(xt_done, c1 + u + 2)
                        for c in range(KC):
                            last = nc.scalar.copy(xhi[:, c], ps_x[:, c])
                        last.then_inc(xhi_done, 1)
                    if g:
                        high(HC - 1)

                run_units(act, step)

            @block.vector
            def _(dve):
                start(dve, counters["dve"])

                def step(u, b, n, g, d):
                    m = u + 1
                    for j in range(HC):
                        if g:
                            dve.wait_ge(sg_done, c1 + 6 * u + j + 1)
                            dve.wait_ge(hlo_done, c1 + 6 * u + j - 1)
                            nc.vector.tensor_tensor(hf[:, j % 2], ps_g[:, j % 2, 1], sg[:, j % 2], ALU.mult).then_inc(hf_done, 1)
                        if n and j == 0:
                            dve.wait_ge(x_loaded[1 - b], (m - (1 - b)) * 8 + 16)
                            for q in range(QT):
                                nc.vector.bn_stats(stats[:, q], xin[:, 1 - b, q]).then_inc(stats_done, 1)
                            for q in range(QT):
                                dve.wait_ge(stats_done, c1 + 4 * m + 1 + q)
                                dve.sem_inc(apart, 1)
                                nc.vector.bn_aggr(mv[:, q], stats[:, q]).then_inc(mv_done, 1)
                        if n and j == 2:
                            dve.wait_ge(rstd_done, c1 + m + 1)
                            dve.wait_ge(xt_done, c1 + m)
                            for q in range(QT):
                                nc.vector.tensor_scalar(xn[:, q], xin[:, 1 - b, q], mv[:, q, 0:1], rstd[:, q:q + 1],
                                                        ALU.subtract, ALU.mult).then_inc(xn_done, 1)
                        if d and j >= 2:
                            t = j - 2
                            dve.wait_ge(y_done, c1 + 4 * (u - 1) + t + 1)
                            if t == 0:
                                dve.wait_ge(res_loaded[1 - b], (u - 1 - (1 - b)) * 8 + 16)
                                if isinstance(u, int):
                                    if (u - 1) // 2 > 0:
                                        dve.wait_ge(stored[1 - b], 16 + 16 * ((u - 1) // 2))
                                else:
                                    dve.wait_ge(stored[1 - b], 16 + (u - 1 - (1 - b)) * 8)
                            nc.vector.scalar_tensor_tensor(yout[:, 1 - b, t], ps_y[:, t % 2, 0:D], S * S, xres[:, 1 - b, t],
                                                           ALU.mult, ALU.add).then_inc(out_done, 1)
                    if n:
                        dve.wait_ge(xhi_done, c1 + m + 1)
                        for c in range(KC):
                            last = nc.vector.tensor_tensor(xlo[:, c], ps_x[:, c], xhi[:, c].bitcast(F32), ALU.subtract)
                        last.then_inc(xlo_done, 1)

                run_units(dve, step)

            @block.tensor
            def _(pe):
                start(pe, counters["pe"])

                def step(u, b, n, g, d):
                    for j in range(HC):
                        if g:
                            if j == 0:
                                pe.wait_ge(xlo_done, c1 + u + 1)
                            pe.wait_ge(hf_done, c1 + 6 * u + j - 1)
                            for i, wt in enumerate((wg, wu)):
                                ops = [(wt[:, a, c, j * P:j * P + P], (xhi, xlo)[x][:, c]) for c in range(KC)
                                       for a, x in ((0, 0), (0, 1), (1, 0))]
                                for k, (l, r) in enumerate(ops):
                                    last = nc.tensor.matmul(ps_g[:, j % 2, i], l, r, start=k == 0, stop=k == 5)
                            last.then_inc(gu_done, 1)
                        if d and j < 4:
                            if j == 0:
                                pe.wait_ge(hlo_done, c1 + 6 * u)
                            pe.wait_ge(out_done, c1 + 4 * (u - 1) + j - 1)
                            toks = slice(j * P, j * P + P)
                            ops = [((hhi, hlo)[a][:, 1 - b, c, toks], wd[:, x, c]) for c in range(HC)
                                   for a, x in ((0, 0), (0, 1), (1, 0))]
                            for k, (l, r) in enumerate(ops):
                                last = nc.tensor.matmul(ps_y[:, j % 2, 0:D], l, r, start=k == 0, stop=k == len(ops) - 1)
                            last.then_inc(y_done, 1)
                        if n and j == 4:
                            pe.wait_ge(xn_done, c1 + 4 * (u + 1) + 4)
                            pe.wait_ge(xlo_done, c1 + u + 1)
                            for q in range(QT):
                                for c in range(KC):
                                    last = nc.tensor.transpose(ps_x[:, c, q * P:q * P + P], xn[:, q, c * P:c * P + P], ident[:])
                            last.then_inc(xt_done, 1)

                run_units(pe, step)


def build(nc, ins, out, only=None):
    x = ins["x"]
    scratch = lambda name: nc.dram_tensor(name, [TOKENS, D], F32, kind="Internal").ap()
    x1 = out if only == "L0" else scratch("x1")
    x2 = out if only == "MOE" else scratch("x2")
    x3 = out if only == "L1" else scratch("x3")

    def natural(a):
        return lambda u: [a[bass.ds(u * UNIT + q * P, P), :] for q in range(2)]

    def wide(a):
        return lambda u: a[bass.ds(u * 512, 512), :].rearrange("(q p) d -> p q d", p=P)

    def by_position(a):
        v = a.rearrange("(b n) d -> n b d", b=16)
        return lambda u: [v[bass.ds(u * 16 + 8 * q, 8)] for q in range(2)]

    def weights(layer):
        w = {n: ins[f"{layer}_{n}"] for n in ("wq", "wk", "wv", "wo", "bq", "bk", "bv", "bo")}
        for n in ("wq", "wk", "wv", "wo"):
            w[n] = w[n].rearrange("(c p) n -> p c n", p=P)
        return w

    def tiles(a):
        return a.rearrange("(q p) k -> p q k", p=P)

    def ctx_units(a):
        return lambda u: a[:, bass.ds(u * UNIT, UNIT)].rearrange("(c p) t -> p c t", p=P)

    if only in (None, "L0"):
        attention(nc, "l0", natural(x), natural(x1), ctx_units(ins["ctxT0"]), weights("L0"), tiles(ins["mask"]), tiles(ins["maskT"]))
    if only in (None, "MOE"):
        routed_experts(nc, ins["x1in"] if only else x1, x2, ins)
    if only in (None, "L1"):
        attention(nc, "l1", by_position(ins["x1in"] if only else x2), by_position(x3), ctx_units(ins["ctxT1"]), weights("L1"), tiles(ins["near"]), tiles(ins["near"]))
    if only in (None, "FFN"):
        gated_ffn(nc, wide(ins["x1in"] if only else x3), wide(out), ins)


_ORDER = np.array([(4 * jj + 2 * m + par) * DH + d for m in range(2) for par in range(2) for d in range(DH) for jj in range(4)])


def layout(i):
    a = {"x": i["x"].reshape(TOKENS, D)}
    ctx = i["ctx_1024"]
    a["ctxT0"] = ctx.transpose(2, 0, 1).reshape(D, TOKENS)
    a["ctxT1"] = ctx.transpose(2, 1, 0).reshape(D, TOKENS)
    a["mask"] = i["mask_1x1xSxS2_if1"][0, 0]
    a["maskT"] = a["mask"].T
    pos = np.arange(UNIT) // 16
    a["near"] = (pos[:, None] == pos[None, :]).astype(np.int32)
    for layer in ("L0", "L1"):
        for n in ("q", "k"):
            a[f"{layer}_w{n}"] = i[f"{layer}_xattn_W{n}"].T[:, _ORDER]
            a[f"{layer}_b{n}"] = i[f"{layer}_xattn_b{n}"][_ORDER].reshape(2, P).T
        a[f"{layer}_wv"] = i[f"{layer}_xattn_Wv"].T
        wo = np.zeros((H, 2, DH, D), np.float32)
        wo[:, 0] = i[f"{layer}_xattn_Wo"].T.reshape(H, DH, D)
        a[f"{layer}_wo"] = wo.reshape(2 * D, D)
        a[f"{layer}_bv"] = i[f"{layer}_xattn_bv"]
        a[f"{layer}_bo"] = i[f"{layer}_xattn_bo"]
    a["router_w"] = i["L0_ffn_router_w"]
    a["router_b"] = i["L0_ffn_router_b"]
    gu = i["L0_ffn_gate_up_proj"].reshape(E, D, D, 2).transpose(0, 1, 3, 2)
    a["gate_up"] = gu.reshape(E * D, 2 * D)
    a["gu_bias"] = i["L0_ffn_gate_up_bias"].reshape(E, D, 2).transpose(0, 2, 1).reshape(E * 4, P).T
    a["down"] = i["L0_ffn_down_proj"].reshape(E * D, D)
    a["d_bias"] = i["L0_ffn_down_bias"]
    a["wg"] = i["L1_ffn_w_gate"].T
    a["wu"] = i["L1_ffn_w_up"].T
    a["wd"] = i["L1_ffn_w_down"].T
    return {k: np.ascontiguousarray(v) for k, v in a.items()}


def kernel(**inputs):
    import concourse.bacc as bacc
    from concourse.bass_utils import run_bass_kernel_spmd

    arrays = {f"in_{k}": v for k, v in layout({k: np.asarray(v) for k, v in inputs.items()}).items()}
    nc = bacc.Bacc("TRN2", target_bir_lowering=False, num_devices=1)
    ins = {k[3:]: nc.dram_tensor(k, v.shape, mybir.dt.from_np(v.dtype), kind="ExternalInput").ap() for k, v in arrays.items()}
    out = nc.dram_tensor("out", [TOKENS, D], F32, kind="ExternalOutput").ap()
    build(nc, ins, out)
    r = run_bass_kernel_spmd(nc, [arrays], core_ids=[0])
    return r.results[0]["out"].reshape(16, 256, D)
```

```python
from contextlib import ExitStack

import numpy as np

import concourse.bass as bass
from concourse import mybir

ALU = mybir.AluOpType
ACT = mybir.ActivationFunctionType
F32 = mybir.dt.float32
F32R = mybir.dt.float32r
F16 = mybir.dt.float16
BF16 = mybir.dt.bfloat16
I32 = mybir.dt.int32
U32 = mybir.dt.uint32
AX_X = mybir.AxisListType.X

P = 128
D = 256
KC = D // P
TOKENS = 4096
H = 16
E = 16
DH = D // H
UNIT = 256
UNITS = TOKENS // UNIT
QT = UNIT // P
EPS = 1e-5
MSTEP = 32768.0
MASKED = 65280.0 * MSTEP
SLOT_ROWS = 256
TILES = 80
LAG = 2
WHEN0 = {"v1": 1, "stats": 0, "xn": 4, "xT": 6, "xhi": 6, "xlo": 8, "q": 11, "qh": 13, "ql": 14, "k": 13, "kh": 14, "kl": 16, "wo": 1, "y": 2}
WHEN1 = {"v1": 1, "add": 0, "stats": 0, "xn": 3, "xT": 6, "xhi": 7, "xlo": 9, "q": 11, "qh": 13, "ql": 14, "k": 15, "kh": 16, "kl": 17, "wo": 1, "y": 4}
CREDIT = 16


def clear(nc, sems):
    with nc.Block() as block:
        @block.gpsimd
        def _(pool):
            for s in sems:
                pool.sem_clear(s)


def run_by_flag(nc, pe, flag, when_zero, when_one):
    value = nc.values_load(flag, engines=[mybir.EngineType.PE], min_val=0, max_val=1,
                           skip_runtime_bounds_check_because="the minimum with 1 bounds it")
    with pe.If(value == 0):
        when_zero()
    with pe.Else():
        when_one()


def attention(nc, tag, x_in, x_out, ctx_t, w, masks, query_rows, key_rows, when, rows=None):
    with ExitStack() as ctx:
        def sb(name, shape, dt=F32):
            return ctx.enter_context(nc.sbuf_tensor(f"{tag}_{name}", shape, dt))

        adding = rows is not None
        K = 4
        kinds = query_rows is not None
        span = P if kinds else UNIT
        rows_s = 96 + (8 if kinds else 0)
        rows_t = rows_s + 4

        sems = []

        def sem(name):
            sems.append(ctx.enter_context(nc.semaphore(f"{tag}_{name}")))
            return sems[-1]

        ps_s = ctx.enter_context(nc.psum_tensor(f"{tag}_ps_s", [P, 2, QT, UNIT], F32))
        ps_t = ctx.enter_context(nc.psum_tensor(f"{tag}_ps_t", [P, 2, QT, UNIT], F32))
        ps_o = ctx.enter_context(nc.psum_tensor(f"{tag}_ps_o", [P, 2, 2, UNIT], F32))
        ps_a = ctx.enter_context(nc.psum_tensor(f"{tag}_ps_a", [P, 2, UNIT], F32))
        ps_b = ctx.enter_context(nc.psum_tensor(f"{tag}_ps_b", [P, 2, UNIT], F32))

        w_raw = sb("w_raw", [P, 10, D])
        wq = sb("wq", [P, 2, KC, D], F32R)
        wk = sb("wk", [P, 2, KC, D], F32R)
        wv = sb("wv", [P, 2, KC, D], F32R)
        wo = sb("wo", [P, 2, 4, D], F32R)
        bq = sb("bq", [P, 2])
        bk = sb("bk", [P, 2])
        bv = sb("bv", [P, D])
        bo = sb("bo", [P, D])
        ident = sb("ident", [P, P])
        ident16 = sb("ident16", [P, P], BF16)
        if masks:
            mraw = sb("mraw", [P, 2, QT, UNIT], I32)
            mbias = sb("mbias", [P, 2, QT, UNIT], BF16)
            lowest = sb("lowest", [P, 1]); ones = sb("ones", [P, 1]); count = sb("count", [1, 1]); any_masked = sb("any_masked", [1, 1], U32)
        half = sb("half", [P, QT])
        if adding:
            y_rows, slots_view, weights_view = rows
            slots = sb("slots", [P, UNITS * QT, K], U32)
            wts = sb("wts", [P, UNITS * QT, K])
            slot = sb("slot", [P, QT, K], U32)
            picked = sb("picked", [P, QT, K, D])
            tables_loaded = sem("tables_loaded"); slot_set = sem("slot_set"); picked_up = sem("picked_up"); added = sem("added")
        xin = sb("xin", [P, 2, QT, D])
        xbo = sb("xbo", [P, 2, QT, D])
        cin = sb("cin", [P, 2, KC, UNIT])
        chi = sb("chi", [P, 2, KC, UNIT], F32R)
        clo = sb("clo", [P, 2, KC, UNIT], F32R)
        qs = sb("qs", [P, 2, 8, UNIT], F16)
        ks = sb("ks", [P, 2, H, UNIT], F16)
        v1 = sb("v1", [P, 2, QT, H, 32])
        stats = sb("stats", [P, QT, 6])
        mv = sb("mv", [P, QT, 2])
        rstd = sb("rstd", [P, QT])
        xn = sb("xn", [P, QT, D])
        xhi = sb("xhi", [P, KC, UNIT], F32R)
        xlo = sb("xlo", [P, KC, UNIT], F32R)
        nat = sb("nat", [P, 4, 2, UNIT], F16)
        mx = sb("mx", [P, QT, H])
        mt = sb("mt", [H, 2, UNIT], F16)
        pt = sb("pt", [P, 8, QT, span])
        rec = sb("rec", [P, UNIT])
        recs = sb("recs", [P, UNIT])
        an = sb("an", [P, 2, UNIT])
        ahi = sb("ahi", [P, 4, UNIT], F32R)
        alo = sb("alo", [P, 4, UNIT], F32R)
        yout = sb("yout", [P, 2, QT, D])

        x_loaded = [sem("x_loaded0"), sem("x_loaded1")]
        ctx_loaded = [sem("ctx_loaded0"), sem("ctx_loaded1")]
        w_loaded = [sem(f"w_loaded{n}") for n in range(4)]
        w_high = sem("w_high")
        const_loaded = sem("const_loaded")
        ks_set = sem("ks_set")
        rows_loaded = sem("rows_loaded")
        gp = sem("gp_setup")
        flagged = sem("flagged")
        counted = sem("counted")
        apart = sem("apart")
        scale = DH ** -0.5
        weights = [(w[name], dst, w_raw[:, 2 * n:2 * n + (4 if name == "wo" else 2)], scale if name == "wq" else 1.0)
                   for n, (name, dst) in enumerate((("wq", wq), ("wk", wk), ("wv", wv), ("wo", wo)))]

        def load_unit(sp, u, b):
            for q, view in enumerate(x_in(u)):
                sp.dma_start(xin[:, b, q], view).then_inc(x_loaded[b], 16)
            sp.dma_start(cin[:, b], ctx_t(u)).then_inc(ctx_loaded[b], 16)

        with nc.Block() as block:
            @block.sync
            def _(sp):
                for n, (src, dst, raw, by) in enumerate(weights):
                    sp.dma_start(raw, src).then_inc(w_loaded[n], 16)
                    if n < 2:
                        load_unit(sp, n, n)
                sp.dma_start(bq[:], w["bq"]).then_inc(const_loaded, 16)
                sp.dma_start(bk[:], w["bk"]).then_inc(const_loaded, 16)
                sp.dma_start(bv[:], w["bv"].partition_broadcast(P)).then_inc(const_loaded, 16)
                sp.dma_start(bo[:], w["bo"].partition_broadcast(P)).then_inc(const_loaded, 16)
                if adding:
                    for n in range(8):
                        sp.dma_start(slots[16 * n:16 * n + 16], slots_view(n)).then_inc(tables_loaded, 16)
                        sp.dma_start(wts[16 * n:16 * n + 16], weights_view(n)).then_inc(tables_loaded, 16)
                    sp.wait_ge(tables_loaded, 256)
                for i in range(2):
                    if masks:
                        sp.dma_start(mraw[:, i], masks[i]).then_inc(const_loaded, 16)
                sp.wait_ge(ks_set, 1)
                sp.dma_start(ks[96:rows_t].rearrange("p b h t -> p (b h t)"), key_rows).then_inc(rows_loaded, 16)
                if kinds:
                    sp.dma_start(qs[96:rows_s].rearrange("p b h t -> p (b h t)"), query_rows).then_inc(rows_loaded, 16)

            @block.scalar
            def _(act):
                for n, (src, dst, raw, by) in enumerate(weights):
                    act.wait_ge(w_loaded[n], 16)
                    nc.scalar.activation(dst[:, 0], raw, ACT.Copy, scale=by).then_inc(w_high, 1)

            @block.gpsimd
            def _(pool):
                nc.gpsimd.memset(ident[:], 0.0).then_inc(gp, 1)
                nc.gpsimd.memset(ident16[:], 0.0).then_inc(gp, 1)
                nc.gpsimd.memset(v1[:], 1.0).then_inc(gp, 1)
                nc.gpsimd.memset(half[:], -0.5).then_inc(gp, 1)
                pool.wait_ge(gp, 4)
                for m in (ident, ident16):
                    nc.gpsimd.affine_select(out=m[:], in_=m[:], compare_op=ALU.not_equal, fill=1.0, base=0,
                                            pattern=[[-1, P]], channel_multiplier=1).then_inc(gp, 1)

            @block.vector
            def _(dve):
                nc.vector.memset(ks[:], 0.0).then_inc(ks_set, 1)
                for n, (src, dst, raw, by) in enumerate(weights):
                    dve.wait_ge(w_high, n + 1)
                    nc.vector.scalar_tensor_tensor(dst[:, 1], raw, by, dst[:, 0].bitcast(F32), ALU.mult, ALU.subtract)
                dve.wait_ge(const_loaded, 96 if masks else 64)
                dve.wait_ge(rows_loaded, 32 if kinds else 16)
                nc.vector.tensor_scalar(bq[:], bq[:], DH ** -0.5, None, ALU.mult)
                if masks:
                    nc.vector.memset(ones[:], 1.0).then_inc(flagged, 1)
                    nc.vector.tensor_scalar(mbias[:], mraw[:], 0.0, -MASKED, ALU.is_equal, ALU.mult).then_inc(flagged, 1)
                    dve.wait_ge(flagged, 2)
                    nc.vector.tensor_reduce(lowest[:], mbias[:].rearrange("p a q t -> p (a q t)"), axis=AX_X, op=ALU.min).then_inc(flagged, 1)
                    dve.wait_ge(flagged, 3)
                    nc.vector.tensor_scalar(lowest[:], lowest[:], 0.0, None, ALU.is_lt).then_inc(flagged, 1)
                    dve.wait_ge(counted, 1)
                    nc.vector.tensor_scalar(count[:], ps_a[0:1, 0, 0:1], 1.0, None, ALU.min).then_inc(flagged, 1)
                    dve.wait_ge(flagged, 5)
                    nc.vector.tensor_copy(any_masked[:], count[:])

            @block.tensor
            def _(pe):
                if masks:
                    pe.wait_ge(flagged, 4)
                    nc.tensor.matmul(ps_a[0:1, 0, 0:1], lowest[:], ones[:], start=True, stop=True).then_inc(counted, 1)

        c1 = CREDIT
        stats_done = sem("stats_done"); mv_done = sem("mv_done"); rs1 = sem("rs1"); rstd_done = sem("rstd_done")
        xn_done = sem("xn_done"); xt_done = sem("xt_done"); xhi_done = sem("xhi_done"); xlo_done = sem("xlo_done")
        chi_done = sem("chi_done"); clo_done = sem("clo_done"); xbo_done = sem("xbo_done")
        q_done = sem("q_done"); k_done = sem("k_done"); v_done = sem("v_done")
        qh_done = sem("qh_done"); ql_done = sem("ql_done"); kh_done = sem("kh_done"); kl_done = sem("kl_done")
        v1_done = sem("v1_done"); qs_stacked = sem("qs_stacked"); ks_stacked = sem("ks_stacked")
        s_done = sem("s_done"); max_done = sem("max_done"); mtr_done = sem("mtr_done"); mh_done = sem("mh_done")
        ml_done = sem("ml_done"); m_stacked = sem("m_stacked")
        st_done = sem("st_done"); exp_done = sem("exp_done"); pv_done = sem("pv_done")
        rec_done = sem("rec_done"); recs_done = sem("recs_done"); an_done = sem("an_done")
        ahi_done = sem("ahi_done"); alo_done = sem("alo_done"); alo3_done = sem("alo3_done"); wo_done = sem("wo_done"); y_done = sem("y_done")
        stored = [sem("stored0"), sem("stored1")]
        counters = {
            "act": [xhi_done, qh_done, kh_done, mh_done, exp_done, ahi_done],
            "dve": [stats_done, mv_done, *([] if when["xn"] is None else [xn_done]), xlo_done, ql_done, kl_done, v1_done, max_done, ml_done,
                    rec_done, recs_done, an_done, alo3_done, y_done],
            "pool": [rs1, rstd_done, *([xn_done] if when["xn"] is None else []), chi_done, clo_done, xbo_done, alo_done],
            "pe": [xt_done, q_done, k_done, v_done, s_done, mtr_done, st_done, pv_done, wo_done],
        }

        def run_units(eng, step, ahead=2):
            def peeled(u):
                step(u, u % 2, 0 <= u < UNITS, 0 <= u + 1 < UNITS, u + 2 < UNITS, 0 <= u - 1)

            for u in range(-2, 2):
                peeled(u)
            with eng.Fori(1, (UNITS - ahead) // 2) as r:
                for b in range(2):
                    step(r * 2 + b, b, True, True, True, True)
            for u in range(UNITS - ahead, UNITS + 1):
                peeled(u)

        def start(eng, sems):
            for s in sems:
                eng.sem_inc(s, CREDIT)

        with nc.Block() as block:
            @block.sync
            def _(sp):
                def load(u, b):
                    sp.wait_ge(xn_done, c1 + 2 * (u - 1))
                    sp.wait_ge(xbo_done, c1 + u - 1)
                    sp.sem_inc(apart, 1)
                    sp.wait_ge(clo_done, c1 + u - 1)
                    sp.sem_inc(apart, 1)
                    load_unit(sp, u, b)

                def step(u, b, t, s, p, o):
                    if o:
                        sp.wait_ge(y_done, c1 + u)
                        for q, view in enumerate(x_out(u - 1)):
                            sp.dma_start(view, yout[:, 1 - b, q]).then_inc(stored[1 - b], 16)
                    if p:
                        if t:
                            sp.wait_ge(st_done, c1 + 16 * u + 16)
                            sp.sem_inc(apart, 1)
                        for n in (0, 2, 1):
                            sp.wait_ge(ql_done if n == 1 else qh_done, c1 + u + 3)
                            sp.dma_start(qs[32 * n:32 * n + 32, b].rearrange("d (j m) t -> d j (m t)", m=2),
                                         nat[:, n % 2].rearrange("p m t -> p (m t)")).then_inc(qs_stacked, 16)
                        for n in (0, 1, 2):
                            sp.wait_ge(kl_done if n == 2 else kh_done, c1 + u + 3)
                            for par in range(2):
                                row = 32 * n + 16 * par
                                sp.dma_start(ks[row:row + 16, b, 8 * par:8 * par + 8].rearrange("d (j m) t -> d j (m t)", m=2),
                                             nat[64 * par:64 * par + 64, 2 + n // 2].rearrange("p m t -> p (m t)")
                                             ).then_inc(ks_stacked, 16)
                    if s:
                        for i, done in ((0, mh_done), (1, ml_done)):
                            sp.wait_ge(done, c1 + u + 2)
                            row = rows_s + 2 * i
                            sp.dma_start(qs[row:row + 2, 1 - b], mt[:, i, :]).then_inc(m_stacked, 16)
                    if p:
                        if not isinstance(u, int) or u + 4 < UNITS:
                            load(u + 4, b)

                for b in range(2):
                    sp.sem_inc(stored[b], 16)
                run_units(sp, step, 4)
                for b in range(2):
                    sp.wait_ge(stored[b], 16 + 32 * (UNITS // 2))

            @block.gpsimd
            def _(pool):
                start(pool, counters["pool"])

                def pick(q):
                    for k in range(K):
                        nc.gpsimd.indirect_dma_start(picked[:, q, k], None, y_rows,
                                                     bass.IndirectOffsetOnAxis(ap=slot[:, q, k:k + 1], axis=0)).then_inc(picked_up, 16)

                def step(u, b, t, s, p, o):
                    def part_low(g):
                        pool.wait_ge(ahi_done, c1 + 4 * u + g + 1)
                        nc.gpsimd.tensor_tensor(alo[:, g], an[:, g % 2], ahi[:, g].bitcast(F32), ALU.subtract).then_inc(alo_done, 1)

                    def residual():
                        if adding:
                            pool.wait_ge(added, c1 + 8 * (u + 2))
                        pool.wait_ge(y_done, c1 + u)
                        pool.wait_ge(x_loaded[1 - b], (u + b) * 16 + 32)
                        for q in range(QT):
                            last = nc.gpsimd.tensor_tensor(xbo[:, 1 - b, q], xin[:, 1 - b, q], bo[:], ALU.add)
                        last.then_inc(xbo_done, 1)

                    if not p:
                        if s:
                            residual()
                        for g in range(3 if t else 0):
                            part_low(g)
                        return
                    n = u + 2
                    pool.wait_ge(mv_done, c1 + 2 * n + 2)
                    pool.wait_ge(xn_done, c1 + 2 * n)
                    pool.sem_inc(apart, 1)
                    nc.gpsimd.tensor_scalar(rstd[:], mv[:, :, 1], EPS, None, ALU.add).then_inc(rs1, 1)
                    pool.wait_ge(rs1, c1 + n + 1)
                    nc.gpsimd.tensor_tensor(rstd[:], rstd[:], half[:], ALU.pow).then_inc(rstd_done, 1)
                    if when["xn"] is None:
                        pool.wait_ge(rstd_done, c1 + n + 1)
                        pool.wait_ge(xt_done, c1 + n)
                        pool.sem_inc(apart, 1)
                        for q in range(QT):
                            nc.gpsimd.tensor_scalar(xn[:, q], xin[:, b, q], mv[:, q, 0:1], rstd[:, q:q + 1],
                                                    ALU.subtract, ALU.mult).then_inc(xn_done, 1)
                    pool.wait_ge(ctx_loaded[b], (n - b) * 8 + 16)
                    pool.wait_ge(v_done, c1 + n - 1)
                    pool.sem_inc(apart, 1)
                    nc.gpsimd.tensor_copy(chi[:, b], cin[:, b]).then_inc(chi_done, 1)
                    pool.wait_ge(chi_done, c1 + n + 1)
                    nc.gpsimd.tensor_tensor(clo[:, b], cin[:, b], chi[:, b].bitcast(F32), ALU.subtract).then_inc(clo_done, 1)
                    if s:
                        residual()
                    for g in range(3):
                        if adding and g < QT and (not isinstance(u, int) or n + 1 < UNITS):
                            if g == 0:
                                pool.wait_ge(slot_set, c1 + n + 2)
                                pool.wait_ge(added, c1 + 8 * (n + 1))
                                pool.sem_inc(apart, 1)
                            pick(g)
                        if t:
                            part_low(g)

                if adding:
                    pool.wait_ge(slot_set, c1 + 1)
                    for q in range(QT):
                        pick(q)
                run_units(pool, step, 4)

            @block.scalar
            def _(act):
                start(act, counters["act"])

                def step(u, b, t, s, p, o):
                    def exps(h):
                        act.wait_ge(st_done, c1 + 16 * u + h + 1)
                        act.wait_ge(pv_done, c1 + 4 * u + h // 4 - 1)
                        nc.scalar.activation(pt[:, h % 8], ps_t[:, h % 2, :, 0:span], ACT.Exp).then_inc(exp_done, 1)

                    def part_high(g):
                        act.wait_ge(an_done, c1 + 4 * u + g + 1)
                        act.wait_ge(wo_done, c1 + u)
                        nc.scalar.copy(ahi[:, g], an[:, g % 2]).then_inc(ahi_done, 1)

                    def project_high(part, done, ps, bias, high_done):
                        if s or t:
                            act.wait_ge(qs_stacked, 48 * (u + 2))
                            act.wait_ge(ks_stacked, 96 * (u + 2))
                        act.wait_ge(done, c1 + u + 3)
                        for m in range(2):
                            last = nc.scalar.activation(nat[:, part, m], ps[:, m], ACT.Identity, bias=bias[:, m:m + 1])
                        last.then_inc(high_done, 1)

                    for step_h in range(H + LAG):
                        if t and step_h < H:
                            exps(step_h)
                        if p and step_h == when["xhi"]:
                            act.wait_ge(xt_done, c1 + u + 3)
                            act.wait_ge(q_done, c1 + u + 2)
                            nc.scalar.copy(xhi[:], ps_a[:]).then_inc(xhi_done, 1)
                        if p and step_h == when["qh"]:
                            project_high(0, q_done, ps_a, bq, qh_done)
                        if p and step_h == when["kh"]:
                            project_high(2, k_done, ps_b, bk, kh_done)
                        if t and step_h in (10, 14):
                            part_high((step_h - 10) // 4)
                    if s:
                        act.wait_ge(mtr_done, c1 + u + 2)
                        if t:
                            act.wait_ge(m_stacked, 32 * (u + 1))
                        nc.scalar.activation(mt[:, 0, :], ps_a[0:H, 0, :], ACT.Copy, scale=1.0 / MSTEP).then_inc(mh_done, 1)
                    if t:
                        part_high(2)
                        part_high(3)

                run_units(act, step)

            @block.vector
            def _(dve):
                start(dve, counters["dve"])

                def set_slots(n):
                    nc.vector.tensor_copy(slot[:], slots[:, bass.ds(n * QT, QT)]).then_inc(slot_set, 1)

                if adding:
                    start(dve, [slot_set, added])
                    set_slots(0)

                def step(u, b, t, s, p, o):
                    n = u + 2

                    def invert(g, part):
                        dve.wait_ge(pv_done, c1 + 4 * u + g + 1)
                        dve.wait_ge(recs_done, c1 + 4 * u + g)
                        cols = slice(part * P, part * P + P)
                        nc.vector.reciprocal(rec[:, cols], ps_o[:, g % 2, g // 2, cols]).then_inc(rec_done, 1)

                    def spread(g):
                        dve.wait_ge(rec_done, c1 + 8 * u + 2 * g + 2)
                        dve.wait_ge(an_done, c1 + 4 * u + g)
                        dve.sem_inc(apart, 1)
                        nc.vector.stream_shuffle(recs[:], rec[:], [16 + i % 16 for i in range(32)]).then_inc(recs_done, 1)

                    def weigh(g):
                        dve.wait_ge(recs_done, c1 + 4 * u + g + 1)
                        dve.wait_ge(ahi_done, c1 + 4 * u + g - 1)
                        if g < 2:
                            dve.wait_ge(alo_done, c1 + 3 * u)
                            dve.wait_ge(alo3_done, c1 + u)
                        else:
                            dve.wait_ge(alo_done, c1 + 3 * u + g - 1)
                        nc.vector.tensor_tensor(an[:, g % 2], ps_o[:, g % 2, g // 2], recs[:], ALU.mult).then_inc(an_done, 1)

                    def project_low(part, hi_done, ps, bias, stacked, lo_done):
                        dve.wait_ge(hi_done, c1 + n + 1)
                        if s or t:
                            dve.wait_ge(stacked, (48 if stacked is qs_stacked else 96) * n)
                        for m in range(2):
                            last = nc.vector.scalar_tensor_tensor(nat[:, part, m], ps[:, m], bias[:, m:m + 1],
                                                                  nat[:, part - 1, m], ALU.add, ALU.subtract)
                        last.then_inc(lo_done, 1)

                    for step_h in range(H + LAG):
                        h = step_h - LAG
                        if s and h >= 0:
                            dve.wait_ge(s_done, c1 + 16 * (u + 1) + h + 1)
                            if h == 0:
                                dve.wait_ge(mtr_done, c1 + u + 1)
                            nc.vector.reduce_max(mx[:, :, 8 * (h % 2) + h // 2], ps_s[:, h % 2, :, 0:span], AX_X).then_inc(max_done, 1)
                        if s and step_h == when["v1"]:
                            dve.wait_ge(v_done, c1 + u + 2)
                            dve.wait_ge(pv_done, c1 + 4 * u)
                            for q in range(QT):
                                last = nc.vector.tensor_tensor(v1[:, 1 - b, q, :, 0:DH],
                                                               ps_b[:, q].rearrange("p (h d) -> p h d", d=DH),
                                                               bv[:].rearrange("p (h d) -> p h d", d=DH), ALU.add)
                            last.then_inc(v1_done, 1)
                        if p and adding and step_h == when["add"]:
                            dve.wait_ge(x_loaded[b], (n - b) * 16 + 32)
                            dve.wait_ge(picked_up, n * (16 * QT * K) + 16 * QT * K)
                            for k in range(K):
                                for q in range(QT):
                                    if k:
                                        dve.wait_ge(added, c1 + 8 * n + 2 * k - 1 + q)
                                    nc.vector.scalar_tensor_tensor(xin[:, b, q], picked[:, q, k], wts[:, bass.ds(n * QT + q, 1), k], xin[:, b, q],
                                                                   ALU.mult, ALU.add).then_inc(added, 1)
                            if not isinstance(u, int) or n + 1 < UNITS:
                                set_slots(n + 1)
                        if p and step_h == when["stats"]:
                            dve.wait_ge(x_loaded[b], (n - b) * 16 + 32)
                            if adding:
                                dve.wait_ge(added, c1 + 8 * (n + 1))
                            dve.sem_inc(apart, 1)
                            for q in range(QT):
                                nc.vector.bn_stats(stats[:, q], xin[:, b, q]).then_inc(stats_done, 1)
                            for q in range(QT):
                                dve.wait_ge(stats_done, c1 + 2 * n + 1 + q)
                                dve.wait_ge(xn_done, c1 + 2 * n)
                                dve.sem_inc(apart, 1)
                                nc.vector.bn_aggr(mv[:, q], stats[:, q]).then_inc(mv_done, 1)
                        if p and step_h == when["xn"]:
                            dve.wait_ge(rstd_done, c1 + n + 1)
                            dve.wait_ge(xt_done, c1 + n)
                            for q in range(QT):
                                nc.vector.tensor_scalar(xn[:, q], xin[:, b, q], mv[:, q, 0:1], rstd[:, q:q + 1],
                                                        ALU.subtract, ALU.mult).then_inc(xn_done, 1)
                        if p and step_h == when["xlo"]:
                            dve.wait_ge(xhi_done, c1 + n + 1)
                            dve.wait_ge(q_done, c1 + n)
                            nc.vector.tensor_tensor(xlo[:], ps_a[:], xhi[:].bitcast(F32), ALU.subtract).then_inc(xlo_done, 1)
                        if p and step_h == when["ql"]:
                            project_low(1, qh_done, ps_a, bq, qs_stacked, ql_done)
                        if p and step_h == when["kl"]:
                            project_low(3, kh_done, ps_b, bk, ks_stacked, kl_done)
                        if t and step_h >= 6:
                            g = (step_h - 6) // 4
                            if step_h % 4 == 2:
                                invert(g, 0)
                            elif step_h % 4 == 3:
                                invert(g, 1)
                            elif step_h % 4 == 0:
                                spread(g)
                            else:
                                weigh(g)
                        if o and step_h == when["y"]:
                            dve.wait_ge(wo_done, c1 + u)
                            dve.wait_ge(xbo_done, c1 + u)
                            dve.wait_ge(stored[1 - b], (u - 2 + b) * 16 + 16)
                            nc.vector.tensor_tensor(yout[:, 1 - b], ps_a[:], xbo[:, 1 - b], ALU.add).then_inc(y_done, 1)
                    if s:
                        dve.wait_ge(mh_done, c1 + u + 2)
                        if t:
                            dve.wait_ge(m_stacked, 32 * (u + 1))
                        nc.vector.scalar_tensor_tensor(mt[:, 1, :], ps_a[0:H, 0, :], 1.0 / MSTEP, mt[:, 0, :],
                                                       ALU.mult, ALU.subtract).then_inc(ml_done, 1)
                    if t:
                        invert(3, 0)
                        invert(3, 1)
                        spread(3)
                        weigh(3)
                        dve.wait_ge(ahi_done, c1 + 4 * u + 4)
                        nc.vector.tensor_tensor(alo[:, 3], an[:, 1], ahi[:, 3].bitcast(F32), ALU.subtract).then_inc(alo3_done, 1)

                run_units(dve, step, 4)

            @block.tensor
            def _(pe):
                start(pe, counters["pe"])

                def three(out, pairs):
                    ops = [(x, y) for ah, al, bh, bl in pairs for x, y in ((ah, bh), (ah, bl), (al, bh))]
                    for i, (x, y) in enumerate(ops):
                        last = nc.tensor.matmul(out, x, y, start=i == 0, stop=i == len(ops) - 1)
                    return last

                def step(u, b, t, s, p, o, masks=masks):
                    n = u + 2

                    def values(g):
                        pe.wait_ge(exp_done, c1 + 16 * u + 4 * g + 4)
                        pe.wait_ge(an_done, c1 + 4 * u + g - 1)
                        for kt in range(QT):
                            for j in range(4):
                                h = 4 * g + j
                                out = ps_o[32 * j:32 * j + 32, g % 2, g // 2]
                                if kinds:
                                    last = nc.tensor.matmul(out[:, kt * P:kt * P + P], v1[:, b, kt, h], pt[:, h % 8, kt],
                                                            start=True, stop=True, tile_position=(0, 32 * j))
                                else:
                                    last = nc.tensor.matmul(out, v1[:, b, kt, h], pt[:, h % 8, kt],
                                                            start=kt == 0, stop=kt == QT - 1, tile_position=(0, 32 * j))
                        last.then_inc(pv_done, 1)

                    for step_h in range(H + LAG):
                        if t and step_h < H:
                            h = step_h
                            key_head = 8 * (h % 2) + h // 2
                            if h == 0:
                                pe.wait_ge(m_stacked, 32 * (u + 1))
                            pe.wait_ge(exp_done, c1 + 16 * u + h - 1)
                            for k in range(QT):
                                if masks:
                                    nc.tensor.matmul(ps_t[:, h % 2, k], ident16[:], mbias[:, 1, k], start=True, stop=False)
                                seen = slice(k * P, k * P + P) if kinds else slice(0, UNIT)
                                last = nc.tensor.matmul(ps_t[:, h % 2, k, 0:span], ks[0:rows_t, b, key_head, k * P:k * P + P],
                                                        qs[0:rows_t, b, h // 2, seen], start=not masks, stop=True)
                            last.then_inc(st_done, 1)
                            if h in (5, 9, 13):
                                if h == 5:
                                    pe.wait_ge(v1_done, c1 + u + 1)
                                values((h - 5) // 4)
                        if s and step_h >= LAG:
                            h = step_h - LAG
                            key_head = 8 * (h % 2) + h // 2
                            if h == 0:
                                pe.wait_ge(qs_stacked, 48 * (u + 2))
                                pe.wait_ge(ks_stacked, 96 * (u + 2))
                            pe.wait_ge(max_done, c1 + 16 * (u + 1) + h - 1)
                            for q in range(QT):
                                if masks:
                                    nc.tensor.matmul(ps_s[:, h % 2, q], ident16[:], mbias[:, 0, q], start=True, stop=False)
                                seen = slice(q * P, q * P + P) if kinds else slice(0, UNIT)
                                last = nc.tensor.matmul(ps_s[:, h % 2, q, 0:span], qs[0:rows_s, 1 - b, h // 2, q * P:q * P + P],
                                                        ks[0:rows_s, 1 - b, key_head, seen], start=not masks, stop=True)
                            last.then_inc(s_done, 1)
                        if o and step_h - when["wo"] in (0, 1):
                            pe.wait_ge(ml_done, c1 + u + 1 if t else c1 + u)
                            pe.wait_ge(alo_done, c1 + 3 * u)
                            q = step_h - when["wo"]
                            toks = slice(q * P, q * P + P)
                            for g in range(4):
                                if g == 3 and q == 0:
                                    pe.wait_ge(alo3_done, c1 + u)
                                for i, (x, y) in enumerate(((ahi, 0), (ahi, 1), (alo, 0))):
                                    last = nc.tensor.matmul(ps_a[:, q], x[:, g, toks], wo[:, y, g], start=g + i == 0, stop=g + i == 5)
                            if q == QT - 1:
                                last.then_inc(wo_done, 1)
                        if t and step_h == H + LAG - 1:
                            values(3)
                        if p and step_h == when["xT"]:
                            pe.wait_ge(xn_done, c1 + 2 * n + 2)
                            pe.wait_ge(y_done, c1 + u)
                            pe.wait_ge(ml_done, c1 + u + 1)
                            for q in range(QT):
                                for c in range(KC):
                                    last = nc.tensor.transpose(ps_a[:, c, q * P:q * P + P], xn[:, q, c * P:c * P + P], ident[:])
                            last.then_inc(xt_done, 1)
                        if p and step_h - when["q"] in (0, 1):
                            pe.wait_ge(xlo_done, c1 + n + 1)
                            m = step_h - when["q"]
                            cols = slice(m * P, m * P + P)
                            last = three(ps_a[:, m], [(wq[:, 0, c, cols], wq[:, 1, c, cols], xhi[:, c], xlo[:, c]) for c in range(KC)])
                            if m == 1:
                                last.then_inc(q_done, 1)
                        if p and step_h - when["k"] in (0, 1):
                            pe.wait_ge(clo_done, c1 + n + 1)
                            pe.wait_ge(v1_done, c1 + n)
                            m = step_h - when["k"]
                            cols = slice(m * P, m * P + P)
                            last = three(ps_b[:, m], [(wk[:, 0, c, cols], wk[:, 1, c, cols], chi[:, b, c], clo[:, b, c]) for c in range(KC)])
                            if m == 1:
                                last.then_inc(k_done, 1)
                    if s:
                        pe.wait_ge(max_done, c1 + 16 * (u + 1) + 16)
                        pe.wait_ge(ql_done, c1 + n + 1 if p else c1 + n)
                        pe.wait_ge(y_done, c1 + u)
                        for q in range(QT):
                            last = nc.tensor.transpose(ps_a[0:H, 0, q * P:q * P + P], mx[:, q, :], ident[:])
                        last.then_inc(mtr_done, 1)
                    if p:
                        pe.wait_ge(kl_done, c1 + n + 1)
                        for q in range(QT):
                            toks = slice(q * P, q * P + P)
                            last = three(ps_b[:, q], [(chi[:, b, c, toks], clo[:, b, c, toks], wv[:, 0, c], wv[:, 1, c]) for c in range(KC)])
                        last.then_inc(v_done, 1)

                if masks:
                    run_by_flag(nc, pe, any_masked[:], lambda: run_units(pe, lambda *s: step(*s, masks=None)), lambda: run_units(pe, step))
                else:
                    run_units(pe, step)

        clear(nc, sems)


def routed_experts(nc, x_in, w, y_dram, slots_dram, weights_dram):
    T = TOKENS // P
    C = 4
    CH = T // C
    K = 4
    R = SLOT_ROWS
    NH = TILES * (R // P)
    WS = 64.0
    LIMIT = 7.0
    ALPHA = 1.702
    with ExitStack() as ctx:
        def sb(name, shape, dt=F32):
            return ctx.enter_context(nc.sbuf_tensor(f"ex_{name}", shape, dt))

        def sem(name):
            return ctx.enter_context(nc.semaphore(f"ex_{name}"))

        rows_dram = nc.dram_tensor("moe_rows", [TOKENS, 2 * D], F16, kind="Internal").ap()

        gu_hi = sb("gu_hi", [P, E, KC, 2 * D], F16); gu_lo = sb("gu_lo", [P, E, KC, 2 * D], F16)
        dn_hi = sb("dn_hi", [P, E, KC, D], F16); dn_lo = sb("dn_lo", [P, E, KC, D], F16)
        g_bias = sb("g_bias", [P, E, 4]); d_bias = sb("d_bias", [E, D])
        bias_rows = sb("bias_rows", [P, E, D], F16); two_rows = sb("two_rows", [P, P], F16)
        wts = sb("wts", [P, T, K]); pos = sb("pos", [P, T, K], U32)
        token = sb("token", [P, NH], U32)
        expert = sb("expert", [1, TILES], U32)
        ident = sb("ident", [P, P]); ident16 = sb("ident16", [P, P], F16)
        apart = sem("apart")

        with ExitStack() as rctx:
            def rt(name, shape, dt=F32):
                return rctx.enter_context(nc.sbuf_tensor(f"rt_{name}", shape, dt))

            def rsem(name):
                return rctx.enter_context(nc.semaphore(f"rt_{name}"))

            ps_x = rctx.enter_context(nc.psum_tensor("rt_ps_x", [P, KC, C * P], F32))
            ps_l = rctx.enter_context(nc.psum_tensor("rt_ps_l", [P, 2, 512], F32))
            ps_r = rctx.enter_context(nc.psum_tensor("rt_ps_r", [P, 2, 512], F32))
            ps_t = rctx.enter_context(nc.psum_tensor("rt_ps_t", [P, 512], F32))
            raw = rt("raw", [P, 4, 3, 2 * D])
            rw = rt("rw", [P, KC, E]); rb = rt("rb", [P, E]); half = rt("half", [P, C])
            before = rt("before", [P, P], BF16); ones = rt("ones", [P, P], BF16)
            iota = rt("iota", [P, E]); fills = rt("fills", [P, E]); row_iota = rt("row_iota", [P, P], F16)
            half_iota = rt("half_iota", [P, NH], F16); tile_iota = rt("tile_iota", [1, TILES])
            token_id = rt("token_id", [P, T]); carry = rt("carry", [P, E, T]); one_e = rt("one_e", [P, E])
            xin = rt("xin", [P, 2, C, D]); xn = rt("xn", [P, 2, C, D]); xh = rt("xh", [P, 2, C, 2, D], F16)
            stats = rt("stats", [P, C, 6]); mv = rt("mv", [P, C, 2]); rstd = rt("rstd", [P, C])
            xt = rt("xt", [P, KC, C * P])
            logits = rt("logits", [P, C, E]); high = rt("high", [P, C, 8]); where = rt("where", [P, C, 8], U32)
            best = rt("best", [P, T, K]); whichf = rt("whichf", [P, T, K])

            loaded = rsem("loaded"); gp = rsem("gp")
            x_loaded = [rsem("x_loaded0"), rsem("x_loaded1")]; w_loaded = [rsem(f"w_loaded{n}") for n in range(4)]
            h_stored = [rsem("h_stored0"), rsem("h_stored1")]
            stats_done = rsem("stats_done"); mv_done = rsem("mv_done"); var_done = rsem("var_done"); rstd_done = rsem("rstd_done")
            xn_done = rsem("xn_done"); hi_done = rsem("hi_done"); lo_done = rsem("lo_done")
            xt_done = rsem("xt_done"); xt_copied = rsem("xt_copied"); lg_done = rsem("lg_done"); lg_added = rsem("lg_added")
            bias_hi = rt("bias_hi", [E, D], F16); bias_lo = rt("bias_lo", [E, D], F16)
            bias_split = rsem("bias_split"); rows_set = rsem("rows_set"); bias_set = rsem("bias_set"); rows_zero = rsem("rows_zero"); placed = rsem("placed"); tables_stored = rsem("tables_stored")
            first_use = rt("first_use", [1, E])
            w_hi = rsem("w_hi"); w_lo = rsem("w_lo"); chosen = rsem("chosen"); max_done = rsem("max_done"); index_done = rsem("index_done")

            def chunks(eng, step):
                with eng.Fori(0, CH // 2 - 1) as r:
                    for b in range(2):
                        step(r * 2 + b, r, b, True)
                for b in range(2):
                    step(CH - 2 + b, CH // 2 - 1, b, False)

            with nc.Block() as block:
                @block.sync
                def _(sp):
                    sp.dma_start(rw[:], w["router_w"].rearrange("(c p) n -> p c n", p=P)).then_inc(loaded, 16)
                    sp.dma_start(rb[:], w["router_b"].partition_broadcast(P)).then_inc(loaded, 16)
                    sp.dma_start(g_bias[:].rearrange("p e f -> p (e f)"), w["gu_bias"]).then_inc(loaded, 16)
                    sp.dma_start(d_bias[:], w["d_bias"]).then_inc(loaded, 16)

                    def load(u, b):
                        sp.dma_start(xin[:, b], x_in[bass.ds(u * C * P, C * P), :].rearrange("(q p) d -> p q d", p=P)).then_inc(x_loaded[b], 16)

                    def load_weights(e, b):
                        sp.dma_start(raw[:, b, 0:KC], w["gate_up"][bass.ds(e * D, D), :].rearrange("(c p) n -> p c n", p=P)).then_inc(w_loaded[b], 16)
                        sp.dma_start(raw[:, b, KC].rearrange("p (c n) -> p c n", c=KC),
                                     w["down"][bass.ds(e * D, D), :].rearrange("(c p) n -> p c n", p=P)).then_inc(w_loaded[b], 16)

                    for b in range(2):
                        load(b, b)
                        load_weights(2 * b, 2 * b)
                        load_weights(2 * b + 1, 2 * b + 1)
                    sp.wait_ge(rows_zero, 1)
                    sp.wait_ge(bias_split, 2)
                    for row, half_of in enumerate((bias_hi, bias_lo)):
                        sp.dma_start(bias_rows[row:row + 1].rearrange("p e d -> p (e d)"), half_of[:]).then_inc(bias_set, 16)

                    def step(u, r, b, more):
                        if more:
                            sp.wait_ge(xn_done, u * C + C)
                            load(u + 2, b)
                        for n in range(2 if more else 0):
                            sp.wait_ge(w_lo, u * 4 + 2 * n + 2)
                            sp.sem_inc(apart, 1)
                            load_weights(u * 2 + n + 4, 2 * b + n)
                        sp.wait_ge(hi_done, u + 1)
                        sp.sem_inc(apart, 1)
                        sp.wait_ge(lo_done, CREDIT + u + 1)
                        sp.sem_inc(apart, 1)
                        sp.dma_start(rows_dram[bass.ds(u * C * P, C * P), :].rearrange("(q p) d -> p q d", p=P),
                                     xh[:, b].rearrange("p q a d -> p q (a d)")).then_inc(h_stored[b], 16)

                    chunks(sp, step)
                    for b in range(2):
                        sp.wait_ge(h_stored[b], 16 * (CH // 2 + 1))
                    sp.wait_ge(bias_set, 32)

                @block.gpsimd
                def _(pool):
                    nc.gpsimd.memset(bias_rows[:], 0.0).then_inc(rows_zero, 1)
                    sets = ((ident, 0.0), (ident16, 0.0), (half, -0.5), (before, 0.0), (ones, 1.0), (carry, 1.0), (one_e, 1.0))
                    for t, v in sets:
                        nc.gpsimd.memset(t[:], v).then_inc(gp, 1)
                    nc.gpsimd.iota(iota[:], [[1, E]], base=0, channel_multiplier=0, allow_small_or_imprecise_dtypes=True).then_inc(gp, 1)
                    nc.gpsimd.iota(fills[:], [[R, E]], base=0, channel_multiplier=0, allow_small_or_imprecise_dtypes=True).then_inc(gp, 1)
                    nc.gpsimd.iota(row_iota[:], [[1, P]], base=0, channel_multiplier=0, allow_small_or_imprecise_dtypes=True).then_inc(gp, 1)
                    nc.gpsimd.iota(half_iota[:], [[1, NH]], base=0, channel_multiplier=0, allow_small_or_imprecise_dtypes=True).then_inc(gp, 1)
                    nc.gpsimd.iota(tile_iota[:], [[1, TILES]], base=0, channel_multiplier=0, allow_small_or_imprecise_dtypes=True).then_inc(gp, 1)
                    nc.gpsimd.iota(token_id[:], [[P, T]], base=-TOKENS // 2, channel_multiplier=1, allow_small_or_imprecise_dtypes=True).then_inc(gp, 1)
                    pool.wait_ge(gp, 13)
                    for m in (ident, ident16):
                        nc.gpsimd.affine_select(out=m[:], in_=m[:], compare_op=ALU.not_equal, fill=1.0, base=0,
                                                pattern=[[-1, P]], channel_multiplier=1).then_inc(gp, 1)
                    nc.gpsimd.affine_select(out=before[:], in_=before[:], compare_op=ALU.is_ge, fill=1.0, base=0,
                                            pattern=[[-1, P]], channel_multiplier=1).then_inc(gp, 1)
                    nc.gpsimd.memset(carry[:, :, 0:1], 0.0).then_inc(gp, 1)

                    def step(u, r, b, more):
                        pool.wait_ge(mv_done, u * C + C)
                        pool.sem_inc(apart, 1)
                        nc.gpsimd.tensor_scalar(rstd[:], mv[:, :, 1], EPS, None, ALU.add).then_inc(var_done, 1)
                        pool.wait_ge(var_done, u + 1)
                        nc.gpsimd.tensor_tensor(rstd[:], rstd[:], half[:], ALU.pow).then_inc(rstd_done, 1)
                        pool.wait_ge(hi_done, u + 1)
                        nc.gpsimd.tensor_tensor(xh[:, b, :, 1], xn[:, b], xh[:, b, :, 0], ALU.subtract).then_inc(lo_done, 1)

                    pool.sem_inc(lo_done, CREDIT)
                    chunks(pool, step)

                @block.vector
                def _(dve):
                    dve.wait_ge(gp, 17)
                    dve.wait_ge(loaded, 64)
                    nc.vector.tensor_scalar(g_bias[:], g_bias[:], WS, None, ALU.mult).then_inc(chosen, 1)
                    dve.wait_ge(chosen, 1)
                    nc.vector.tensor_scalar(g_bias[:, :, 2:4], g_bias[:, :, 2:4], WS, None, ALU.add)
                    nc.vector.tensor_scalar(bias_hi[:], d_bias[:], WS, None, ALU.mult).then_inc(bias_split, 1)
                    dve.wait_ge(bias_split, 1)
                    nc.vector.scalar_tensor_tensor(bias_lo[:], d_bias[:], WS, bias_hi[:], ALU.mult, ALU.subtract).then_inc(bias_split, 1)
                    nc.vector.memset(two_rows[:], 0.0).then_inc(rows_set, 1)
                    dve.wait_ge(rows_set, 1)
                    nc.vector.memset(two_rows[0:2], 1.0)
                    dve.sem_inc(lg_added, CREDIT)

                    def choose(u, b):
                        dve.wait_ge(lg_done, CREDIT + u + 1)
                        nc.vector.tensor_tensor(logits[:], ps_l[:, b, 0:C * E].rearrange("p (q e) -> p q e", e=E),
                                                rb[:].unsqueeze(1).to_broadcast([P, C, E]), ALU.add).then_inc(lg_added, 1)
                        dve.wait_ge(lg_added, CREDIT + u + 1)
                        dve.sem_inc(apart, 1)
                        for q in range(C):
                            nc.vector.max(high[:, q], logits[:, q]).then_inc(max_done, 1)
                        dve.wait_ge(max_done, u * C + C)
                        dve.sem_inc(apart, 1)
                        for q in range(C):
                            nc.vector.max_index(where[:, q], high[:, q], logits[:, q]).then_inc(index_done, 1)
                        nc.vector.tensor_copy(best[:, bass.ds(u * C, C)], high[:, :, 0:K]).then_inc(chosen, 1)
                        dve.wait_ge(index_done, u * C + C)
                        nc.vector.tensor_copy(whichf[:, bass.ds(u * C, C)], where[:, :, 0:K]).then_inc(chosen, 1)

                    def step(u, r, b, prev):
                        dve.wait_ge(x_loaded[b], r * 16 + 16)
                        dve.sem_inc(apart, 1)
                        for q in range(C):
                            nc.vector.bn_stats(stats[:, q], xin[:, b, q]).then_inc(stats_done, 1)
                        dve.wait_ge(stats_done, u * C + C)
                        dve.sem_inc(apart, 1)
                        for q in range(C):
                            nc.vector.bn_aggr(mv[:, q], stats[:, q]).then_inc(mv_done, 1)
                        dve.wait_ge(rstd_done, u + 1)
                        dve.wait_ge(lo_done, CREDIT + u - 1)
                        dve.wait_ge(xt_done, CREDIT + u - 1)
                        for q in range(C):
                            nc.vector.tensor_scalar(xn[:, b, q], xin[:, b, q], mv[:, q, 0:1], rstd[:, q:q + 1], ALU.subtract, ALU.mult).then_inc(xn_done, 1)
                        if prev is not None:
                            choose(prev, 1 - b)
                        for n in range(2):
                            e = u * 2 + n
                            dve.wait_ge(w_hi, e * 2 + 2)
                            nc.vector.scalar_tensor_tensor(gu_lo[:, bass.ds(e, 1)].rearrange("p o c n -> p (o c) n"), raw[:, 2 * b + n, 0:KC], WS,
                                                           gu_hi[:, bass.ds(e, 1)].rearrange("p o c n -> p (o c) n"), ALU.mult, ALU.subtract).then_inc(w_lo, 1)
                            nc.vector.scalar_tensor_tensor(dn_lo[:, bass.ds(e, 1)].rearrange("p o c n -> p (o c) n"), raw[:, 2 * b + n, KC].rearrange("p (c n) -> p c n", c=KC), WS,
                                                           dn_hi[:, bass.ds(e, 1)].rearrange("p o c n -> p (o c) n"), ALU.mult, ALU.subtract).then_inc(w_lo, 1)

                    step(0, 0, 0, None)
                    step(1, 0, 1, 0)
                    with dve.Fori(1, CH // 2) as r:
                        step(r * 2, r, 0, r * 2 - 1)
                        step(r * 2 + 1, r, 1, r * 2)
                    choose(CH - 1, 1)

                @block.scalar
                def _(act):
                    def step(u, r, b, more):
                        for n in range(2):
                            e = u * 2 + n
                            act.wait_ge(w_loaded[2 * b + n], r * 32 + 32)
                            nc.scalar.activation(gu_hi[:, bass.ds(e, 1)].rearrange("p o c n -> p (o c) n"), raw[:, 2 * b + n, 0:KC], ACT.Copy, scale=WS).then_inc(w_hi, 1)
                            nc.scalar.activation(dn_hi[:, bass.ds(e, 1)].rearrange("p o c n -> p (o c) n"), raw[:, 2 * b + n, KC].rearrange("p (c n) -> p c n", c=KC), ACT.Copy, scale=WS).then_inc(w_hi, 1)
                        act.wait_ge(xn_done, u * C + C)
                        act.wait_ge(h_stored[b], r * 16 + 16)
                        nc.scalar.copy(xh[:, b, :, 0], xn[:, b]).then_inc(hi_done, 1)
                        act.wait_ge(xt_done, CREDIT + u + 1)
                        nc.scalar.copy(xt[:], ps_x[:]).then_inc(xt_copied, 1)

                    for s in h_stored:
                        act.sem_inc(s, 16)
                    act.wait_ge(loaded, 64)
                    nc.scalar.copy(first_use[:], rb[0:1])
                    chunks(act, step)

                @block.tensor
                def _(pe):
                    def step(u, r, b, more):
                        pe.wait_ge(xn_done, u * C + C)
                        for q in range(C):
                            for c in range(KC):
                                last = nc.tensor.transpose(ps_x[:, c, q * P:q * P + P], xn[:, b, q, c * P:c * P + P], ident[:])
                        last.then_inc(xt_done, 1)
                        pe.wait_ge(xt_copied, u + 1)
                        pe.wait_ge(lg_added, CREDIT + u - 1)
                        for q in range(C):
                            for c in range(KC):
                                last = nc.tensor.matmul(ps_l[:, b, q * E:q * E + E], xt[:, c, q * P:q * P + P], rw[:, c], start=c == 0, stop=c == KC - 1)
                        last.then_inc(lg_done, 1)

                    pe.wait_ge(gp, 17)
                    pe.wait_ge(loaded, 64)
                    for s in (xt_done, lg_done):
                        pe.sem_inc(s, CREDIT)
                    chunks(pe, step)

            ex = rt("ex", [P, T, K]); total = rt("total", [P, T])
            hot = rt("hot", [P, T, K, E]); prod = rt("prod", [P, T, K, E]); took = rt("took", [P, T, E], BF16)
            sums = rt("sums", [P, T, E]); upto = rt("upto", [P, E, T]); rank = rt("rank", [P, T, E])
            over = rt("over", [P, E, E]); tiles = rt("tiles", [P, E]); end = rt("end", [P, E]); first = rt("first", [P, E])
            posf = rt("posf", [P, T, K]); lane = rt("lane", [P, T, K], U32);
            lanef = rt("lanef", [P, T, K]); groupf = rt("groupf", [P, T, K])
            past = rt("past", [1, TILES, E]); owner = rt("owner", [1, TILES]); tokenf = rt("tokenf", [P, NH])
            at_lane = rt("at_lane", [P, 2, K, P], F16); at_group = rt("at_group", [P, 2, K, NH], F16)
            step_done = rsem("step_done"); ex_done = rsem("ex_done"); took_done = rsem("took_done"); rank_done = rsem("rank_done")
            lanes_done = rsem("lanes_done"); lanef_done = rsem("lanef_done"); groups_done = rsem("groups_done"); added = rsem("added"); inverted = rsem("inverted")
            with nc.Block() as block:
                @block.sync
                def _(sp):
                    sp.wait_ge(placed, 1)
                    sp.dma_start(slots_dram.rearrange("(t p) k -> p t k", p=P), pos[:]).then_inc(tables_stored, 16)
                    sp.dma_start(weights_dram.rearrange("(t p) k -> p t k", p=P), wts[:]).then_inc(tables_stored, 16)
                    sp.wait_ge(tables_stored, 32)

                @block.vector
                def _(dve):
                    n = 0

                    def then(ins):
                        nonlocal n
                        n += 1
                        ins.then_inc(step_done, 1)
                        dve.wait_ge(step_done, n)

                    nc.vector.tensor_tensor(ex[:], best[:, :, 0:K], best[:, :, 0:1].to_broadcast([P, T, K]), ALU.subtract).then_inc(ex_done, 1)
                    then(nc.vector.tensor_tensor(hot[:], whichf[:].unsqueeze(3).to_broadcast([P, T, K, E]),
                                                 iota[:].unsqueeze(1).unsqueeze(1).to_broadcast([P, T, K, E]), ALU.is_equal))
                    then(nc.vector.reduce_sum(sums[:], hot[:].rearrange("p t k e -> p t e k"), axis=AX_X))
                    nc.vector.tensor_copy(took[:], sums[:]).then_inc(took_done, 1)
                    dve.wait_ge(ex_done, 2)
                    then(nc.vector.reduce_sum(total[:], ex[:], axis=AX_X))
                    then(nc.vector.reciprocal(total[:], total[:]))
                    then(nc.vector.tensor_tensor(wts[:], ex[:], total[:].unsqueeze(2).to_broadcast([P, T, K]), ALU.mult))
                    dve.wait_ge(rank_done, 1)
                    then(nc.vector.tensor_copy(sums[:], ps_r[:, 0].rearrange("p (t e) -> p t e", e=E)))
                    then(nc.vector.tensor_copy(prod[:, 0:T // K].rearrange("p a k e -> p (a k e)").rearrange("p (e t) -> p e t", e=E), sums[:].rearrange("p t e -> p e t")))
                    then(nc.vector.tensor_tensor_scan(upto[:].rearrange("p e t -> p (e t)"), carry[:].rearrange("p e t -> p (e t)"),
                                                      prod[:, 0:T // K].rearrange("p a k e -> p (a k e)"), 0.0, ALU.mult, ALU.add))
                    then(nc.vector.tensor_tensor(over[:], upto[:, :, T - 1:T].to_broadcast([P, E, E]),
                                                 fills[:].unsqueeze(1).to_broadcast([P, E, E]), ALU.is_gt))
                    then(nc.vector.reduce_sum(tiles[:], over[:], axis=AX_X))
                    then(nc.vector.tensor_tensor_scan(end[:], one_e[:], tiles[:], 0.0, ALU.mult, ALU.add))
                    then(nc.vector.tensor_tensor(first[:], end[:], tiles[:], ALU.subtract))
                    then(nc.vector.tensor_scalar(first[:], first[:], float(R), None, ALU.mult))
                    then(nc.vector.tensor_tensor(rank[:], upto[:].rearrange("p e t -> p t e"), sums[:], ALU.subtract))
                    then(nc.vector.tensor_tensor(rank[:], rank[:], ps_r[:, 1].rearrange("p (t e) -> p t e", e=E), ALU.add))
                    then(nc.vector.tensor_tensor(rank[:], rank[:], first[:].unsqueeze(1).to_broadcast([P, T, E]), ALU.add))
                    then(nc.vector.tensor_tensor(prod[:], hot[:], rank[:].unsqueeze(2).to_broadcast([P, T, K, E]), ALU.mult))
                    then(nc.vector.reduce_sum(posf[:], prod[:], axis=AX_X))
                    nc.vector.tensor_copy(pos[:], posf[:]).then_inc(placed, 1)
                    dve.wait_ge(placed, 1)
                    then(nc.vector.tensor_scalar(lane[:], pos[:], P - 1, None, ALU.bitwise_and))
                    nc.vector.tensor_copy(lanef[:], lane[:]).then_inc(lanef_done, 1)
                    dve.wait_ge(lanef_done, 1)
                    then(nc.vector.tensor_tensor(groupf[:], posf[:], lanef[:], ALU.subtract))
                    then(nc.vector.tensor_scalar(groupf[:], groupf[:], 1.0 / P, None, ALU.mult))
                    for t in range(T):
                        s = t % 2
                        if t >= 2:
                            dve.wait_ge(added, t - 1)
                        for k in range(2):
                            nc.vector.tensor_scalar(at_lane[:, s, k], row_iota[:], lanef[:, t, k:k + 1], None, ALU.is_equal).then_inc(groups_done, 1)
                        for k in range(K):
                            nc.vector.tensor_scalar(at_group[:, s, k], half_iota[:], groupf[:, t, k:k + 1], token_id[:, t:t + 1],
                                                    ALU.is_equal, ALU.mult).then_inc(groups_done, 1)
                    then(nc.vector.tensor_tensor(past[:], end[0:1].unsqueeze(1).to_broadcast([1, TILES, E]),
                                                 tile_iota[:].unsqueeze(2).to_broadcast([1, TILES, E]), ALU.is_le))
                    then(nc.vector.reduce_sum(owner[:], past[:], axis=AX_X))
                    nc.vector.tensor_scalar(expert[:], owner[:], float(E - 1), None, ALU.min)
                    dve.wait_ge(inverted, 1)
                    then(nc.vector.tensor_scalar(tokenf[:], ps_t[:, 0:NH], float(TOKENS // 2), None, ALU.add))
                    nc.vector.tensor_copy(token[:], tokenf[:])

                @block.gpsimd
                def _(pool):
                    pool.wait_ge(lanef_done, 1)
                    for t in range(T):
                        if t >= 2:
                            pool.wait_ge(added, t - 1)
                        for k in range(2, K):
                            nc.gpsimd.tensor_scalar(at_lane[:, t % 2, k], row_iota[:], lanef[:, t, k:k + 1], None, ALU.is_equal).then_inc(lanes_done, 1)

                @block.scalar
                def _(act):
                    act.wait_ge(ex_done, 1)
                    nc.scalar.activation(ex[:], ex[:], ACT.Exp).then_inc(ex_done, 1)

                @block.tensor
                def _(pe):
                    pe.wait_ge(took_done, 1)
                    nc.tensor.matmul(ps_r[:, 0], ones[:], took[:].rearrange("p t e -> p (t e)"), start=True, stop=True)
                    nc.tensor.matmul(ps_r[:, 1], before[:], took[:].rearrange("p t e -> p (t e)"), start=True, stop=True).then_inc(rank_done, 1)
                    for t in range(T):
                        pe.wait_ge(lanes_done, 2 * (t + 1))
                        pe.wait_ge(groups_done, (K + 2) * (t + 1))
                        for k in range(K):
                            last = nc.tensor.matmul(ps_t[:, 0:NH], at_lane[:, t % 2, k], at_group[:, t % 2, k],
                                                    start=t == 0 and k == 0, stop=t == T - 1 and k == K - 1)
                        last.then_inc(added, 1)
                    pe.wait_ge(added, T)
                    pe.sem_inc(inverted, 1)

        with ExitStack() as cctx:
            def cb(name, shape, dt=F32):
                return cctx.enter_context(nc.sbuf_tensor(f"cp_{name}", shape, dt))

            def csem(name):
                return cctx.enter_context(nc.semaphore(f"cp_{name}"))

            ps_x = cctx.enter_context(nc.psum_tensor("cp_ps_x", [P, 2, 2, KC, R], F16))
            ps_g = cctx.enter_context(nc.psum_tensor("cp_ps_g", [P, 2, 4, R], F32))
            ps_y = cctx.enter_context(nc.psum_tensor("cp_ps_y", [P, 2, 2, D], F32))
            slot_token = cb("slot_token", [P, 2, 2], U32)
            rows = cb("rows", [P, 2, 2, 2 * D], F16)
            xt = cb("xt", [P, 2, 2, KC, R], F16)
            gate = cb("gate", [P, 2, 2, R]); up = cb("up", [P, 2, 2, R]); sg = cb("sg", [P, 2, 2, R])
            act_f = cb("act_f", [P, 2, 2, R]); a_hi = cb("a_hi", [P, 2, 2, R], F16); a_lo = cb("a_lo", [P, 2, 2, R], F16)
            yout = cb("yout", [P, 2, 2, D])
            idx_set = csem("idx_set"); xt_done = csem("xt_done"); xt_copied = csem("xt_copied"); gu_done = csem("gu_done")
            gate_done = csem("gate_done"); up_done = csem("up_done"); upg_done = csem("upg_done"); sg_done = csem("sg_done")
            act_done = csem("act_done"); ahi_done = csem("ahi_done"); alo_done = csem("alo_done")
            y_done = csem("y_done"); y_copied = csem("y_copied")
            gathered = [csem("gathered0"), csem("gathered1")]; stored = [csem("stored0"), csem("stored1")]

            def run(eng, counts, step):
                for s in counts:
                    eng.sem_inc(s, CREDIT)
                for i in range(-3, 2):
                    step(i, i % 2)
                with eng.Fori(1, TILES // 2 - 2) as r:
                    for b in range(2):
                        step(r * 2 + b, b)
                for i in range(TILES - 4, TILES + 2):
                    step(i, i % 2)

            def live(i, ahead):
                return not isinstance(i, int) or 0 <= i + ahead < TILES

            def at(i, each=1):
                return i * each + (each + CREDIT)

            def at_gather(i, b):
                return (i - b) * 16 + 32

            def at_store(i, b):
                return (i - b) * 8 + (16 + PAIR_CREDIT)

            PAIR_CREDIT = 64

            def expert_of(i, engine):
                return nc.values_load(expert[0:1, bass.ds(i, 1)], engines=[engine], min_val=0, max_val=E - 1,
                                      skip_runtime_bounds_check_because="the minimum with E - 1 bounds it")

            with nc.Block() as block:
                @block.sync
                def _(sp):
                    def step(i, b):
                        if live(i, -2):
                            sp.wait_ge(y_copied, at(i - 2))
                            sp.sem_inc(apart, 1)
                            sp.dma_start(y_dram[bass.ds((i - 2) * R, R), :].rearrange("(q p) d -> p q d", p=P), yout[:, b]).then_inc(stored[b], 16)

                    for s in stored:
                        sp.sem_inc(s, PAIR_CREDIT)
                    run(sp, [], step)
                    for b in range(2):
                        sp.wait_ge(stored[b], at_store(TILES - 2 + b, b))

                @block.gpsimd
                def _(pool):
                    def step(i, b):
                        if live(i, 3):
                            n = 1 - b
                            pool.wait_ge(idx_set, at(i + 3))
                            pool.wait_ge(xt_done, at(i + 1))
                            pool.sem_inc(apart, 1)
                            for h in range(2):
                                nc.gpsimd.indirect_dma_start(rows[:, n, h], None, rows_dram[:, :],
                                                             bass.IndirectOffsetOnAxis(ap=slot_token[:, n, h:h + 1], axis=0)).then_inc(gathered[n], 16)
                        if live(i, 0):
                            pool.wait_ge(ahi_done, at(i))
                            pool.wait_ge(y_done, at(i - 2))
                            nc.gpsimd.tensor_tensor(a_lo[:, b], act_f[:, b], a_hi[:, b], ALU.subtract).then_inc(alo_done, 1)

                    run(pool, [alo_done], step)

                @block.vector
                def _(dve):
                    def step(i, b):
                        if live(i, 3):
                            n = 1 - b
                            if live(i, 1):
                                dve.wait_ge(gathered[n], at_gather(i + 1, n))
                            nc.vector.tensor_copy(slot_token[:, n], token[:, bass.ds(i * 2 + 6, 2)]).then_inc(idx_set, 1)
                        if live(i, 0):
                            e = expert_of(i, mybir.EngineType.DVE)
                            dve.wait_ge(gu_done, at(i))
                            for m in range(2):
                                nc.vector.tensor_scalar(gate[:, b, m], ps_g[:, b, m], g_bias[:, bass.ds(e, 1), m], LIMIT * WS, ALU.add, ALU.min).then_inc(gate_done, 1)
                            for m in range(2):
                                nc.vector.tensor_scalar(up[:, b, m], ps_g[:, b, 2 + m], g_bias[:, bass.ds(e, 1), 2 + m], (1 - LIMIT) * WS, ALU.add, ALU.max).then_inc(up_done, 1)
                            dve.wait_ge(up_done, at(i, 2))
                            nc.vector.scalar_tensor_tensor(up[:, b], up[:, b], (1 + LIMIT) * WS, gate[:, b], ALU.min, ALU.mult).then_inc(upg_done, 1)
                            dve.wait_ge(upg_done, at(i))
                            dve.wait_ge(sg_done, at(i))
                            dve.wait_ge(alo_done, at(i - 2))
                            nc.vector.scalar_tensor_tensor(act_f[:, b], up[:, b], 1.0 / (WS * WS), sg[:, b], ALU.mult, ALU.mult).then_inc(act_done, 1)

                    run(dve, [idx_set, gate_done, up_done, upg_done, act_done], step)

                @block.scalar
                def _(act):
                    def step(i, b):
                        if live(i, 1):
                            act.wait_ge(xt_done, at(i + 1))
                            act.wait_ge(gu_done, at(i - 1))
                            nc.scalar.copy(xt[:, 1 - b], ps_x[:, 1 - b]).then_inc(xt_copied, 1)
                        if live(i, 0):
                            act.wait_ge(gate_done, at(i, 2))
                            act.wait_ge(act_done, at(i - 2))
                            nc.scalar.activation(sg[:, b], gate[:, b], ACT.Sigmoid, scale=ALPHA / WS).then_inc(sg_done, 1)
                            act.wait_ge(act_done, at(i))
                            act.wait_ge(y_done, at(i - 2))
                            nc.scalar.copy(a_hi[:, b], act_f[:, b]).then_inc(ahi_done, 1)
                        if live(i, -2):
                            act.wait_ge(y_done, at(i - 2))
                            act.wait_ge(stored[b], at_store(i - 4, b))
                            nc.scalar.activation(yout[:, b], ps_y[:, b], ACT.Copy, scale=1.0 / WS).then_inc(y_copied, 1)

                    run(act, [xt_copied, sg_done, ahi_done, y_copied], step)

                @block.tensor
                def _(pe):
                    def step(i, b):
                        if live(i, 1):
                            n = 1 - b
                            pe.wait_ge(gathered[n], at_gather(i + 1, n))
                            pe.wait_ge(xt_copied, at(i - 1))
                            for part in range(2):
                                for c in range(KC):
                                    for h in range(2):
                                        last = nc.tensor.transpose(ps_x[:, n, part, c, h * P:h * P + P], rows[:, n, h, part * D + c * P:part * D + c * P + P], ident16[:])
                            last.then_inc(xt_done, 1)
                        if live(i, 0):
                            e = expert_of(i, mybir.EngineType.PE)
                            pe.wait_ge(xt_copied, at(i))
                            pe.wait_ge(gate_done, at(i - 2, 2))
                            pe.wait_ge(up_done, at(i - 2, 2))
                            pe.sem_inc(apart, 1)
                            for m in range(4):
                                ops = [(wt, part, c) for c in range(KC) for wt, part in ((gu_hi, 0), (gu_hi, 1), (gu_lo, 0))]
                                for n, (wt, part, c) in enumerate(ops):
                                    last = nc.tensor.matmul(ps_g[:, b, m], wt[:, bass.ds(e, 1), c, m * P:m * P + P].rearrange("p o n -> p (o n)"),
                                                            xt[:, b, part, c], start=n == 0, stop=n == len(ops) - 1)
                            last.then_inc(gu_done, 1)
                        if live(i, -2):
                            e = expert_of(i - 2, mybir.EngineType.PE)
                            pe.wait_ge(alo_done, at(i - 2))
                            pe.wait_ge(y_copied, at(i - 4))
                            for h in range(2):
                                ops = [(a, wt, c) for c in range(KC) for a, wt in ((a_hi, dn_hi), (a_hi, dn_lo), (a_lo, dn_hi))]
                                nc.tensor.matmul(ps_y[:, b, h], two_rows[:], bias_rows[:, bass.ds(e, 1)].rearrange("p o n -> p (o n)"), start=True, stop=False)
                                for n, (a, wt, c) in enumerate(ops):
                                    last = nc.tensor.matmul(ps_y[:, b, h], a[:, b, c, h * P:h * P + P], wt[:, bass.ds(e, 1), c].rearrange("p o n -> p (o n)"),
                                                            start=False, stop=n == len(ops) - 1)
                            last.then_inc(y_done, 1)

                    run(pe, [xt_done, gu_done, y_done], step)


def gated_ffn(nc, x_in, x_out, w):
    U = 512
    UN = TOKENS // U
    QT = U // P
    HC = 768 // P
    S = float(np.float32(1.0 / 127.0))
    with ExitStack() as ctx:
        def sb(name, shape, dt=F32):
            return ctx.enter_context(nc.sbuf_tensor(f"ff_{name}", shape, dt))

        def sem(name):
            return ctx.enter_context(nc.semaphore(f"ff_{name}"))

        ps_x = ctx.enter_context(nc.psum_tensor("ff_ps_x", [P, KC, U], F32))
        ps_g = ctx.enter_context(nc.psum_tensor("ff_ps_g", [P, 2, 2, U], F32))
        ps_y = ctx.enter_context(nc.psum_tensor("ff_ps_y", [P, 2, U], F32))
        wint = sb("wint", [P, 6, 768], I32)
        wf = sb("wf", [P, 3, 768])
        lows = sb("lows", [P, 6]); unused = sb("unused", [P, 768])
        largest = sb("largest", [P, 1]); ones = sb("ones", [P, 1]); count = sb("count", [1, 1]); any_low = sb("any_low", [1, 1], U32)
        wg = sb("wg", [P, 2, KC, 768], F32R)
        wu = sb("wu", [P, 2, KC, 768], F32R)
        wd = sb("wd", [P, 2, HC, D], F32R)
        ident = sb("ident", [P, P]); half = sb("half", [P, QT])
        xin = sb("xin", [P, 2, QT, D])
        xres = sb("xres", [P, 2, QT, D])
        stats = sb("stats", [P, QT, 6]); mv = sb("mv", [P, QT, 2]); rstd = sb("rstd", [P, QT])
        xn = sb("xn", [P, QT, D])
        xhi = sb("xhi", [P, 2, KC, U], F32R); xlo = sb("xlo", [P, 2, KC, U], F32R)
        sg = sb("sg", [P, 2, U]); hf = sb("hf", [P, 2, U])
        hhi = sb("hhi", [P, 2, HC, U], F32R); hlo = sb("hlo", [P, 2, HC, U], F32R)
        yout = sb("yout", [P, 2, QT, D])

        w_loaded = [sem(f"w_loaded{n}") for n in range(6)]
        w_float = sem("w_float"); w_high = sem("w_high"); w_low = sem("w_low")
        w_summed = sem("w_summed"); flagged = sem("flagged"); counted = sem("counted")
        gp = sem("gp"); apart = sem("apart"); x_loaded = [sem("x_loaded0"), sem("x_loaded1")]
        parts = [(t[:, 0, c], t[:, 1, c]) for c in range(KC) for t in (wg, wu)]
        parts += [(wd[:, 0, 3 * g:3 * g + 3].rearrange("p c n -> p (c n)"),
                   wd[:, 1, 3 * g:3 * g + 3].rearrange("p c n -> p (c n)")) for g in range(2)]
        with nc.Block() as block:
            @block.sync
            def _(sp):
                n = 0
                for c in range(KC):
                    for name in ("wg", "wu"):
                        sp.dma_start(wint[:, n], w[name][c * P:c * P + P, :]).then_inc(w_loaded[n], 16)
                        n += 1
                    sp.dma_start(xin[:, c], x_in(c)).then_inc(x_loaded[c], 16)
                for g in range(2):
                    sp.dma_start(wint[:, n].rearrange("p (c n) -> p c n", n=D), w["wd"][g * 384:g * 384 + 384, :].rearrange("(c p) n -> p c n", p=P)).then_inc(w_loaded[n], 16)
                    n += 1

            @block.scalar
            def _(act):
                def sum_low(n):
                    act.wait_ge(w_low, n + 1)
                    if n:
                        act.wait_ge(w_summed, n)
                    nc.scalar.activation(unused[:], parts[n][1].bitcast(F32), ACT.Abs, accum_out=lows[:, n:n + 1]).then_inc(w_summed, 1)

                for n, (hi, lo) in enumerate(parts):
                    act.wait_ge(w_float, n + 1)
                    nc.scalar.copy(hi, wf[:, n % 3]).then_inc(w_high, 1)
                    if n >= 2:
                        sum_low(n - 2)
                sum_low(4)
                sum_low(5)

            @block.gpsimd
            def _(pool):
                nc.gpsimd.memset(ident[:], 0.0).then_inc(gp, 1)
                nc.gpsimd.memset(half[:], -0.5).then_inc(gp, 1)
                pool.wait_ge(gp, 2)
                nc.gpsimd.affine_select(out=ident[:], in_=ident[:], compare_op=ALU.not_equal, fill=1.0, base=0,
                                        pattern=[[-1, P]], channel_multiplier=1).then_inc(gp, 1)

            @block.vector
            def _(dve):
                def to_float(n):
                    dve.wait_ge(w_loaded[n], 16)
                    if n >= 3:
                        dve.wait_ge(w_low, n - 2)
                    nc.vector.tensor_copy(wf[:, n % 3], wint[:, n]).then_inc(w_float, 1)

                to_float(0)
                to_float(1)
                for n, (hi, lo) in enumerate(parts):
                    if n + 2 < len(parts):
                        to_float(n + 2)
                    dve.wait_ge(w_high, n + 1)
                    nc.vector.tensor_tensor(lo, wf[:, n % 3], hi.bitcast(F32), ALU.subtract).then_inc(w_low, 1)
                nc.vector.memset(ones[:], 1.0).then_inc(flagged, 1)
                dve.wait_ge(w_summed, 6)
                nc.vector.reduce_max(largest[:], lows[:], AX_X).then_inc(flagged, 1)
                dve.wait_ge(flagged, 2)
                nc.vector.tensor_scalar(largest[:], largest[:], 0.0, None, ALU.is_gt).then_inc(flagged, 1)
                dve.wait_ge(counted, 1)
                nc.vector.tensor_scalar(count[:], ps_x[0:1, 0, 0:1], 1.0, None, ALU.min).then_inc(flagged, 1)
                dve.wait_ge(flagged, 4)
                nc.vector.tensor_copy(any_low[:], count[:])

            @block.tensor
            def _(pe):
                pe.wait_ge(flagged, 3)
                nc.tensor.matmul(ps_x[0:1, 0, 0:1], largest[:], ones[:], start=True, stop=True).then_inc(counted, 1)

        c1 = CREDIT
        res_loaded = [sem("res_loaded0"), sem("res_loaded1")]
        stats_done = sem("stats_done"); mv_done = sem("mv_done"); rs1 = sem("rs1"); rstd_done = sem("rstd_done")
        xn_done = sem("xn_done"); xt_done = sem("xt_done"); xhi_done = sem("xhi_done"); xlo_done = sem("xlo_done")
        gu_done = sem("gu_done"); sg_done = sem("sg_done"); hf_done = sem("hf_done"); hhi_done = sem("hhi_done")
        hlo_done = sem("hlo_done"); y_done = sem("y_done"); out_done = sem("out_done")
        stored = [sem("stored0"), sem("stored1")]
        counters = {
            "act": [xhi_done, sg_done, hhi_done],
            "dve": [stats_done, mv_done, xn_done, xlo_done, hf_done, out_done],
            "pool": [rs1, rstd_done, hlo_done],
            "pe": [xt_done, gu_done, y_done],
        }

        def start(eng, sems):
            for s in sems:
                eng.sem_inc(s, CREDIT)

        def run_units(eng, step):
            step(-1, 1, True, False, False)
            step(0, 0, True, True, False)
            with eng.Fori(0, UN // 2 - 1) as r:
                step(r * 2 + 1, 1, True, True, True)
                step(r * 2 + 2, 0, True, True, True)
            step(UN - 1, 1, False, True, True)
            step(UN, 0, False, False, True)

        with nc.Block() as block:
            @block.sync
            def _(sp):
                def step(u, b, more, here, d):
                    if more:
                        sp.wait_ge(xn_done, c1 + 4 * (u + 1))
                        sp.dma_start(xin[:, b], x_in(u + 2)).then_inc(x_loaded[b], 16)
                    if here:
                        sp.wait_ge(out_done, c1 + 4 * (u - 1))
                        sp.dma_start(xres[:, b], x_in(u)).then_inc(res_loaded[b], 16)
                    if d:
                        sp.wait_ge(out_done, c1 + 4 * u)
                        sp.dma_start(x_out(u - 1), yout[:, 1 - b]).then_inc(stored[1 - b], 16)

                for b in range(2):
                    sp.sem_inc(stored[b], 16)
                step(0, 0, True, True, False)
                with sp.Fori(0, UN // 2 - 2) as r:
                    step(r * 2 + 1, 1, True, True, True)
                    step(r * 2 + 2, 0, True, True, True)
                step(UN - 3, 1, True, True, True)
                step(UN - 2, 0, False, True, True)
                step(UN - 1, 1, False, True, True)
                step(UN, 0, False, False, True)
                for b in range(2):
                    sp.wait_ge(stored[b], 16 + 16 * (UN // 2))

            @block.gpsimd
            def _(pool):
                start(pool, counters["pool"])

                def step(u, b, n, g, d):
                    def low(j):
                        pool.wait_ge(hhi_done, c1 + 6 * u + j + 1)
                        nc.gpsimd.tensor_tensor(hlo[:, b, j], hf[:, j % 2], hhi[:, b, j].bitcast(F32), ALU.subtract).then_inc(hlo_done, 1)

                    for j in range(HC):
                        if g:
                            low(j)
                        if n and j == 0:
                            pool.wait_ge(mv_done, c1 + 4 * (u + 1) + 4)
                            pool.wait_ge(xn_done, c1 + 4 * (u + 1))
                            pool.sem_inc(apart, 1)
                            nc.gpsimd.tensor_scalar(rstd[:], mv[:, :, 1], EPS, None, ALU.add).then_inc(rs1, 1)
                            pool.wait_ge(rs1, c1 + u + 2)
                            nc.gpsimd.tensor_tensor(rstd[:], rstd[:], half[:], ALU.pow).then_inc(rstd_done, 1)

                run_units(pool, step)

            @block.scalar
            def _(act):
                start(act, counters["act"])

                def step(u, b, n, g, d):
                    def silu(j):
                        act.wait_ge(gu_done, c1 + 6 * u + j + 1)
                        act.wait_ge(hf_done, c1 + 6 * u + j - 1)
                        nc.scalar.activation(sg[:, j % 2], ps_g[:, j % 2, 0], ACT.Silu, scale=S).then_inc(sg_done, 1)

                    def high(j):
                        act.wait_ge(hf_done, c1 + 6 * u + j + 1)
                        if j == 0:
                            act.wait_ge(y_done, c1 + 4 * (u - 1))
                        nc.scalar.copy(hhi[:, b, j], hf[:, j % 2]).then_inc(hhi_done, 1)

                    for j in range(HC):
                        if n and j == 4:
                            act.wait_ge(xt_done, c1 + u + 2)
                            for c in range(KC):
                                last = nc.scalar.copy(xhi[:, 1 - b, c], ps_x[:, c])
                            last.then_inc(xhi_done, 1)
                        if g:
                            silu(j)
                            if j:
                                high(j - 1)
                    if g:
                        high(HC - 1)

                run_units(act, step)

            @block.vector
            def _(dve):
                start(dve, counters["dve"])

                def step(u, b, n, g, d):
                    m = u + 1
                    for j in range(HC):
                        if n and j == 4:
                            dve.wait_ge(xhi_done, c1 + m + 1)
                            for c in range(KC):
                                last = nc.vector.tensor_tensor(xlo[:, 1 - b, c], ps_x[:, c], xhi[:, 1 - b, c].bitcast(F32), ALU.subtract)
                            last.then_inc(xlo_done, 1)
                        if g:
                            dve.wait_ge(sg_done, c1 + 6 * u + j + 1)
                            dve.wait_ge(hlo_done, c1 + 6 * u + j - 1)
                            nc.vector.tensor_tensor(hf[:, j % 2], ps_g[:, j % 2, 1], sg[:, j % 2], ALU.mult).then_inc(hf_done, 1)
                        if n and j == 0:
                            dve.wait_ge(x_loaded[1 - b], (m - (1 - b)) * 8 + 16)
                            for q in range(QT):
                                nc.vector.bn_stats(stats[:, q], xin[:, 1 - b, q]).then_inc(stats_done, 1)
                            for q in range(QT):
                                dve.wait_ge(stats_done, c1 + 4 * m + 1 + q)
                                dve.sem_inc(apart, 1)
                                nc.vector.bn_aggr(mv[:, q], stats[:, q]).then_inc(mv_done, 1)
                        if n and j == 1:
                            dve.wait_ge(rstd_done, c1 + m + 1)
                            dve.wait_ge(xt_done, c1 + m)
                            for q in range(QT):
                                nc.vector.tensor_scalar(xn[:, q], xin[:, 1 - b, q], mv[:, q, 0:1], rstd[:, q:q + 1],
                                                        ALU.subtract, ALU.mult).then_inc(xn_done, 1)
                        if d and j >= 2:
                            t = j - 2
                            dve.wait_ge(y_done, c1 + 4 * (u - 1) + t + 1)
                            if t == 0:
                                dve.wait_ge(res_loaded[1 - b], (u - 1 - (1 - b)) * 8 + 16)
                                if isinstance(u, int):
                                    if (u - 1) // 2 > 0:
                                        dve.wait_ge(stored[1 - b], 16 + 16 * ((u - 1) // 2))
                                else:
                                    dve.wait_ge(stored[1 - b], 16 + (u - 1 - (1 - b)) * 8)
                            nc.vector.scalar_tensor_tensor(yout[:, 1 - b, t], ps_y[:, t % 2, 0:D], S * S, xres[:, 1 - b, t],
                                                           ALU.mult, ALU.add).then_inc(out_done, 1)
                run_units(dve, step)

            @block.tensor
            def _(pe):
                start(pe, counters["pe"])

                def step(u, b, n, g, d, split=True):
                    products = ((0, 0), (0, 1), (1, 0)) if split else ((0, 0), (0, 1))
                    for j in range(HC):
                        if g:
                            if j == 0:
                                pe.wait_ge(xlo_done, c1 + u + 1)
                            pe.wait_ge(hf_done, c1 + 6 * u + j - 1)
                            for i, wt in enumerate((wg, wu)):
                                ops = [(wt[:, a, c, j * P:j * P + P], (xhi, xlo)[x][:, b, c]) for c in range(KC)
                                       for a, x in products]
                                for k, (l, r) in enumerate(ops):
                                    last = nc.tensor.matmul(ps_g[:, j % 2, i], l, r, start=k == 0, stop=k == len(ops) - 1)
                            last.then_inc(gu_done, 1)
                        if d and 1 <= j <= 4:
                            if j == 1:
                                pe.wait_ge(hlo_done, c1 + 6 * u)
                            pe.wait_ge(out_done, c1 + 4 * (u - 1) + j - 2)
                            toks = slice((j - 1) * P, j * P)
                            ops = [((hhi, hlo)[x][:, 1 - b, c, toks], wd[:, a, c]) for c in range(HC) for a, x in products]
                            for k, (l, r) in enumerate(ops):
                                last = nc.tensor.matmul(ps_y[:, (j - 1) % 2, 0:D], l, r, start=k == 0, stop=k == len(ops) - 1)
                            last.then_inc(y_done, 1)
                        if n and j == 3:
                            pe.wait_ge(xn_done, c1 + 4 * (u + 1) + 4)
                            pe.wait_ge(xlo_done, c1 + u + 1)
                            for q in range(QT):
                                for c in range(KC):
                                    last = nc.tensor.transpose(ps_x[:, c, q * P:q * P + P], xn[:, q, c * P:c * P + P], ident[:])
                            last.then_inc(xt_done, 1)

                run_by_flag(nc, pe, any_low[:], lambda: run_units(pe, lambda *s: step(*s, split=False)), lambda: run_units(pe, step))


def build(nc, ins, out, only=None):
    x = ins["x"]
    scratch = lambda name: nc.dram_tensor(name, [TOKENS, D], F32, kind="Internal").ap()
    x1 = out if only == "L0" else scratch("x1")
    x3 = out if only in ("L1", "ML1") else scratch("x3")

    def natural(a):
        return lambda u: [a[bass.ds(u * UNIT + q * P, P), :] for q in range(2)]

    def wide(a):
        return lambda u: a[bass.ds(u * 512, 512), :].rearrange("(q p) d -> p q d", p=P)

    def by_position(a):
        v = a.rearrange("(b n) d -> n b d", b=16)
        return lambda u: [v[bass.ds(u * 16 + 8 * q, 8)] for q in range(2)]

    def weights(layer):
        w = {n: ins[f"{layer}_{n}"] for n in ("wq", "wk", "wv", "wo", "bq", "bk", "bv", "bo")}
        for n in ("wq", "wk", "wv", "wo"):
            w[n] = w[n].rearrange("(c p) n -> p c n", p=P)
        return w

    def tiles(a):
        return a.rearrange("(q p) k -> p q k", p=P)

    def ctx_units(a):
        return lambda u: a[:, bass.ds(u * UNIT, UNIT)].rearrange("(c p) t -> p c t", p=P)

    if only in (None, "L0"):
        attention(nc, "l0", natural(x), natural(x1), ctx_units(ins["ctxT0"]), weights("L0"), (tiles(ins["mask"]), tiles(ins["maskT"])), None, ins["key_rows0"], WHEN0)
    experts = (nc.dram_tensor("expert_rows", [TILES * SLOT_ROWS, D], F32, kind="Internal").ap(),
               nc.dram_tensor("slots", [TOKENS, 4], U32, kind="Internal").ap(),
               nc.dram_tensor("weights", [TOKENS, 4], F32, kind="Internal").ap())

    def table(a):
        v = a.rearrange("(b g n) k -> n b g k", b=16, n=8)
        return lambda n: v[n]

    if only in (None, "ML1"):
        routed_experts(nc, ins["x1in"] if only else x1, ins, *experts)
    if only in (None, "L1", "ML1"):
        attention(nc, "l1", by_position(ins["x1in"] if only else x1), by_position(x3), ctx_units(ins["ctxT1"]), weights("L1"), None, ins["query_rows1"], ins["key_rows1"], WHEN1,
                  None if only == "L1" else (experts[0], table(experts[1]), table(experts[2])))
    if only in (None, "FFN"):
        gated_ffn(nc, wide(ins["x1in"] if only else x3), wide(out), ins)


_ORDER = np.array([(4 * jj + 2 * m + par) * DH + d for m in range(2) for par in range(2) for d in range(DH) for jj in range(4)])


def layout(i):
    a = {"x": i["x"].reshape(TOKENS, D)}
    ctx = i["ctx_1024"]
    a["ctxT0"] = ctx.transpose(2, 0, 1).reshape(D, TOKENS)
    a["ctxT1"] = ctx.transpose(2, 1, 0).reshape(D, TOKENS)
    a["mask"] = i["mask_1x1xSxS2_if1"][0, 0]
    a["maskT"] = a["mask"].T
    parity = np.arange(2)[:, None, None, None, None] == np.arange(2)[None, None, :, None, None]
    off = np.tile(np.where(parity, -MSTEP, 0) + np.zeros((2, 2, 2, 8, UNIT)), (2, 1, 1, 1, 1)).reshape(4, 2 * H * UNIT)
    a["key_rows0"] = off.astype(np.float16)
    at = np.arange(8)[:, None] == np.arange(P)[None, :] // 16
    a["query_rows1"] = np.tile(np.where(at, MSTEP, 0), (1, 2 * 8 * UNIT // P)).astype(np.float16)
    other = np.tile(np.where(at, 0, -MASKED / MSTEP), (1, 2 * H * UNIT // P))
    a["key_rows1"] = np.concatenate([other, off]).astype(np.float16)
    for layer in ("L0", "L1"):
        for n in ("q", "k"):
            a[f"{layer}_w{n}"] = i[f"{layer}_xattn_W{n}"].T[:, _ORDER]
            a[f"{layer}_b{n}"] = i[f"{layer}_xattn_b{n}"][_ORDER].reshape(2, P).T
        a[f"{layer}_wv"] = i[f"{layer}_xattn_Wv"].T
        wo = np.zeros((H, 2, DH, D), np.float32)
        wo[:, 0] = i[f"{layer}_xattn_Wo"].T.reshape(H, DH, D)
        a[f"{layer}_wo"] = wo.reshape(2 * D, D)
        a[f"{layer}_bv"] = i[f"{layer}_xattn_bv"]
        a[f"{layer}_bo"] = i[f"{layer}_xattn_bo"]
    a["router_w"] = i["L0_ffn_router_w"]
    a["router_b"] = i["L0_ffn_router_b"]
    gu = i["L0_ffn_gate_up_proj"].reshape(E, D, D, 2).transpose(0, 1, 3, 2)
    a["gate_up"] = gu.reshape(E * D, 2 * D)
    a["gu_bias"] = i["L0_ffn_gate_up_bias"].reshape(E, D, 2).transpose(0, 2, 1).reshape(E * 4, P).T
    a["down"] = i["L0_ffn_down_proj"].reshape(E * D, D)
    a["d_bias"] = i["L0_ffn_down_bias"]
    a["wg"] = i["L1_ffn_w_gate"].T
    a["wu"] = i["L1_ffn_w_up"].T
    a["wd"] = i["L1_ffn_w_down"].T
    return {k: np.ascontiguousarray(v) for k, v in a.items()}


def kernel(**inputs):
    import concourse.bacc as bacc
    from concourse.bass_utils import run_bass_kernel_spmd

    arrays = {f"in_{k}": v for k, v in layout({k: np.asarray(v) for k, v in inputs.items()}).items()}
    nc = bacc.Bacc("TRN2", target_bir_lowering=False, num_devices=1)
    ins = {k[3:]: nc.dram_tensor(k, v.shape, mybir.dt.from_np(v.dtype), kind="ExternalInput").ap() for k, v in arrays.items()}
    out = nc.dram_tensor("out", [TOKENS, D], F32, kind="ExternalOutput").ap()
    build(nc, ins, out)
    r = run_bass_kernel_spmd(nc, [arrays], core_ids=[0])
    return r.results[0]["out"].reshape(16, 256, D)
```
